# Optimizing a Trainium2 kernel written in Bass

```python
import numpy as np
import jax
import jax.numpy as jnp

def _softmax(x, axis=-1):
    return jax.nn.softmax(x, axis=axis)

def _gelu(x):
    return jax.nn.gelu(x, approximate=True)

def _silu(x):
    return jax.nn.silu(x)

def _sigmoid(x):
    return jax.nn.sigmoid(x)

def _layernorm(x, axis=-1, eps=1e-05):
    m = jnp.mean(x, axis=axis, keepdims=True)
    v = jnp.var(x, axis=axis, keepdims=True)
    return (x - m) / jnp.sqrt(v + eps)

def _scatter_add(tgt, idx, src, axis=0):
    return tgt.at[idx].add(src)

def _segment_sum(src, seg, n):
    return jax.ops.segment_sum(src, seg, n)
kernel_name = 'mk_sandwich_d1_jaxref_r8_ba730a'

def setup_inputs(seed: int=0):
    np.random.seed(seed)
    _w = jnp.asarray

    def _L0_attn_setup():
        import jax, jax.numpy as jnp
        import numpy as np
        H = 256
        I = 512
        N = 64
        K = 4
        G = 1
        NH = 64
        P = I // NH
        CH = 32
        EPS = 1e-05
        CONV_DIM = I + 2 * G * N
        PROJ = I + CONV_DIM + NH

        def _segsum(x):
            T = x.shape[-1]
            xe = jnp.broadcast_to(x[..., None], (*x.shape, T))
            i = jnp.arange(T)[:, None]
            j = jnp.arange(T)[None, :]
            xs = jnp.cumsum(jnp.where(i > j, xe, 0.0), axis=-2)
            return jnp.where(i >= j, xs, -jnp.inf)

        def _forward(hidden_states, ln_weight, in_proj_w, conv_w, conv_b, dt_bias, A_log, D, norm_weight, out_proj_w):
            residual = hidden_states
            x = hidden_states
            x = x * jax.lax.rsqrt(jnp.mean(x * x, -1, keepdims=True) + EPS) * ln_weight
            proj = jnp.einsum('bth,ph->btp', x, in_proj_w)
            gate, xBC, dt = jnp.split(proj, [I, I + CONV_DIM], axis=-1)
            xBC_t = jnp.transpose(xBC, (0, 2, 1))
            xBC_t = jax.lax.conv_general_dilated(xBC_t, conv_w[:, None, :], (1,), [(K - 1, 0)], dimension_numbers=('NCH', 'OIH', 'NCH'), feature_group_count=CONV_DIM)
            xBC = jax.nn.silu(jnp.transpose(xBC_t, (0, 2, 1)) + conv_b)
            xs, Bc, Cc = jnp.split(xBC, [I, I + G * N], axis=-1)
            b, t, _ = xs.shape
            Xh = xs.reshape(b, t, NH, P)
            Bh = jnp.repeat(Bc.reshape(b, t, G, N), NH // G, axis=2)
            Ch = jnp.repeat(Cc.reshape(b, t, G, N), NH // G, axis=2)
            dt = jax.nn.softplus(dt + dt_bias)
            A = -jnp.exp(A_log)
            c = t // CH
            Xc = (Xh * dt[..., None]).reshape(b, c, CH, NH, P)
            Bcn = Bh.reshape(b, c, CH, NH, N)
            Ccn = Ch.reshape(b, c, CH, NH, N)
            dA = (dt * A).reshape(b, c, CH, NH).transpose(0, 3, 1, 2)
            A_cum = jnp.cumsum(dA, axis=-1)
            Lmat = jnp.exp(_segsum(dA))
            Y_diag = jnp.einsum('bclhn,bcshn,bhcls,bcshp->bclhp', Ccn, Bcn, Lmat, Xc)
            decay_states = jnp.exp(A_cum[..., -1:] - A_cum)
            states = jnp.einsum('bclhn,bhcl,bclhp->bchpn', Bcn, decay_states, Xc)
            chunk_decay = jnp.exp(A_cum[..., -1])

            def step(carry, inp):
                st, dec = inp
                new = dec[..., None, None] * carry + st
                return (new, carry)
            states_c = jnp.moveaxis(states, 1, 0)
            decay_c = jnp.moveaxis(chunk_decay, 2, 0)
            init = jnp.zeros((b, NH, P, N), xs.dtype)
            _, prev_states = jax.lax.scan(step, init, (states_c, decay_c))
            prev_states = jnp.moveaxis(prev_states, 0, 1)
            state_decay = jnp.exp(A_cum)
            Y_off = jnp.einsum('bclhn,bchpn,bhcl->bclhp', Ccn, prev_states, state_decay)
            Y = (Y_diag + Y_off).reshape(b, t, NH, P) + D[None, None, :, None] * Xh
            y = Y.reshape(b, t, I)
            y = y * jax.nn.silu(gate)
            y = y * jax.lax.rsqrt(jnp.mean(y * y, -1, keepdims=True) + EPS) * norm_weight
            out = jnp.einsum('bti,hi->bth', y, out_proj_w)
            return residual + out
        key = jax.random.key(seed)
        ks = jax.random.split(key, 8)
        B, T = (2, 256)
        return {'hidden_states': jax.random.normal(ks[0], (B, T, H), jnp.float32), 'ln_weight': jnp.ones((H,), jnp.float32), 'in_proj_w': jax.random.normal(ks[1], (PROJ, H), jnp.float32) * 0.02, 'conv_w': jax.random.normal(ks[2], (CONV_DIM, K), jnp.float32) * 0.1, 'conv_b': jax.random.normal(ks[3], (CONV_DIM,), jnp.float32) * 0.02, 'dt_bias': jax.random.normal(ks[4], (NH,), jnp.float32) * 0.1, 'A_log': jnp.log(jnp.arange(1, NH + 1, dtype=jnp.float32)), 'D': jnp.ones((NH,), jnp.float32), 'norm_weight': jnp.ones((I,), jnp.float32), 'out_proj_w': jax.random.normal(ks[5], (H, I), jnp.float32) * 0.02}
    _L0_attn_in = _L0_attn_setup()

    def _L0_ffn_setup():
        import jax, jax.numpy as jnp
        import numpy as np
        B, S, H = (2, 64, 256)
        E, I, K = (64, 176, 6)
        NS = 2
        SH_I = I * NS
        key = jax.random.key(seed)
        ks = jax.random.split(key, 6)
        s = 0.02
        return {'hidden_states': jax.random.normal(ks[0], (B, S, H), jnp.float32), 'gate_w': jax.random.normal(ks[1], (E, H), jnp.float32) * s, 'experts_w1': jax.random.normal(ks[2], (E, I, H), jnp.float32) * s, 'experts_w2': jax.random.normal(ks[3], (E, H, I), jnp.float32) * s, 'shared_gate_up': jax.random.normal(ks[4], (2 * SH_I, H), jnp.float32) * s, 'shared_down': jax.random.normal(ks[5], (H, SH_I), jnp.float32) * s}
    _L0_ffn_in = _L0_ffn_setup()
    _d = {'L0_attn_hidden_states': _L0_attn_in['hidden_states'], 'L0_attn_ln_weight': _L0_attn_in['ln_weight'], 'L0_attn_in_proj_w': _L0_attn_in['in_proj_w'], 'L0_attn_conv_w': _L0_attn_in['conv_w'], 'L0_attn_conv_b': _L0_attn_in['conv_b'], 'L0_attn_dt_bias': _L0_attn_in['dt_bias'], 'L0_attn_A_log': _L0_attn_in['A_log'], 'L0_attn_D': _L0_attn_in['D'], 'L0_attn_norm_weight': _L0_attn_in['norm_weight'], 'L0_attn_out_proj_w': _L0_attn_in['out_proj_w'], 'L0_ffn_gate_w': _L0_ffn_in['gate_w'], 'L0_ffn_experts_w1': _L0_ffn_in['experts_w1'], 'L0_ffn_experts_w2': _L0_ffn_in['experts_w2'], 'L0_ffn_shared_gate_up': _L0_ffn_in['shared_gate_up'], 'L0_ffn_shared_down': _L0_ffn_in['shared_down']}
    _x0 = _d['L0_attn_hidden_states']
    _d['L0_attn_hidden_states'] = jax.random.normal(jax.random.fold_in(jax.random.key(seed), 1), (4, 1024, 256), dtype=_x0.dtype)
    del _x0
    return _d

def reference(L0_attn_hidden_states, L0_attn_ln_weight, L0_attn_in_proj_w, L0_attn_conv_w, L0_attn_conv_b, L0_attn_dt_bias, L0_attn_A_log, L0_attn_D, L0_attn_norm_weight, L0_attn_out_proj_w, L0_ffn_gate_w, L0_ffn_experts_w1, L0_ffn_experts_w2, L0_ffn_shared_gate_up, L0_ffn_shared_down):

    def _L0_attn_ref(hidden_states, ln_weight, in_proj_w, conv_w, conv_b, dt_bias, A_log, D, norm_weight, out_proj_w):
        import jax, jax.numpy as jnp
        import numpy as np
        H = 256
        I = 512
        N = 64
        K = 4
        G = 1
        NH = 64
        P = I // NH
        CH = 32
        EPS = 1e-05
        CONV_DIM = I + 2 * G * N
        PROJ = I + CONV_DIM + NH

        def _segsum(x):
            T = x.shape[-1]
            xe = jnp.broadcast_to(x[..., None], (*x.shape, T))
            i = jnp.arange(T)[:, None]
            j = jnp.arange(T)[None, :]
            xs = jnp.cumsum(jnp.where(i > j, xe, 0.0), axis=-2)
            return jnp.where(i >= j, xs, -jnp.inf)

        def _forward(hidden_states, ln_weight, in_proj_w, conv_w, conv_b, dt_bias, A_log, D, norm_weight, out_proj_w):
            residual = hidden_states
            x = hidden_states
            x = x * jax.lax.rsqrt(jnp.mean(x * x, -1, keepdims=True) + EPS) * ln_weight
            proj = jnp.einsum('bth,ph->btp', x, in_proj_w)
            gate, xBC, dt = jnp.split(proj, [I, I + CONV_DIM], axis=-1)
            xBC_t = jnp.transpose(xBC, (0, 2, 1))
            xBC_t = jax.lax.conv_general_dilated(xBC_t, conv_w[:, None, :], (1,), [(K - 1, 0)], dimension_numbers=('NCH', 'OIH', 'NCH'), feature_group_count=CONV_DIM)
            xBC = jax.nn.silu(jnp.transpose(xBC_t, (0, 2, 1)) + conv_b)
            xs, Bc, Cc = jnp.split(xBC, [I, I + G * N], axis=-1)
            b, t, _ = xs.shape
            Xh = xs.reshape(b, t, NH, P)
            Bh = jnp.repeat(Bc.reshape(b, t, G, N), NH // G, axis=2)
            Ch = jnp.repeat(Cc.reshape(b, t, G, N), NH // G, axis=2)
            dt = jax.nn.softplus(dt + dt_bias)
            A = -jnp.exp(A_log)
            c = t // CH
            Xc = (Xh * dt[..., None]).reshape(b, c, CH, NH, P)
            Bcn = Bh.reshape(b, c, CH, NH, N)
            Ccn = Ch.reshape(b, c, CH, NH, N)
            dA = (dt * A).reshape(b, c, CH, NH).transpose(0, 3, 1, 2)
            A_cum = jnp.cumsum(dA, axis=-1)
            Lmat = jnp.exp(_segsum(dA))
            Y_diag = jnp.einsum('bclhn,bcshn,bhcls,bcshp->bclhp', Ccn, Bcn, Lmat, Xc)
            decay_states = jnp.exp(A_cum[..., -1:] - A_cum)
            states = jnp.einsum('bclhn,bhcl,bclhp->bchpn', Bcn, decay_states, Xc)
            chunk_decay = jnp.exp(A_cum[..., -1])

            def step(carry, inp):
                st, dec = inp
                new = dec[..., None, None] * carry + st
                return (new, carry)
            states_c = jnp.moveaxis(states, 1, 0)
            decay_c = jnp.moveaxis(chunk_decay, 2, 0)
            init = jnp.zeros((b, NH, P, N), xs.dtype)
            _, prev_states = jax.lax.scan(step, init, (states_c, decay_c))
            prev_states = jnp.moveaxis(prev_states, 0, 1)
            state_decay = jnp.exp(A_cum)
            Y_off = jnp.einsum('bclhn,bchpn,bhcl->bclhp', Ccn, prev_states, state_decay)
            Y = (Y_diag + Y_off).reshape(b, t, NH, P) + D[None, None, :, None] * Xh
            y = Y.reshape(b, t, I)
            y = y * jax.nn.silu(gate)
            y = y * jax.lax.rsqrt(jnp.mean(y * y, -1, keepdims=True) + EPS) * norm_weight
            out = jnp.einsum('bti,hi->bth', y, out_proj_w)
            return residual + out
        return _forward(hidden_states, ln_weight, in_proj_w, conv_w, conv_b, dt_bias, A_log, D, norm_weight, out_proj_w)

    def _L0_ffn_ref(hidden_states, gate_w, experts_w1, experts_w2, shared_gate_up, shared_down):
        import jax, jax.numpy as jnp
        import numpy as np
        B, S, H = (2, 64, 256)
        E, I, K = (64, 176, 6)
        NS = 2
        SH_I = I * NS
        orig_shape = hidden_states.shape
        x = hidden_states.reshape(-1, orig_shape[-1])
        router_logits = x @ gate_w.T
        probs = jax.nn.softmax(router_logits, axis=-1)
        topk_w, topk_idx = jax.lax.top_k(probs, K)
        topk_w = topk_w / jnp.sum(topk_w, axis=-1, keepdims=True)
        combine = jnp.sum(jax.nn.one_hot(topk_idx, E, dtype=x.dtype) * topk_w[..., None], axis=1)
        h = jax.nn.silu(jnp.einsum('th,eih->tei', x, experts_w1))
        y = jnp.einsum('tei,ehi->teh', h, experts_w2)
        routed_out = jnp.einsum('teh,te->th', y, combine)
        gu = x @ shared_gate_up.T
        g, u = jnp.split(gu, 2, axis=-1)
        shared_out = jax.nn.silu(g) * u @ shared_down.T
        return (routed_out + shared_out).reshape(orig_shape)
    x = L0_attn_hidden_states
    x = x + _layernorm(_L0_attn_ref(_layernorm(x, axis=-1), L0_attn_ln_weight, L0_attn_in_proj_w, L0_attn_conv_w, L0_attn_conv_b, L0_attn_dt_bias, L0_attn_A_log, L0_attn_D, L0_attn_norm_weight, L0_attn_out_proj_w), axis=-1)
    x = x + _layernorm(_L0_ffn_ref(_layernorm(x, axis=-1), L0_ffn_gate_w, L0_ffn_experts_w1, L0_ffn_experts_w2, L0_ffn_shared_gate_up, L0_ffn_shared_down), axis=-1)
    return x

_drawn_inputs = setup_inputs


def setup_inputs(seed=0):
    import zlib

    import numpy as np

    out = dict(_drawn_inputs(seed))
    spreads = {'L0_attn_ln_weight': (1.0, 0.2),
     'L0_attn_D': (1.0, 0.2),
     'L0_attn_norm_weight': (1.0, 0.2)}
    factors = {}
    for name, (base, spread) in spreads.items():
        noise = np.random.default_rng([zlib.crc32(name.encode()), seed]).standard_normal(out[name].shape)
        drawn = base * np.exp(spread * noise) if base else spread * noise
        out[name] = jnp.asarray(drawn.astype(out[name].dtype))
    for name, factor in factors.items():
        out[name] = (out[name] * factor).astype(out[name].dtype)
    return out
```

```python
import numpy as np
import concourse.bass as bass
from concourse import mybir
from contextlib import ExitStack, contextmanager

F32 = mybir.dt.float32
ALU = mybir.AluOpType
ACT = mybir.ActivationFunctionType

B, T, H = 4, 1024, 256
CI, NS, NH, P = 512, 64, 64, 8
TAPS, CH = 4, 32
EPS = 1e-5
TILE = 128
NT = B * T // TILE
HALF = TILE // 2
PAIRS = B // 2
KH = H // 128
XB = CI // 128
NB = XB + 1
CT = TILE // CH
HQ = 4
HG = NH // HQ
GT = 4
NG = NT // GT
NE, EI, TOPK = 64, 176, 6
EK = EI // 2
SI = 2 * EI
SB = -(-SI // 128)
REGION = B * T + 128
MAXT = 256
assert MAXT >= B * T * TOPK // 128 + NE
FIELDS = 2
LEAD = 2


def done(n, back=0):
    return n + 1 + LEAD - back


def wait_alone(eng, sem, value, passed):
    eng.wait_ge(sem, value)
    eng.sem_inc(passed, 1)


@contextmanager
def loop_semaphores(nc, names):
    with ExitStack() as ctx:
        sems = {name: ctx.enter_context(nc.semaphore(name)) for name in names.split()}
        with nc.Block() as block:
            @block.vector
            def _(dve):
                for s in sems.values():
                    dve.sem_inc(s, LEAD)
        yield sems
        with nc.Block() as block:
            @block.vector
            def _(dve):
                for s in sems.values():
                    dve.sem_clear(s)


def load_constants(nc, sb, once, src):
    c = {}
    loaded, scaled = once("constants_loaded"), once("constants_scaled")
    for name, ap in src.items():
        c[name] = sb("c_" + name, list(ap.shape), F32)
    with nc.Block() as block:
        @block.sync
        def _(sp):
            for name, ap in src.items():
                sp.dma_start(c[name][:], ap).then_inc(loaded, 16)
            sp.wait_ge(loaded, 16 * len(src))

        @block.scalar
        def _(act):
            act.wait_ge(loaded, 16 * len(src))
            nc.scalar.activation(c["a_log"][:], c["a_log"][:], ACT.Exp).then_inc(scaled, 1)

        @block.vector
        def _(dve):
            dve.wait_ge(loaded, 16 * len(src))
            for b in range(XB):
                nc.vector.tensor_scalar(c["w_out"][:, b, :], c["w_out"][:, b, :],
                                        c["norm_w"][:, b:b + 1], None, ALU.mult)
            nc.vector.tensor_scalar(c["skip"][:], c["skip"][:], 0.5, None, ALU.mult).then_inc(scaled, 1)
            dve.wait_ge(scaled, 2)
    return c


def norm_in(nc, c, res, x_tiles):
    names = ("x_loaded0 x_loaded1 stats mean_var var_eps rstd nbias ln sum_sq ms_eps rms xn turned "
             "scaled kept dt_done dt_kept kept_stats dve_passed pool_passed")
    with loop_semaphores(nc, names) as s, ExitStack() as ctx:
        def sb(name, shape):
            return ctx.enter_context(nc.sbuf_tensor(name, shape, F32))
        xin = sb("p1_x", [128, 2, GT, H])
        xl = sb("p1_xl", [128, 2, GT, H])
        sq = sb("p1_sq", [128, 2, GT, H])
        st = sb("p1_st", [128, 2, GT, 6])
        mv = sb("p1_mv", [128, 2, GT, 2])
        small = sb("p1_small", [128, 2, 6, GT])
        xs = sb("p1_xs", [128, 2, KH, GT * TILE])
        ps_turn = [[ctx.enter_context(nc.psum_tensor(f"p1_turn{q}{k}", [128, GT * TILE], F32)) for k in range(KH)]
                   for q in range(2)]
        ps_dt = [ctx.enter_context(nc.psum_tensor(f"p1_dt{q}", [128, GT, NH], F32)) for q in range(2)]
        block = ctx.enter_context(nc.Block())

        @block.sync
        def _(sp):
            with sp.Fori(0, NG // 2) as it:
                for q in range(2):
                    n = 2 * it + q
                    sp.wait_ge(s["ln"], done(n, 2))
                    sp.dma_start(xin[:, q], x_tiles[:, bass.ds(n * GT, GT), :]).then_inc(s[f"x_loaded{q}"], 16)

        @block.vector
        def _(dve):
            with dve.Fori(0, NG // 2) as it:
                for q in range(2):
                    n = 2 * it + q
                    veps, mseps = small[:, q, 0], small[:, q, 1]
                    dve.wait_ge(s[f"x_loaded{q}"], 16 * it + 16 + LEAD)
                    for t in range(GT):
                        last = nc.vector.bn_stats(st[:, q, t, :], xin[:, q, t, :])
                    last.then_inc(s["stats"], 1)
                    wait_alone(dve, s["stats"], done(n), s["dve_passed"])
                    for t in range(GT):
                        last = nc.vector.bn_aggr(mv[:, q, t, :], st[:, q, t, :])
                    last.then_inc(s["mean_var"], 1)
                    dve.wait_ge(s["mean_var"], done(n))
                    nc.vector.tensor_scalar(veps, mv[:, q, :, 1], EPS, None, ALU.add).then_inc(s["var_eps"], 1)
                    dve.wait_ge(s["rstd"], done(n))
                    nc.vector.scalar_tensor_tensor(small[:, q, 3], mv[:, q, :, 0], -1.0, small[:, q, 2],
                                                   ALU.mult, ALU.mult).then_inc(s["nbias"], 1)
                    dve.wait_ge(s["nbias"], done(n))
                    nc.vector.tensor_copy(res["rstd"][:, bass.ds(n * GT, GT)], small[:, q, 2])
                    nc.vector.tensor_copy(res["nbias"][:, bass.ds(n * GT, GT)], small[:, q, 3]).then_inc(s["kept_stats"], 1)
                    dve.wait_ge(s["sum_sq"], done(n))
                    nc.vector.tensor_scalar(mseps, small[:, q, 4], 1.0 / H, EPS, ALU.mult, ALU.add)\
                        .then_inc(s["ms_eps"], 1)
                    dve.wait_ge(s["rms"], done(n))
                    for t in range(GT):
                        last = nc.vector.tensor_scalar(xl[:, q, t, :], xl[:, q, t, :], small[:, q, 5, t:t + 1],
                                                       None, ALU.mult)
                    last.then_inc(s["xn"], 1)
                    dve.wait_ge(s["dt_done"], done(n))
                    nc.vector.tensor_tensor(res["dt"][:, bass.ds(n * GT, GT), :], ps_dt[q][:, :, :],
                                            c["dt_bias"][:, None, :].to_broadcast([128, GT, NH]),
                                            ALU.add).then_inc(s["dt_kept"], 1)

        @block.gpsimd
        def _(pool):
            with pool.Fori(0, NG // 2) as it:
                for q in range(2):
                    n = 2 * it + q
                    pool.wait_ge(s["var_eps"], done(n))
                    nc.gpsimd.tensor_tensor(small[:, q, 2], small[:, q, 0], c["minus_half"][:, 0:GT], ALU.pow)\
                        .then_inc(s["rstd"], 1)
                    pool.wait_ge(s["ms_eps"], done(n))
                    nc.gpsimd.tensor_tensor(small[:, q, 5], small[:, q, 1], c["minus_half"][:, 0:GT], ALU.pow)\
                        .then_inc(s["rms"], 1)
                    wait_alone(pool, s["scaled"], done(n), s["pool_passed"])
                    for k in range(KH):
                        last = nc.gpsimd.tensor_copy(res["tokT"][:, bass.ds(n * GT, GT), k, :],
                                                     xs[:, q, k, :].rearrange("p (a b) -> p a b", a=GT))
                    last.then_inc(s["kept"], 1)

        @block.scalar
        def _(act):
            with act.Fori(0, NG // 2) as it:
                for q in range(2):
                    n = 2 * it + q
                    act.wait_ge(s["nbias"], done(n))
                    act.wait_ge(s["turned"], done(n, 2))
                    for t in range(GT):
                        last = nc.scalar.activation(xl[:, q, t, :], xin[:, q, t, :], ACT.Identity,
                                                    bias=small[:, q, 3, t:t + 1], scale=small[:, q, 2, t:t + 1])
                    last.then_inc(s["ln"], 1)
                    act.wait_ge(s["ln"], done(n))
                    for t in range(GT):
                        last = nc.scalar.activation(sq[:, q, t, :], xl[:, q, t, :], ACT.Square,
                                                    accum_out=small[:, q, 4, t:t + 1])
                    last.then_inc(s["sum_sq"], 1)
                    act.wait_ge(s["turned"], done(n))
                    act.wait_ge(s["kept"], done(n, 2))
                    act.wait_ge(s["dt_done"], done(n, 2))
                    for k in range(KH):
                        last = nc.scalar.activation(xs[:, q, k, :], ps_turn[q][k][:, :], ACT.Identity,
                                                    scale=c["ln_w"][:, k:k + 1])
                    last.then_inc(s["scaled"], 1)

        @block.tensor
        def _(pe):
            with pe.Fori(0, NG // 2) as it:
                for q in range(2):
                    n = 2 * it + q
                    pe.wait_ge(s["xn"], done(n))
                    pe.wait_ge(s["scaled"], done(n, 2))
                    for k in range(KH):
                        for t in range(GT):
                            last = nc.tensor.transpose(ps_turn[q][k][:, t * TILE:(t + 1) * TILE],
                                                       xl[:, q, t, k * 128:(k + 1) * 128], c["ident"][:])
                    last.then_inc(s["turned"], 1)
                    pe.wait_ge(s["scaled"], done(n))
                    pe.wait_ge(s["dt_kept"], done(n, 2))
                    for t in range(GT):
                        for k in range(KH):
                            last = nc.tensor.matmul(ps_dt[q][:, t, :], xs[:, q, k, t * TILE:(t + 1) * TILE],
                                                    c["w_dt"][:, k, :], start=(k == 0), stop=(k == KH - 1))
                    last.then_inc(s["dt_done"], 1)


def decays(nc, c, res):
    QT = 8
    NQ = NT // QT
    W = QT * NH
    names = "absolute small_exp one_more log correction correction2 halved softplus dA sums exps states_dt permuted permuted_kept"
    with loop_semaphores(nc, names) as s, ExitStack() as ctx:
        def sb(name, shape):
            return ctx.enter_context(nc.sbuf_tensor(name, shape, F32))
        e = sb("p2_e", [128, W])
        u = sb("p2_u", [128, W])
        lg = sb("p2_l", [128, W])
        ps = [ctx.enter_context(nc.psum_tensor(f"p2_sum{k}", [128, W], F32)) for k in range(3)]
        ps_perm = [ctx.enter_context(nc.psum_tensor(f"p2_perm{k}", [128, W], F32)) for k in range(CT)]
        block = ctx.enter_context(nc.Block())

        def piece(name, n):
            return res[name][:, n * QT:(n + 1) * QT, :].rearrange("p a b -> p (a b)")

        @block.scalar
        def _(act):
            for n in range(NQ):
                act.wait_ge(s["correction"], done(n, 1))
                nc.scalar.activation(e[:], piece("dt", n), ACT.Abs).then_inc(s["absolute"], 1)
                act.wait_ge(s["absolute"], done(n))
                nc.scalar.activation(e[:], e[:], ACT.Exp, scale=-1.0).then_inc(s["small_exp"], 1)
                act.wait_ge(s["one_more"], done(n))
                nc.scalar.activation(lg[:], u[:], ACT.Ln).then_inc(s["log"], 1)
                act.wait_ge(s["sums"], done(n))
                for k, name in enumerate(("to_end", "decay0", "decay1")):
                    last = nc.scalar.activation(piece(name, n), ps[k][:], ACT.Exp)
                last.then_inc(s["exps"], 1)
                act.wait_ge(s["permuted"], done(n))
                for ch in range(CT):
                    last = nc.scalar.activation(res["dAp"][:, ch, n * QT:(n + 1) * QT, :],
                                                ps_perm[ch][:, 0:QT * HG].rearrange("p (a b) -> p a b", a=QT),
                                                ACT.Copy)
                last.then_inc(s["permuted_kept"], 1)

        @block.vector
        def _(dve):
            for n in range(NQ):
                z = piece("dt", n)
                dve.wait_ge(s["small_exp"], done(n))
                nc.vector.tensor_scalar(u[:], e[:], 1.0, None, ALU.add).then_inc(s["one_more"], 1)
                dve.wait_ge(s["log"], done(n))
                nc.vector.scalar_tensor_tensor(u[:], u[:], -1.0, e[:], ALU.add, ALU.subtract).then_inc(s["correction"], 1)
                dve.wait_ge(s["correction"], done(n))
                nc.vector.tensor_tensor(u[:], lg[:], u[:], ALU.subtract).then_inc(s["correction2"], 1)
                dve.wait_ge(s["correction2"], done(n))
                nc.vector.scalar_tensor_tensor(z, z, 0.0, u[:], ALU.max, ALU.add).then_inc(s["softplus"], 1)
                dve.wait_ge(s["softplus"], done(n))
                nc.vector.scalar_tensor_tensor(res["dA"][:, n * QT:(n + 1) * QT, :], res["dt"][:, n * QT:(n + 1) * QT, :], -1.0,
                                               c["a_log"][:, None, :].to_broadcast([128, QT, NH]),
                                               ALU.mult, ALU.mult).then_inc(s["dA"], 1)
                dve.wait_ge(s["exps"], done(n))
                nc.vector.scalar_tensor_tensor(piece("to_end", n), piece("to_end", n), 0.25, z, ALU.mult, ALU.mult)\
                    .then_inc(s["states_dt"], 1)
                dve.wait_ge(s["dA"], done(n))
                dve.wait_ge(s["states_dt"], done(n))
                nc.vector.tensor_scalar(z, z, 0.5, None, ALU.mult).then_inc(s["halved"], 1)

        @block.tensor
        def _(pe):
            for n in range(NQ):
                pe.wait_ge(s["dA"], done(n))
                pe.wait_ge(s["exps"], done(n, 1))
                dA = piece("dA", n)
                for k, name in enumerate(("later", "whole0", "whole1")):
                    last = nc.tensor.matmul(ps[k][:], c[name][:], dA, start=True, stop=True)
                last.then_inc(s["sums"], 1)
                pe.wait_ge(s["permuted_kept"], done(n, 1))
                for ch in range(CT):
                    rows = slice(CH * ch, CH * ch + CH)
                    for h in range(HQ):
                        src = res["dA"][rows, n * QT:(n + 1) * QT, :].rearrange("p a (g h) -> p a g h", h=HQ)[:, :, :, h]
                        last = nc.tensor.matmul(ps_perm[ch][CH * h:CH * h + CH, 0:QT * HG], c["ident"][rows, rows], src,
                                                start=True, stop=True)
                last.then_inc(s["permuted"], 1)


def scan(nc, once, c, res, x_tiles):
    names = ("proj_xbc proj_gate tap_now taps_a taps_b conv taps_halo conv_tanh xbc gate_tanh gate turned_x turned_bc moved_bc b_kept "
             "cb_done cb_masked masked_dA stage_dA "
             "d0 d1 d2 d3 e0 e1 e2 e3 m0 m1 m2 m3 x_dt x_dec spread y_diag e_sum e_exp y_off0 y_off1 "
             "s0 s1 decayed0 state0 decayed1 state1 "
             "y_scaled y_both y_skip y_skipped y_gated y_sq out_done sum_sq ms_eps rms xl attn x_loaded0 x_loaded1 pool_passed")
    with loop_semaphores(nc, names) as s, ExitStack() as ctx:
        def sb(name, shape):
            return ctx.enter_context(nc.sbuf_tensor(name, shape, F32))

        def bank(name):
            return ctx.enter_context(nc.psum_tensor(name, [128, 512], F32))
        xw = sb("xw", [128, 2, NB, 2, TAPS - 1 + HALF])
        cv = sb("cv", [128, 2, NB, 2, HALF])
        th = sb("th", [128, 2, NB, TILE])
        gate = sb("gate", [128, 2, CI])
        gth = gate
        cx = sb("cx", [NS, 2, HALF])
        brep = sb("brep", [128, 2, 2, HQ, CH])
        bn = sb("bn", [128, 2, NS])
        cbm = sb("cbm", [128, 2, CT, CH])
        v = sb("v", [128, 2, CT, HG, CH])
        m = v
        dst = sb("dst", [128, 2, CI])
        xdt = sb("xdt", [128, 2, CI])
        xdec = sb("xdec", [128, 2, CI])
        xbd = sb("xbd", [128, 2, CT, HG, HQ * P])
        et = sb("et", [128, 2, CI])
        state = sb("state", [128, 2, CI])
        y = sb("y", [128, 2, CI])
        ysq = et
        xin = sb("xin", [128, 2, H])
        xl = sb("xl", [128, 2, H])
        small = sb("small", [128, 2, 4])
        pa, pb, pc, pd, pg, ph = (bank(f"bank_{k}") for k in ("xbc", "bc", "out", "x", "diag", "off"))
        ring = [bank("ring0"), bank("ring1")]
        cb = [pb[:, 0:HALF], pa[:, 0:HALF]]
        off = [p[:, 0:256].rearrange("p (k t) -> p k t", k=XB) for p in (ph, pc)]

        cleared = once("scan_cleared")
        with nc.Block() as block:
            @block.vector
            def _(dve):
                nc.vector.memset(xw[:], 0.0)
                nc.vector.memset(state[:], 0.0)
                nc.vector.memset(xbd[:], 0.0).then_inc(cleared, 1)
                dve.wait_ge(cleared, 1)

        block = ctx.enter_context(nc.Block())

        @block.sync
        def _(sp):
            with sp.Fori(0, NT // 2) as it:
                for q in range(2):
                    n = 2 * it + q
                    sp.wait_ge(s["xl"], done(n, 2))
                    sp.dma_start(xin[:, q], x_tiles[:, bass.ds(n, 1), :].rearrange("p a b -> p (a b)")).then_inc(s[f"x_loaded{q}"], 16)

        @block.tensor
        def _(pe):
            with pe.Fori(0, NT // 2) as it:
                for q in range(2):
                    n = 2 * it + q
                    xt = [res["tokT"][:, bass.ds(n, 1), k, :].rearrange("p a b -> p (a b)") for k in range(KH)]
                    xbc = cv[:, q].rearrange("p a b c -> p a (b c)")
                    pe.wait_ge(s["cb_masked"], done(n, 1))
                    for b in range(NB):
                        out = pa[:, b * 128:(b + 1) * 128] if b < XB else pb[:, 0:128]
                        for k in range(KH):
                            last = nc.tensor.matmul(out, c["w_xbc"][:, k, b * 128:(b + 1) * 128], xt[k],
                                                    start=(k == 0), stop=(k == KH - 1))
                    last.then_inc(s["proj_xbc"], 1)
                    pe.wait_ge(s["tap_now"], done(n))
                    for b in range(XB):
                        for k in range(KH):
                            last = nc.tensor.matmul(pa[:, b * 128:(b + 1) * 128], c["w_gate"][:, k, b * 128:(b + 1) * 128],
                                                    xt[k], start=(k == 0), stop=(k == KH - 1))
                    last.then_inc(s["proj_gate"], 1)
                    pe.wait_ge(s["xbc"], done(n))
                    pe.wait_ge(s["e_exp"], done(n, 1))
                    for b in range(XB):
                        last = nc.tensor.transpose(pd[:, b * 128:(b + 1) * 128], xbc[:, b, :], c["ident"][:])
                    last.then_inc(s["turned_x"], 1)
                    nc.tensor.transpose(pb[:, 0:128], xbc[:, XB, :], c["ident"][:]).then_inc(s["turned_bc"], 1)
                    pe.wait_ge(s["moved_bc"], done(n))
                    pe.wait_ge(s["b_kept"], done(n))
                    for ch in range(CT):
                        if ch == 2:
                            pe.wait_ge(s["gate"], done(n))
                        b, half = ch // 2, slice(NS * (ch // 2), NS * (ch // 2) + NS)
                        cc = cx[:, q, CH * ch:CH * ch + CH] if b == 0 else xbc[half, XB, CH * ch:CH * ch + CH]
                        last = nc.tensor.matmul(cb[b][:, CH * (ch % 2):CH * (ch % 2) + CH],
                                                brep[half, q, ch % 2].rearrange("p a b -> p (a b)"), cc,
                                                start=True, stop=True)
                    last.then_inc(s["cb_done"], 1)
                    pe.wait_ge(s["masked_dA"], done(n))
                    for ch in range(CT):
                        if ch >= 2:
                            pe.wait_ge(s[f"m{ch - 2}"], done(n))
                        else:
                            pe.wait_ge(s[f"state{ch}"], done(n, 1))
                        nc.tensor.matmul(ring[ch % 2][:], c["later"][:], v[:, q, ch].rearrange("p a b -> p (a b)"),
                                         start=True, stop=True).then_inc(s[f"d{ch}"], 1)
                    pe.wait_ge(s["stage_dA"], done(n))
                    pe.wait_ge(s["x_dec"], done(n))
                    for b in range(XB):
                        last = nc.tensor.matmul(pd[:, b * 128:(b + 1) * 128], dst[:, q, b * 128:(b + 1) * 128],
                                                c["until"][:], start=True, stop=True)
                    last.then_inc(s["e_sum"], 1)
                    pe.wait_ge(s["spread"], done(n))
                    pe.wait_ge(s["y_both"], done(n, 1))
                    for ch in range(CT):
                        pe.wait_ge(s[f"m{ch}"], done(n))
                        for g in range(HG):
                            last = nc.tensor.matmul(pg[32 * (g % 4):32 * (g % 4) + 32,
                                                       128 * (g // 4) + CH * ch:128 * (g // 4) + CH * ch + CH],
                                                    xbd[:, q, ch, g, :], m[:, q, ch, g, :], start=True, stop=True)
                    last.then_inc(s["y_diag"], 1)
                    pe.wait_ge(s["y_scaled"], done(n, 1))
                    pe.wait_ge(s["attn"], done(n, 1))
                    for j in range(2):
                        if j == 0:
                            pe.wait_ge(s["state1"], done(n, 2))
                        else:
                            pe.wait_ge(s["state0"], done(n))
                        for b in range(2):
                            ch, half = 2 * b + j, slice(NS * b, NS * b + NS)
                            cc = cx[:, q, CH * j:CH * j + CH] if b == 0 else xbc[half, XB, CH * ch:CH * ch + CH]
                            for k in range(XB):
                                last = nc.tensor.matmul(off[b][:, k, CH * j:CH * j + CH],
                                                        state[half, q, 128 * k:128 * k + 128], cc, start=True, stop=True)
                        last.then_inc(s[f"y_off{j}"], 1)
                        for b in range(2):
                            ch, rows = 2 * b + j, slice(CH * (2 * b + j), CH * (2 * b + j) + CH)
                            last = nc.tensor.matmul(ring[j][NS * b:NS * b + NS, :], bn[rows, q, :], xdec[rows, q, :],
                                                    start=True, stop=True)
                        last.then_inc(s[f"s{j}"], 1)
                    pe.wait_ge(s["y_gated"], done(n))
                    for b in range(XB):
                        last = nc.tensor.matmul(pc[:, 0:H], y[:, q, b * 128:(b + 1) * 128], c["w_out"][:, b, :],
                                                start=(b == 0), stop=(b == XB - 1))
                    pe.wait_ge(s["y_sq"], done(n))
                    for b in range(XB):
                        last = nc.tensor.matmul(pc[:, H:H + 1], ysq[:, q, b * 128:(b + 1) * 128], c["ones"][:, 0:1],
                                                start=(b == 0), stop=(b == XB - 1))
                    last.then_inc(s["out_done"], 1)

        @block.scalar
        def _(act):
            with act.Fori(0, NT // 2) as it:
                for q in range(2):
                    n = 2 * it + q
                    act.wait_ge(s["proj_xbc"], done(n))
                    act.wait_ge(s["taps_halo"], done(n, 2))
                    act.wait_ge(s["y_skipped"], done(n, 2))
                    act.wait_ge(s["y_off1"], done(n, 2))
                    for b in range(NB):
                        src = pa[:, b * 128:(b + 1) * 128] if b < XB else pb[:, 0:128]
                        src = src.rearrange("p (a t) -> p a t", a=2)
                        nc.scalar.activation(xw[:, q, b, :, TAPS - 1:], src, ACT.Copy)
                        last = nc.scalar.activation(cv[:, q, b], src, ACT.Identity,
                                                    bias=c["conv_b"][:, b:b + 1], scale=c["conv_w"][:, b, TAPS - 1:TAPS])
                    last.then_inc(s["tap_now"], 1)
                    act.wait_ge(s["proj_gate"], done(n))
                    act.wait_ge(s["y_gated"], done(n, 2))
                    nc.scalar.activation(gth[:, q], pa[:], ACT.Tanh, scale=0.5).then_inc(s["gate_tanh"], 1)
                    act.wait_ge(s["conv"], done(n))
                    nc.scalar.activation(th[:, q].rearrange("p a b -> p (a b)"), cv[:, q].rearrange("p a b c -> p (a b c)"),
                                         ACT.Tanh, scale=0.5).then_inc(s["conv_tanh"], 1)
                    act.wait_ge(s["turned_bc"], done(n))
                    act.wait_ge(s["s1"], done(n, 2))
                    nc.scalar.activation(bn[:, q], pb[:, 0:NS], ACT.Copy).then_inc(s["b_kept"], 1)
                    for ch in range(CT):
                        act.wait_ge(s[f"d{ch}"], done(n))
                        nc.scalar.activation(ring[ch % 2][:], ring[ch % 2][:], ACT.Exp).then_inc(s[f"e{ch}"], 1)
                    act.wait_ge(s["x_dt"], done(n))
                    act.wait_ge(s["y_diag"], done(n, 2))
                    for ch in range(CT):
                        for h in range(HQ):
                            src = xdt[CH * ch:CH * ch + CH, q, :].rearrange("p (g h c) -> p g h c", h=HQ, c=P)[:, :, h, :]
                            last = nc.scalar.activation(xbd[CH * h:CH * h + CH, q, ch, :, P * h:P * h + P], src, ACT.Copy)
                    last.then_inc(s["spread"], 1)
                    act.wait_ge(s["e_sum"], done(n))
                    act.wait_ge(s["out_done"], done(n, 2))
                    nc.scalar.activation(et[:, q], pd[:], ACT.Exp).then_inc(s["e_exp"], 1)
                    act.wait_ge(s["y_gated"], done(n))
                    nc.scalar.activation(ysq[:, q], y[:, q], ACT.Square).then_inc(s["y_sq"], 1)
                    act.wait_ge(s[f"x_loaded{q}"], 16 * it + 16 + LEAD)
                    act.wait_ge(s["attn"], done(n, 2))
                    nc.scalar.activation(xl[:, q], xin[:, q], ACT.Identity, bias=res["nbias"][:, bass.ds(n, 1)],
                                         scale=res["rstd"][:, bass.ds(n, 1)]).then_inc(s["xl"], 1)

        @block.gpsimd
        def _(pool):
            with pool.Fori(0, NT // 2) as it:
                for q in range(2):
                    n = 2 * it + q
                    wait_alone(pool, s["e_sum"], done(n, 2), s["pool_passed"])
                    dA = res["dA"][:, bass.ds(n, 1), :].rearrange("p a b -> p (a b)")
                    nc.gpsimd.tensor_copy(dst[:, q].rearrange("p (a b) -> p a b", b=P),
                                          dA[:, :, None].to_broadcast([128, NH, P]))\
                        .then_inc(s["stage_dA"], 1)
                    pool.wait_ge(s["y_diag"], done(n, 2))
                    for ch in range(CT):
                        dA = res["dAp"][:, ch, bass.ds(n, 1), :].rearrange("p a b -> p (a b)")
                        last = nc.gpsimd.tensor_tensor(v[:, q, ch], dA[:, :, None].to_broadcast([128, HG, CH]),
                                                       c["until32"][:, None, :].to_broadcast([128, HG, CH]), ALU.mult)
                    last.then_inc(s["masked_dA"], 1)
                    pool.wait_ge(s["ms_eps"], done(n))
                    nc.gpsimd.tensor_tensor(small[:, q, 1:2], small[:, q, 0:1], c["minus_half"][:, 0:1], ALU.pow)\
                        .then_inc(s["rms"], 1)

        @block.vector
        def _(dve):
            with dve.Fori(0, NT // 2) as it:
                for q in range(2):
                    n = 2 * it + q
                    dve.wait_ge(s["tap_now"], done(n))
                    for k in range(TAPS - 1):
                        if k:
                            dve.wait_ge(s[("taps_a", "taps_b")[k - 1]], done(n))
                        for b in range(NB):
                            last = nc.vector.scalar_tensor_tensor(cv[:, q, b], xw[:, q, b, :, k:k + HALF],
                                                                  c["conv_w"][:, b, k:k + 1], cv[:, q, b],
                                                                  ALU.mult, ALU.add)
                        last.then_inc(s[("taps_a", "taps_b", "conv")[k]], 1)
                    dve.wait_ge(s["conv"], done(n))
                    nc.vector.tensor_copy(xw[:, q, :, :, 0:TAPS - 1], xw[:, q, :, :, HALF:HALF + TAPS - 1])\
                        .then_inc(s["taps_halo"], 1)
                    dve.wait_ge(s["gate_tanh"], done(n))
                    nc.vector.scalar_tensor_tensor(gate[:, q], gth[:, q], 1.0, pa[:], ALU.add, ALU.mult)\
                        .then_inc(s["gate"], 1)
                    dve.wait_ge(s["conv_tanh"], done(n))
                    xbc = cv[:, q].rearrange("p a b c -> p a (b c)")
                    nc.vector.scalar_tensor_tensor(cv[:, q].rearrange("p a b c -> p (a b c)"),
                                                   th[:, q].rearrange("p a b -> p (a b)"), 1.0,
                                                   cv[:, q].rearrange("p a b c -> p (a b c)"), ALU.add, ALU.mult)\
                        .then_inc(s["xbc"], 1)
                    dve.wait_ge(s["xbc"], done(n))
                    dve.wait_ge(s["y_off1"], done(n, 2))
                    nc.vector.tensor_copy(cx[:, q], xbc[NS:2 * NS, XB, 0:HALF])
                    for b in range(2):
                        bt = xbc[0:NS, XB, HALF * b:HALF * b + HALF].rearrange("p (a b) -> p a b", a=2)
                        last = nc.vector.tensor_copy(brep[NS * b:NS * b + NS, q],
                                                     bt[:, :, None, :].to_broadcast([NS, 2, HQ, CH]))
                    last.then_inc(s["moved_bc"], 1)
                    dve.wait_ge(s["turned_x"], done(n))
                    dve.wait_ge(s["spread"], done(n, 2))
                    px = pd[:].rearrange("p (h c) -> p h c", c=P)
                    for out, by, sem in ((xdt, "dt", "x_dt"), (xdec, "to_end", "x_dec")):
                        if sem == "x_dec":
                            dve.wait_ge(s["s1"], done(n, 2))
                        f = res[by][:, bass.ds(n, 1), :].rearrange("p a b -> p (a b)")
                        nc.vector.tensor_tensor(out[:, q].rearrange("p (h c) -> p h c", c=P), px,
                                                f[:, :, None].to_broadcast([128, NH, P]), ALU.mult).then_inc(s[sem], 1)
                    dve.wait_ge(s["cb_done"], done(n))
                    for b in range(2):
                        last = nc.vector.tensor_tensor(cbm[:, q, 2 * b:2 * b + 2], cb[b].rearrange("p (a b) -> p a b", a=2),
                                                       c["until32q"][:, None, :].to_broadcast([128, 2, CH]), ALU.mult)
                    last.then_inc(s["cb_masked"], 1)
                    dve.wait_ge(s["cb_masked"], done(n))
                    dve.wait_ge(s["y_diag"], done(n, 2))
                    for ch in range(CT):
                        dve.wait_ge(s[f"e{ch}"], done(n))
                        nc.vector.tensor_tensor(m[:, q, ch], ring[ch % 2][:].rearrange("p (a b) -> p a b", a=HG),
                                                cbm[:, q, ch][:, None, :].to_broadcast([128, HG, CH]), ALU.mult)\
                            .then_inc(s[f"m{ch}"], 1)
                    for j in range(2):
                        st = state[:, q].rearrange("p (h c) -> p h c", c=P)
                        f = res[f"decay{j}"][:, bass.ds(n, 1), :].rearrange("p a b -> p (a b)")
                        dve.wait_ge(s[f"y_off{j}"], done(n))
                        dve.wait_ge(s["state0" if j else "state1"], done(n) if j else done(n, 2))
                        nc.vector.tensor_tensor(st, st, f[:, :, None].to_broadcast([128, NH, P]), ALU.mult)\
                            .then_inc(s[f"decayed{j}"], 1)
                        dve.wait_ge(s[f"decayed{j}"], done(n))
                        dve.wait_ge(s[f"s{j}"], done(n))
                        nc.vector.tensor_tensor(state[:, q], state[:, q], ring[j][:], ALU.add).then_inc(s[f"state{j}"], 1)
                    dve.wait_ge(s["e_exp"], done(n))
                    dve.wait_ge(s["y_sq"], done(n, 2))
                    dve.wait_ge(s["out_done"], done(n, 2))
                    for b in range(2):
                        yb, eb = (a[:, q].rearrange("p (k b t) -> p k b t", k=XB, b=2)[:, :, b] for a in (y, et))
                        last = nc.vector.scalar_tensor_tensor(yb, off[b], 0.5, eb, ALU.mult, ALU.mult)
                    last.then_inc(s["y_scaled"], 1)
                    dve.wait_ge(s["y_scaled"], done(n))
                    dve.wait_ge(s["y_diag"], done(n))
                    nc.vector.tensor_tensor(y[:, q], y[:, q], pg[:], ALU.add).then_inc(s["y_both"], 1)
                    dve.wait_ge(s["y_both"], done(n))
                    for b in range(XB):
                        last = nc.vector.scalar_tensor_tensor(y[:, q, b * 128:(b + 1) * 128], xbc[:, b, :], c["skip"][:, b:b + 1],
                                                              y[:, q, b * 128:(b + 1) * 128], ALU.mult, ALU.add)
                    last.then_inc(s["y_skipped"], 1)
                    dve.wait_ge(s["y_skipped"], done(n))
                    dve.wait_ge(s["gate"], done(n))
                    nc.vector.scalar_tensor_tensor(y[:, q], y[:, q], 0.5, gate[:, q], ALU.mult, ALU.mult)\
                        .then_inc(s["y_gated"], 1)
                    dve.wait_ge(s["out_done"], done(n))
                    nc.vector.tensor_scalar(small[:, q, 0:1], pc[:, H:H + 1], 1.0 / CI, EPS, ALU.mult, ALU.add)\
                        .then_inc(s["ms_eps"], 1)
                    dve.wait_ge(s["rms"], done(n))
                    dve.wait_ge(s["xl"], done(n))
                    nc.vector.scalar_tensor_tensor(res["attn"][:, bass.ds(n, 1), :].rearrange("p a b -> p (a b)"),
                                                   pc[:, 0:H], small[:, q, 1:2], xl[:, q], ALU.mult, ALU.add)\
                        .then_inc(s["attn"], 1)


def route(nc, once, c, tok, x_tiles, xm_rows, places):
    names = ("x_loaded0 x_loaded1 a_stats a_mean_var a_var a_rstd a_nbias a_norm x2 x2_kept b_stats b_mean_var b_var b_rstd "
             "b_nbias xm turned xm_turned logits top_max exps inv_sum probs top8 top_idx top_f top_sum top_inv "
             "weights scatters_done idx0 sel0 sel1 sel2 sel3 sel4 sel5 pos_done pos_kept slots_f slots own_rows xm_stored0 xm_stored1 dve_passed pool_passed "
             "gu0 gu1 gu2 gate_tanh0 gate_tanh1 gate_tanh2 silu0 silu1 silu2 h0 h1 h2 down down_kept run0 run1 run2 run3")
    with loop_semaphores(nc, names) as s, ExitStack() as ctx:
        def sb(name, shape, dt=F32):
            return ctx.enter_context(nc.sbuf_tensor(name, shape, dt))
        xin = sb("p3_x", [128, 2, GT, H])
        an = sb("p3_an", [128, 2, GT, H])
        x2 = sb("p3_x2", [128, 2, GT, H])
        xm = sb("p3_xm", [128, 2, GT, H])
        xmT = sb("p3_xmT", [128, 2, KH, GT * TILE])
        st = sb("p3_st", [128, 2, 2, GT, 6])
        mv = sb("p3_mv", [128, 2, 2, GT, 2])
        small = sb("p3_small", [128, 2, 12, GT])
        ex = sb("p3_ex", [128, 2, GT, NE])
        top = sb("p3_top", [128, 2, GT, 8])
        idx = sb("p3_idx", [128, 2, GT, 8], mybir.dt.uint32)
        idf = sb("p3_idf", [128, 2, GT, 8])
        sel = sb("p3_sel", [128, 2, GT, NE])
        run = sb("p3_run", [128, 2, GT, NE])
        runs = tok["run"]
        pos = sb("p3_pos", [128, 2, GT, NE])
        junk = sb("p3_junk", [128, 2, GT * TOPK, NE], mybir.dt.bfloat16)
        slot_f = sb("p3_slotf", [128, 2, GT, TOPK])
        slot = sb("p3_slot", [128, 2, GT, TOPK], mybir.dt.uint32)
        own = sb("p3_own", [128, 2, GT])
        blank = an[:].rearrange("p a b c -> p (a b c)")[:, 0:NE * REGION // 256]
        gt = sb("p3_gt", [128, 2, SB, GT * TILE])
        hT = gt
        banks = [ctx.enter_context(nc.psum_tensor(f"p3_bank{k}", [128, 512], F32)) for k in range(8)]
        turn, rt, gbank, ubank, cnt = banks[0:2], banks[2], banks[3:5], banks[5:7], banks[7]
        scattered = [once(f"scattered{q}") for q in range(2)]
        blocks = [(b, min(128, SI - 128 * b)) for b in range(SB)]

        cleared, blanked = once("route_cleared"), once("blanked")
        with nc.Block() as block:
            @block.vector
            def _(dve):
                nc.vector.memset(blank, float(B * T))
                nc.vector.memset(x2[:], 0.0)
                nc.vector.memset(runs[:], 0.0).then_inc(cleared, 1)
                dve.wait_ge(cleared, 1)

            @block.sync
            def _(sp):
                sp.wait_ge(cleared, 1)
                for half in places.rearrange("(a p r) o -> a p (r o)", a=2, p=128):
                    sp.dma_start(half, blank).then_inc(blanked, 16)
                sp.dma_start(xm_rows[B * T:B * T + 128, :], x2[:, 0, 0, :]).then_inc(blanked, 16)
                sp.wait_ge(blanked, 48)

        block = ctx.enter_context(nc.Block())

        @block.sync
        def _(sp):
            with sp.Fori(0, NG // 2) as it:
                for q in range(2):
                    n = 2 * it + q
                    sp.wait_ge(s["x2"], done(n, 2))
                    sp.dma_start(xin[:, q], x_tiles[:, bass.ds(n * GT, GT), :]).then_inc(s[f"x_loaded{q}"], 16)
                for q in range(2):
                    n = 2 * it + q
                    sp.wait_ge(s["xm"], done(n))
                    sp.dma_start(xm_rows[bass.ds(n * GT * TILE, GT * TILE), :].rearrange("(t p) h -> p t h", p=128), xm[:, q])\
                        .then_inc(s[f"xm_stored{q}"], 16)
            for q in range(2):
                sp.wait_ge(s[f"xm_stored{q}"], 16 * (NG // 2) + LEAD)

        @block.vector
        def _(dve):
            def stats(n, q, w, src, names):
                a_stats, a_mean_var, a_var, a_rstd, a_nbias = names
                for t in range(GT):
                    last = nc.vector.bn_stats(st[:, q, w, t, :], src(t))
                last.then_inc(s[a_stats], 1)
                wait_alone(dve, s[a_stats], done(n), s["dve_passed"])
                for t in range(GT):
                    last = nc.vector.bn_aggr(mv[:, q, w, t, :], st[:, q, w, t, :])
                last.then_inc(s[a_mean_var], 1)
                dve.wait_ge(s[a_mean_var], done(n))
                nc.vector.tensor_scalar(small[:, q, 3 * w], mv[:, q, w, :, 1], EPS, None, ALU.add).then_inc(s[a_var], 1)
                dve.wait_ge(s[a_rstd], done(n))
                nc.vector.scalar_tensor_tensor(small[:, q, 3 * w + 2], mv[:, q, w, :, 0], -1.0, small[:, q, 3 * w + 1],
                                               ALU.mult, ALU.mult).then_inc(s[a_nbias], 1)

            with dve.Fori(0, NG // 2) as it:
                for q in range(2):
                    n = 2 * it + q
                    stats(n, q, 0, lambda t: tok["xm"][:, bass.ds(n * GT + t, 1), :].rearrange("p a b -> p (a b)"),
                          ("a_stats", "a_mean_var", "a_var", "a_rstd", "a_nbias"))
                    dve.wait_ge(s["a_norm"], done(n))
                    dve.wait_ge(s[f"x_loaded{q}"], 16 * it + 16 + LEAD)
                    dve.wait_ge(s["x2_kept"], done(n, 2))
                    nc.vector.tensor_tensor(x2[:, q], an[:, q], xin[:, q], ALU.add).then_inc(s["x2"], 1)
                    dve.wait_ge(s["x2"], done(n))
                    stats(n, q, 1, lambda t: x2[:, q, t, :], ("b_stats", "b_mean_var", "b_var", "b_rstd", "b_nbias"))
                    dve.wait_ge(s["logits"], done(n))
                    nc.vector.tensor_reduce(small[:, q, 6], rt[:, 0:GT * NE].rearrange("p (a b) -> p a b", a=GT),
                                            mybir.AxisListType.X, ALU.max, negate=True).then_inc(s["top_max"], 1)
                    for b, rows in blocks:
                        r = (q * SB + b) % 2
                        dve.wait_ge(s[f"gate_tanh{b}"], done(n))
                        nc.vector.scalar_tensor_tensor(gt[0:rows, q, b, :], gt[0:rows, q, b, :], 1.0, gbank[r][0:rows, :],
                                                       ALU.add, ALU.mult).then_inc(s[f"silu{b}"], 1)
                        dve.wait_ge(s[f"silu{b}"], done(n))
                        nc.vector.tensor_tensor(hT[0:rows, q, b, :], gt[0:rows, q, b, :], ubank[r][0:rows, :], ALU.mult)\
                            .then_inc(s[f"h{b}"], 1)
                    dve.wait_ge(s["exps"], done(n))
                    nc.vector.reciprocal(small[:, q, 8], small[:, q, 7]).then_inc(s["inv_sum"], 1)
                    dve.wait_ge(s["inv_sum"], done(n))
                    nc.vector.tensor_tensor(ex[:, q], ex[:, q], small[:, q, 8][:, :, None].to_broadcast([128, GT, NE]),
                                            ALU.mult).then_inc(s["probs"], 1)
                    wait_alone(dve, s["probs"], done(n), s["dve_passed"])
                    for t in range(GT):
                        last = nc.vector.max(top[:, q, t, :], ex[:, q, t, :])
                    last.then_inc(s["top8"], 1)
                    wait_alone(dve, s["top8"], done(n), s["dve_passed"])
                    for t in range(GT):
                        last = nc.vector.max_index(idx[:, q, t, :], top[:, q, t, :], ex[:, q, t, :])
                    last.then_inc(s["top_idx"], 1)
                    dve.wait_ge(s["top_idx"], done(n))
                    nc.vector.tensor_copy(idf[:, q], idx[:, q]).then_inc(s["top_f"], 1)
                    nc.vector.tensor_reduce(small[:, q, 9], top[:, q, :, 0:TOPK], mybir.AxisListType.X, ALU.add)\
                        .then_inc(s["top_sum"], 1)
                    dve.wait_ge(s["top_sum"], done(n))
                    nc.vector.reciprocal(small[:, q, 10], small[:, q, 9]).then_inc(s["top_inv"], 1)
                    dve.wait_ge(s["top_inv"], done(n))
                    nc.vector.tensor_tensor(tok["weight"][:, bass.ds(n * GT, GT), :], top[:, q, :, 0:TOPK],
                                            small[:, q, 10][:, :, None].to_broadcast([128, GT, TOPK]), ALU.mult)\
                        .then_inc(s["weights"], 1)
                    dve.wait_ge(s["top_f"], done(n))
                    dve.wait_ge(s["pos_done"], done(n, 2))
                    for k in range(TOPK):
                        if k:
                            dve.wait_ge(s[f"sel{k - 1}"], done(n))
                        for t in range(GT):
                            if k == 0:
                                last = nc.vector.tensor_scalar(sel[:, q, t, :], c["expert"][:], idf[:, q, t, 0:1], None,
                                                               ALU.is_equal)
                            else:
                                last = nc.vector.scalar_tensor_tensor(sel[:, q, t, :], c["expert"][:], idf[:, q, t, k:k + 1],
                                                                      sel[:, q, t, :], ALU.is_equal, ALU.add)
                        last.then_inc(s[f"sel{k}"], 1)
                    dve.wait_ge(s[f"sel{TOPK - 1}"], done(n))
                    for t in range(GT):
                        before = runs[:] if t == 0 else run[:, q, t, :]
                        after = run[:, q, t + 1, :] if t < GT - 1 else runs[:]
                        if t == 0:
                            dve.wait_ge(s["run3"], done(n, 1))
                            nc.vector.tensor_copy(run[:, q, 0, :], runs[:]).then_inc(s["idx0"], 1)
                            dve.wait_ge(s["idx0"], done(n))
                        else:
                            dve.wait_ge(s[f"run{t - 1}"], done(n))
                        nc.vector.tensor_tensor(after, run[:, q, t, :], sel[:, q, t, :], ALU.add).then_inc(s[f"run{t}"], 1)
                    dve.wait_ge(s["pos_done"], done(n))
                    nc.vector.tensor_tensor(pos[:, q], cnt[:, 0:GT * NE].rearrange("p (a b) -> p a b", a=GT),
                                            c["region"][:, None, :].to_broadcast([128, GT, NE]), ALU.add)\
                        .then_inc(s["pos_kept"], 1)
                    dve.wait_ge(s["pos_kept"], done(n))
                    for t in range(GT):
                        for k in range(TOPK):
                            last = nc.vector.scalar_tensor_tensor(junk[:, q, t * TOPK + k, :], c["expert"][:],
                                                                  idf[:, q, t, k:k + 1], pos[:, q, t, :],
                                                                  ALU.is_equal, ALU.mult,
                                                                  accum_out=slot_f[:, q, t, k:k + 1])
                    last.then_inc(s["slots_f"], 1)
                    dve.wait_ge(s["slots_f"], done(n))
                    dve.wait_ge(s["scatters_done"], done(n, 2))
                    nc.vector.tensor_copy(slot[:, q], slot_f[:, q])
                    nc.vector.tensor_copy(own[:, q], c["token"][:, bass.ds(n * GT, GT)])
                    nc.vector.tensor_copy(tok["choice"][:, bass.ds(n * GT, GT), :], idf[:, q, :, 0:TOPK])
                    nc.vector.tensor_copy(tok["slot"][:, bass.ds(n * GT, GT), :], slot_f[:, q]).then_inc(s["slots"], 1)
        @block.gpsimd
        def _(pool):
            with pool.Fori(0, NG // 2) as it:
                for q in range(2):
                    n = 2 * it + q
                    for w, v, r in ((0, "a_var", "a_rstd"), (1, "b_var", "b_rstd")):
                        pool.wait_ge(s[v], done(n))
                        nc.gpsimd.tensor_tensor(small[:, q, 3 * w + 1], small[:, q, 3 * w], c["minus_half"][:, 0:GT], ALU.pow)\
                            .then_inc(s[r], 1)
                    wait_alone(pool, s["x2"], done(n), s["pool_passed"])
                    nc.gpsimd.tensor_copy(tok["x2"][:, bass.ds(n * GT, GT), :], x2[:, q]).then_inc(s["x2_kept"], 1)
                    wait_alone(pool, s["slots"], done(n), s["pool_passed"])
                    for t in range(GT):
                        for k in range(TOPK):
                            pool.indirect_dma_start(places, bass.IndirectOffsetOnAxis(ap=slot[:, q, t, k:k + 1], axis=0),
                                                    own[:, q, t:t + 1], None).then_inc(scattered[q], 16)
                    wait_alone(pool, scattered[q], 16 * GT * TOPK * it + 16 * GT * TOPK, s["scatters_done"])

        @block.scalar
        def _(act):
            with act.Fori(0, NG // 2) as it:
                for q in range(2):
                    n = 2 * it + q
                    act.wait_ge(s["a_nbias"], done(n))
                    act.wait_ge(s["x2"], done(n, 2))
                    for t in range(GT):
                        last = nc.scalar.activation(an[:, q, t, :],
                                                    tok["xm"][:, bass.ds(n * GT + t, 1), :].rearrange("p a b -> p (a b)"),
                                                    ACT.Identity, bias=small[:, q, 2, t:t + 1], scale=small[:, q, 1, t:t + 1])
                    last.then_inc(s["a_norm"], 1)
                    act.wait_ge(s["b_nbias"], done(n))
                    act.wait_ge(s["turned"], done(n, 2))
                    act.wait_ge(s[f"xm_stored{q}"], 16 * it + LEAD)
                    for t in range(GT):
                        last = nc.scalar.activation(xm[:, q, t, :], x2[:, q, t, :], ACT.Identity,
                                                    bias=small[:, q, 5, t:t + 1], scale=small[:, q, 4, t:t + 1])
                    last.then_inc(s["xm"], 1)
                    act.wait_ge(s["turned"], done(n))
                    act.wait_ge(s["down"], done(n, 2))
                    for k in range(KH):
                        last = nc.scalar.activation(xmT[:, q, k, :], turn[k][:], ACT.Copy)
                    last.then_inc(s["xm_turned"], 1)
                    act.wait_ge(s["top_max"], done(n))
                    act.wait_ge(s["slots_f"], done(n, 2))
                    for t in range(GT):
                        last = nc.scalar.activation(ex[:, q, t, :], rt[:, t * NE:(t + 1) * NE], ACT.Exp,
                                                    bias=small[:, q, 6, t:t + 1], accum_out=small[:, q, 7, t:t + 1])
                    last.then_inc(s["exps"], 1)
                    for b, rows in blocks:
                        act.wait_ge(s[f"gu{b}"], done(n))
                        nc.scalar.activation(gt[0:rows, q, b, :], gbank[(q * SB + b) % 2][0:rows, :], ACT.Tanh, scale=0.5)\
                            .then_inc(s[f"gate_tanh{b}"], 1)
                    act.wait_ge(s["down"], done(n))
                    for t in range(GT):
                        last = nc.scalar.activation(tok["shared"][:, bass.ds(n * GT + t, 1), :].rearrange("p a b -> p (a b)"),
                                                    turn[t // 2][:, H * (t % 2):H * (t % 2) + H], ACT.Copy, scale=0.5)
                    last.then_inc(s["down_kept"], 1)

        @block.tensor
        def _(pe):
            with pe.Fori(0, NG // 2) as it:
                for q in range(2):
                    n = 2 * it + q
                    pe.wait_ge(s["xm"], done(n))
                    pe.wait_ge(s["down_kept"], done(n, 1))
                    for k in range(KH):
                        for t in range(GT):
                            last = nc.tensor.transpose(turn[k][:, t * TILE:(t + 1) * TILE],
                                                       xm[:, q, t, k * 128:(k + 1) * 128], c["ident"][:])
                    last.then_inc(s["turned"], 1)
                    pe.wait_ge(s["xm_turned"], done(n))
                    pe.wait_ge(s["exps"], done(n, 1))
                    for t in range(GT):
                        for k in range(KH):
                            last = nc.tensor.matmul(rt[:, t * NE:(t + 1) * NE], xmT[:, q, k, t * TILE:(t + 1) * TILE],
                                                    c["router_w"][:, k, :], start=(k == 0), stop=(k == KH - 1))
                    last.then_inc(s["logits"], 1)
                    for b, rows in blocks:
                        i = q * SB + b
                        prev = (f"h{b - 2}", 0) if b >= 2 else (f"h{b + 1}", 1)
                        pe.wait_ge(s[prev[0]], done(n, prev[1]))
                        for bank, w in ((gbank, "sg_w"), (ubank, "su_w")):
                            for k in range(KH):
                                last = nc.tensor.matmul(bank[i % 2][0:rows, :], c[w][:, k, 128 * b:128 * b + rows],
                                                        xmT[:, q, k, :], start=(k == 0), stop=(k == KH - 1))
                        last.then_inc(s[f"gu{b}"], 1)
                    pe.wait_ge(s[f"h{SB - 1}"], done(n))
                    for t in range(GT):
                        for b, rows in blocks:
                            last = nc.tensor.matmul(turn[t // 2][:, H * (t % 2):H * (t % 2) + H],
                                                    hT[0:rows, q, b, t * TILE:(t + 1) * TILE], c["sd_w"][0:rows, b, :],
                                                    start=(b == 0), stop=(b == SB - 1))
                    last.then_inc(s["down"], 1)
                    pe.wait_ge(s["run3"], done(n))
                    pe.wait_ge(s["pos_kept"], done(n, 1))
                    nc.tensor.matmul(cnt[:, 0:GT * NE], c["before"][:], sel[:, q].rearrange("p a b -> p (a b)"),
                                     start=True, stop=False)
                    nc.tensor.matmul(cnt[:, 0:GT * NE], c["all"][:], run[:, q].rearrange("p a b -> p (a b)"),
                                     start=False, stop=True).then_inc(s["pos_done"], 1)


def tables(nc, once, c, tok, places, tab_dram, y_rows):
    I32 = mybir.dt.int32
    J = MAXT // 128
    with ExitStack() as ctx:
        def sb(name, shape, dt=F32):
            return ctx.enter_context(nc.sbuf_tensor(name, shape, dt))
        cnt = sb("p4_cnt", [128, NE])
        cnt_i = sb("p4_cnti", [128, NE], I32)
        num = sb("p4_num", [128, NE])
        end = sb("p4_end", [128, NE])
        begin = sb("p4_begin", [128, NE])
        hit = sb("p4_hit", [128, NE])
        first = sb("p4_first", [128, NE])
        one = sb("p4_one", [128, NE])
        cell = sb("p4_cell", [128, J, 6])
        page = sb("p4_page", [128, J], mybir.dt.uint32)
        fields = sb("p4_fields", [128, J, FIELDS], I32)
        listed = sb("p4_listed", [128, J, 128])
        zero = sb("p4_zero", [128, H])
        left = sb("p4_left", [1, 1], I32)
        ps = ctx.enter_context(nc.psum_tensor("p4_ps", [128, NE], F32))
        ps_rows = ctx.enter_context(nc.psum_tensor("p4_rows", [128, MAXT], F32))
        pairs_ready, zeroed, sp_passed = once("pairs_ready"), once("y_rows_zeroed"), once("sp_passed")
        step, counted, fields_ready, pages_ready = once("tables_step"), once("experts_counted"), once("fields_ready"), once("pages_ready")
        fields_stored, fields_loaded, rows_turned = once("fields_stored"), once("fields_loaded"), once("rows_turned")
        listed_loaded = [once(f"listed_loaded{j}") for j in range(J)]
        block = ctx.enter_context(nc.Block())

        @block.tensor
        def _(pe):
            nc.tensor.matmul(ps[:], c["all"][:], tok["run"][:], start=True, stop=True).then_inc(counted, 1)
            for j in range(J):
                pe.wait_ge(listed_loaded[j], 16)
                nc.tensor.transpose(ps_rows[:, 128 * j:128 * j + 128], listed[:, j], c["ident"][:]).then_inc(rows_turned, 1)

        @block.vector
        def _(dve):
            steps = [0]

            def then(ins):
                steps[0] += 1
                ins.then_inc(step, 1)
                dve.wait_ge(step, steps[0])
            nc.vector.memset(one[:], 1.0)
            nc.vector.memset(zero[:], 0.0)
            dve.wait_ge(counted, 1)
            then(nc.vector.tensor_scalar(cnt[:], ps[:], 127.0, None, ALU.add))
            then(nc.vector.tensor_copy(cnt_i[:], cnt[:]))
            then(nc.vector.tensor_scalar(cnt_i[:], cnt_i[:], 7, None, ALU.logical_shift_right))
            then(nc.vector.tensor_copy(num[:], cnt_i[:]))
            then(nc.vector.tensor_scalar(num[:], num[:], 1.0, None, ALU.max))
            then(nc.vector.tensor_tensor_scan(end[:], one[:], num[:], 0.0, ALU.mult, ALU.add))
            then(nc.vector.tensor_tensor(begin[:], end[:], num[:], ALU.subtract))
            nc.vector.scalar_tensor_tensor(tok["shift"][:], begin[:], 128.0, c["region"][:], ALU.mult, ALU.subtract)
            then(nc.vector.memset(tok["freed"][:, 0:2], 0))
            then(nc.vector.tensor_copy(tok["freed"][:, 2:NE], end[0:1, 0:NE - 2]))
            then(nc.vector.tensor_scalar(hit[0:1, 0:1], end[0:1, NE - 1:NE], 1.0, None, ALU.add))
            then(nc.vector.tensor_copy(tok["pairs"][:], hit[0:1, 0:1]))
            then(nc.vector.tensor_scalar(tok["pairs"][:], tok["pairs"][:], 1, None, ALU.logical_shift_right))
            then(nc.vector.tensor_copy(hit[0:1, 1:2], tok["pairs"][:]))
            then(nc.vector.tensor_scalar(hit[0:1, 1:2], hit[0:1, 1:2], -32.0, 16.0 * (MAXT + 1), ALU.mult, ALU.add))
            then(nc.vector.tensor_copy(left[:], hit[0:1, 1:2]))
            dve.sem_inc(pairs_ready, 1)
            for j in range(J):
                t = c["tile"][:, j:j + 1]
                then(nc.vector.scalar_tensor_tensor(hit[:], begin[:], t, one[:], ALU.is_le, ALU.mult,
                                                    accum_out=cell[:, j, 0:1]))
                then(nc.vector.scalar_tensor_tensor(first[:], begin[:], t, begin[:], ALU.is_le, ALU.mult))
                then(nc.vector.tensor_reduce(cell[:, j, 1:2], first[:], mybir.AxisListType.X, ALU.max))
                then(nc.vector.tensor_scalar(cell[:, j, 0:1], cell[:, j, 0:1], -1.0, None, ALU.add))
                then(nc.vector.tensor_tensor(cell[:, j, 2:3], t, cell[:, j, 1:2], ALU.subtract))
                then(nc.vector.tensor_scalar(cell[:, j, 2:3], cell[:, j, 2:3], float(REGION // 128 - 1), None, ALU.min))
                then(nc.vector.tensor_scalar(cell[:, j, 3:4], cell[:, j, 0:1], float(REGION // 128), None, ALU.mult))
                then(nc.vector.tensor_tensor(cell[:, j, 2:3], cell[:, j, 2:3], cell[:, j, 3:4], ALU.add))
                nc.vector.tensor_copy(page[:, j:j + 1], cell[:, j, 2:3]).then_inc(pages_ready, 1)
                then(nc.vector.tensor_copy(fields[:, j, 0:1], cell[:, j, 0:1]))
                then(nc.vector.tensor_scalar(fields[:, j, 1:2], fields[:, j, 0:1], 1, None, ALU.bitwise_and))
            dve.sem_inc(fields_ready, 1)
            dve.wait_ge(rows_turned, J)
            nc.vector.memset(tok["rows"][:, MAXT:MAXT + 2], 0.0)
            then(nc.vector.tensor_copy(tok["rows"][:, 0:MAXT], ps_rows[:]))

        @block.sync
        def _(sp):
            sp.wait_ge(pairs_ready, 1)
            n_pairs = sp.value_load(tok["pairs"][0:1, 0:1], min_val=1, max_val=MAXT // 2)
            with sp.Fori(2 * n_pairs, MAXT + 1) as t:
                sp.dma_start(y_rows[bass.ds(t * 128, 128), :], zero[:]).then_inc(zeroed, 16)
            n_left = sp.value_load(left[0:1, 0:1], min_val=16, max_val=16 * (MAXT + 1))
            wait_alone(sp, zeroed, n_left, sp_passed)

        @block.gpsimd
        def _(pool):
            for j in range(J):
                pool.wait_ge(pages_ready, j + 1)
                pool.indirect_dma_start(listed[:, j], None, places.rearrange("(a b) o -> a (b o)", b=128),
                                        bass.IndirectOffsetOnAxis(ap=page[:, j:j + 1], axis=0)).then_inc(listed_loaded[j], 16)

        @block.scalar
        def _(act):
            act.wait_ge(fields_ready, 1)
            act.dma_start(tab_dram.rearrange("(j p) f -> p j f", p=128), fields[:]).then_inc(fields_stored, 16)
            act.wait_ge(fields_stored, 16)
            act.dma_start(tok["tile"][:], tab_dram.rearrange("t f -> (t f)")[None, :]).then_inc(fields_loaded, 16)
            act.wait_ge(fields_loaded, 16)


def experts(nc, once, c, tok, dram, xm_rows, y_rows):
    x_loaded = [once(f"expert_x_loaded{q}") for q in range(2)]
    names = ("w_loaded turned rows xT h tanh silu h_turned hT y y_kept pool_passed act_passed y_stored0 y_stored1")
    with loop_semaphores(nc, names) as s, ExitStack() as ctx:
        def sb(name, shape, dt=F32):
            return ctx.enter_context(nc.sbuf_tensor(name, shape, dt))

        def banks(name):
            return [ctx.enter_context(nc.psum_tensor(f"p5_{name}{q}", [128, 512], F32)) for q in range(2)]
        w1 = sb("p5_w1", [128, 2, KH * EI])
        w2 = sb("p5_w2", [EK, 2, 2 * H])
        idx = sb("p5_idx", [128, 2, 1], mybir.dt.uint32)
        xe = sb("p5_xe", [128, 2, H])
        xT = sb("p5_xT", [128, 2, KH * TILE])
        th = sb("p5_th", [128, 2, EI])
        hh = sb("p5_h", [128, 2, EI])
        hT = sb("p5_hT", [EK, 2, 2 * TILE])
        ys = sb("p5_y", [128, 2, H])
        ps_x, ps_h, ps_t, ps_y = banks("turn"), banks("h"), banks("ht"), banks("y")
        block = ctx.enter_context(nc.Block())

        def field(eng, n, k, top):
            return eng.value_load(tok["tile"][0:1, bass.ds(n * FIELDS + k, 1)], min_val=0, max_val=top)

        def pairs(eng):
            return eng.value_load(tok["pairs"][0:1, 0:1], min_val=1, max_val=MAXT // 2)

        @block.sync
        def _(sp):
            with sp.Fori(0, NE) as e:
                freed = sp.value_load(tok["freed"][0:1, bass.ds(e, 1)], min_val=0, max_val=MAXT)
                sp.wait_ge(s["y"], freed + LEAD)
                sp.wait_ge(s["w_loaded"], 32 * e + LEAD)
                sp.dma_start(w1[:, bass.ds(e % 2, 1), :].rearrange("p a b -> p (a b)"),
                             dram["w1"][bass.ds(e, 1)].rearrange("a p b -> (a p) b")).then_inc(s["w_loaded"], 16)
                sp.dma_start(w2[:, bass.ds(e % 2, 1), :].rearrange("p a b -> p (a b)"),
                             dram["w2"][bass.ds(e, 1)].rearrange("a p b -> (a p) b")).then_inc(s["w_loaded"], 16)
            sp.wait_ge(s["w_loaded"], 32 * NE + LEAD)

        @block.gpsimd
        def _(pool):
            with pool.Fori(0, pairs(pool)) as it:
                for q in range(2):
                    n = 2 * it + q
                    wait_alone(pool, s["rows"], done(n), s["pool_passed"])
                    wait_alone(pool, s["turned"], done(n, 2), s["pool_passed"])
                    pool.indirect_dma_start(xe[:, q], None, xm_rows, bass.IndirectOffsetOnAxis(ap=idx[:, q], axis=0))\
                        .then_inc(x_loaded[q], 16)

        @block.tensor
        def _(pe):
            with pe.Fori(0, pairs(pe)) as it:
                for q in range(2):
                    n = 2 * it + q
                    e, half = field(pe, n, 0, NE - 1), field(pe, n, 1, 1)
                    pe.wait_ge(x_loaded[q], 16 * it + 16)
                    pe.wait_ge(s["xT"], done(n, 2))
                    for k in range(KH):
                        last = nc.tensor.transpose(ps_x[q][:, k * TILE:(k + 1) * TILE], xe[:, q, k * 128:(k + 1) * 128],
                                                   c["ident"][:])
                    last.then_inc(s["turned"], 1)
                    pe.wait_ge(s["w_loaded"], 32 * e + 32 + LEAD)
                    pe.wait_ge(s["xT"], done(n))
                    pe.wait_ge(s["silu"], done(n, 2))
                    for k in range(KH):
                        last = nc.tensor.matmul(ps_h[q][:, 0:EI], xT[:, q, k * TILE:(k + 1) * TILE],
                                                w1[:, bass.ds(half, 1), k * EI:(k + 1) * EI].rearrange("p a b -> p (a b)"),
                                                start=(k == 0), stop=(k == KH - 1))
                    last.then_inc(s["h"], 1)
                    pe.wait_ge(s["silu"], done(n))
                    pe.wait_ge(s["hT"], done(n, 2))
                    for k in range(2):
                        last = nc.tensor.transpose(ps_t[q][0:EK, k * TILE:(k + 1) * TILE], hh[:, q, k * EK:(k + 1) * EK],
                                                   c["ident"][:])
                    last.then_inc(s["h_turned"], 1)
                    pe.wait_ge(s["hT"], done(n))
                    pe.wait_ge(s["y_kept"], done(n, 2))
                    for k in range(2):
                        last = nc.tensor.matmul(ps_y[q][:, 0:H], hT[:, q, k * TILE:(k + 1) * TILE],
                                                w2[:, bass.ds(half, 1), k * H:(k + 1) * H].rearrange("p a b -> p (a b)"),
                                                start=(k == 0), stop=(k == 1))
                    last.then_inc(s["y"], 1)

        @block.vector
        def _(dve):
            for q in range(2):
                last = nc.vector.tensor_copy(idx[:, q], tok["rows"][:, q:q + 1])
                last.then_inc(s["rows"], 1)
            with dve.Fori(0, pairs(dve)) as it:
                for q in range(2):
                    n = 2 * it + q
                    dve.wait_ge(x_loaded[q], 16 * it + 16)
                    nc.vector.tensor_copy(idx[:, q], tok["rows"][:, bass.ds(n + 2, 1)]).then_inc(s["rows"], 1)
                    dve.wait_ge(s["turned"], done(n))
                    dve.wait_ge(s["h"], done(n, 2))
                    nc.vector.tensor_copy(xT[:, q], ps_x[q][:, 0:KH * TILE]).then_inc(s["xT"], 1)
                    dve.wait_ge(s["tanh"], done(n))
                    dve.wait_ge(s["h_turned"], done(n, 2))
                    nc.vector.scalar_tensor_tensor(hh[:, q], th[:, q], 1.0, ps_h[q][:, 0:EI], ALU.add, ALU.mult)\
                        .then_inc(s["silu"], 1)

        @block.scalar
        def _(act):
            with act.Fori(0, pairs(act)) as it:
                for q in range(2):
                    n = 2 * it + q
                    act.wait_ge(s["h"], done(n))
                    act.wait_ge(s["silu"], done(n, 2))
                    nc.scalar.activation(th[:, q], ps_h[q][:, 0:EI], ACT.Tanh, scale=0.5).then_inc(s["tanh"], 1)
                    act.wait_ge(s["h_turned"], done(n))
                    act.wait_ge(s["y"], done(n, 2))
                    nc.scalar.activation(hT[:, q], ps_t[q][0:EK, 0:2 * TILE], ACT.Copy).then_inc(s["hT"], 1)
                    act.wait_ge(s["y"], done(n))
                    act.wait_ge(s[f"y_stored{q}"], 16 * it + LEAD)
                    nc.scalar.activation(ys[:, q], ps_y[q][:, 0:H], ACT.Copy, scale=0.5).then_inc(s["y_kept"], 1)
                    act.wait_ge(s["y_kept"], done(n))
                    act.dma_start(y_rows[bass.ds(n * 128, 128), :], ys[:, q]).then_inc(s[f"y_stored{q}"], 16)
            n_pairs = pairs(act)
            for q in range(2):
                wait_alone(act, s[f"y_stored{q}"], 16 * n_pairs + LEAD, s["act_passed"])


def combine(nc, once, c, tok, y_rows, out):
    gathered = [once(f"gathered{q}") for q in range(2)]
    names = ("copied shifts slots sum0 sum1 sum2 sum3 sum4 sum5 stats mean_var var rstd nbias norm result pool_passed "
             "dve_passed stored0 stored1")
    with loop_semaphores(nc, names) as s, ExitStack() as ctx:
        def sb(name, shape, dt=F32):
            return ctx.enter_context(nc.sbuf_tensor(name, shape, dt))
        slot = sb("p6_slot", [128, 2, TOPK], mybir.dt.uint32)
        shift = sb("p6_shift", [128, 2, TOPK])
        choice = sb("p6_choice", [128, 2, TOPK])
        junk = sb("p6_junk", [128, 2, TOPK, NE])
        wt = sb("p6_w", [128, 2, TOPK])
        yg = sb("p6_y", [128, 2, TOPK, H])
        acc = sb("p6_acc", [128, 2, H])
        res = sb("p6_res", [128, 2, H])
        st = sb("p6_st", [128, 2, 6])
        mv = sb("p6_mv", [128, 2, 2])
        small = sb("p6_small", [128, 2, 4])
        block = ctx.enter_context(nc.Block())

        @block.gpsimd
        def _(pool):
            with pool.Fori(0, NT // 2) as it:
                for q in range(2):
                    n = 2 * it + q
                    wait_alone(pool, s["slots"], done(n), s["pool_passed"])
                    wait_alone(pool, s[f"sum{TOPK - 1}"], done(n, 2), s["pool_passed"])
                    for k in range(TOPK):
                        pool.indirect_dma_start(yg[:, q, k, :], None, y_rows,
                                                bass.IndirectOffsetOnAxis(ap=slot[:, q, k:k + 1], axis=0))\
                            .then_inc(gathered[q], 16)
                    if q == 1:
                        for r in range(2):
                            pool.wait_ge(s["var"], done(2 * it + r))
                            nc.gpsimd.tensor_tensor(small[:, r, 1:2], small[:, r, 0:1], c["minus_half"][:, 0:1], ALU.pow)\
                                .then_inc(s["rstd"], 1)

        @block.vector
        def _(dve):
            with dve.Fori(0, NT // 2) as it:
                for q in range(2):
                    n = 2 * it + q
                    dve.wait_ge(s[f"sum{TOPK - 1}"], done(n, 2))
                    nc.vector.tensor_copy(wt[:, q], tok["weight"][:, bass.ds(n, 1), :].rearrange("p a b -> p (a b)"))
                    nc.vector.tensor_copy(choice[:, q], tok["choice"][:, bass.ds(n, 1), :].rearrange("p a b -> p (a b)"))\
                        .then_inc(s["copied"], 1)
                    dve.wait_ge(s["copied"], done(n))
                    for k in range(TOPK):
                        last = nc.vector.scalar_tensor_tensor(junk[:, q, k], c["expert"][:], choice[:, q, k:k + 1],
                                                              tok["shift"][:], ALU.is_equal, ALU.mult,
                                                              accum_out=shift[:, q, k:k + 1])
                    last.then_inc(s["shifts"], 1)
                    dve.wait_ge(s["shifts"], done(n))
                    nc.vector.tensor_tensor(slot[:, q], tok["slot"][:, bass.ds(n, 1), :].rearrange("p a b -> p (a b)"),
                                            shift[:, q], ALU.add).then_inc(s["slots"], 1)
                for q in range(2):
                    n = 2 * it + q
                    dve.wait_ge(gathered[q], 16 * TOPK * it + 16 * TOPK)
                    dve.wait_ge(s["slots"], done(n))
                    dve.wait_ge(s["norm"], done(n, 2))
                    for k in range(TOPK):
                        if k:
                            dve.wait_ge(s[f"sum{k - 1}"], done(n))
                        before = acc[:, q] if k else tok["shared"][:, bass.ds(n, 1), :].rearrange("p a b -> p (a b)")
                        nc.vector.scalar_tensor_tensor(acc[:, q], yg[:, q, k, :], wt[:, q, k:k + 1], before,
                                                       ALU.mult, ALU.add).then_inc(s[f"sum{k}"], 1)
                    dve.wait_ge(s[f"sum{TOPK - 1}"], done(n))
                    nc.vector.bn_stats(st[:, q], acc[:, q]).then_inc(s["stats"], 1)
                    wait_alone(dve, s["stats"], done(n), s["dve_passed"])
                    nc.vector.bn_aggr(mv[:, q], st[:, q]).then_inc(s["mean_var"], 1)
                    dve.wait_ge(s["mean_var"], done(n))
                    nc.vector.tensor_scalar(small[:, q, 0:1], mv[:, q, 1:2], EPS, None, ALU.add).then_inc(s["var"], 1)
                for q in range(2):
                    n = 2 * it + q
                    dve.wait_ge(s["rstd"], done(n))
                    nc.vector.scalar_tensor_tensor(small[:, q, 2:3], mv[:, q, 0:1], -1.0, small[:, q, 1:2],
                                                   ALU.mult, ALU.mult).then_inc(s["nbias"], 1)
                    dve.wait_ge(s["norm"], done(n))
                    dve.wait_ge(s[f"stored{q}"], 16 * it + LEAD)
                    nc.vector.tensor_tensor(res[:, q], acc[:, q], tok["x2"][:, bass.ds(n, 1), :].rearrange("p a b -> p (a b)"),
                                            ALU.add).then_inc(s["result"], 1)

        @block.scalar
        def _(act):
            with act.Fori(0, NT // 2) as it:
                for q in range(2):
                    n = 2 * it + q
                    act.wait_ge(s["nbias"], done(n))
                    nc.scalar.activation(acc[:, q], acc[:, q], ACT.Identity, bias=small[:, q, 2:3], scale=small[:, q, 1:2])\
                        .then_inc(s["norm"], 1)

        @block.sync
        def _(sp):
            with sp.Fori(0, NT // 2) as it:
                for q in range(2):
                    n = 2 * it + q
                    sp.wait_ge(s["result"], done(n))
                    sp.dma_start(out[:, bass.ds(n, 1), :].rearrange("p a b -> p (a b)"), res[:, q])\
                        .then_inc(s[f"stored{q}"], 16)
            for q in range(2):
                sp.wait_ge(s[f"stored{q}"], 16 * (NT // 2) + LEAD)


def build(nc, src, dram, out):
    xm_rows = nc.dram_tensor("xm_rows", (B * T + 128, H), F32, kind="Internal").ap()
    places = nc.dram_tensor("places", (NE * REGION, 1), F32, kind="Internal").ap()
    y_rows = nc.dram_tensor("y_rows", (MAXT * 128 + 128, H), F32, kind="Internal").ap()
    tab_dram = nc.dram_tensor("tile_table", (MAXT, FIELDS), mybir.dt.int32, kind="Internal").ap()
    with ExitStack() as ctx:
        def sb(name, shape, dt=F32):
            return ctx.enter_context(nc.sbuf_tensor(name, shape, dt))
        def once(name):
            return ctx.enter_context(nc.semaphore(name))
        c = load_constants(nc, sb, once, src)
        tokT = sb("tokT", [128, NT, KH, TILE])
        attn = tokT[:].rearrange("p n k t -> p n (k t)")
        with ExitStack() as inner:
            res = {"tokT": tokT, "attn": attn}
            for name, shape in (("rstd", [128, NT]), ("nbias", [128, NT]), ("dt", [128, NT, NH]), ("dA", [128, NT, NH]),
                                ("to_end", [128, NT, NH]), ("decay0", [128, NT, NH]), ("decay1", [128, NT, NH]),
                                ("dAp", [128, CT, NT, HG])):
                res[name] = inner.enter_context(nc.sbuf_tensor("r_" + name, shape, F32))
            norm_in(nc, c, res, dram["x"])
            decays(nc, c, res)
            scan(nc, once, c, res, dram["x"])
        tok = {"xm": attn, "x2": sb("x2", [128, NT, H]), "shared": sb("shared", [128, NT, H]),
               "weight": sb("weight", [128, NT, TOPK]), "slot": sb("slot", [128, NT, TOPK]),
               "choice": sb("choice", [128, NT, TOPK]), "shift": sb("shift", [128, NE]), "rows": sb("rows", [128, MAXT + 2]),
               "run": sb("run", [128, NE]), "tile": sb("tile", [1, MAXT * FIELDS], mybir.dt.int32),
               "freed": sb("freed", [1, NE], mybir.dt.int32), "pairs": sb("pairs", [1, 1], mybir.dt.int32)}
        route(nc, once, c, tok, dram["x"], xm_rows, places)
        tables(nc, once, c, tok, places, tab_dram, y_rows)
        experts(nc, once, c, tok, dram, xm_rows, y_rows)
        combine(nc, once, c, tok, y_rows, out)


def constants():
    p, l = np.arange(128)[:, None], np.arange(128)[None, :]
    same = (p // CH) == (l // CH)
    f = np.float32
    k = {"ident": np.eye(128), "ones": np.ones((128, 4)), "minus_half": np.full((128, 8), -0.5)}
    k["later"] = same & (p > l)
    k["until"] = same & (p <= l)
    k["until32"] = (p % CH) <= l[:, :CH]
    k["until32q"] = 0.25 * ((p % CH) <= l[:, :CH])
    for j in range(2):
        k[f"whole{j}"] = (p // CH) == 2 * (l // NS) + j
    k["before"] = p < l
    k["all"] = np.ones((128, 128))
    k["expert"] = np.broadcast_to(np.arange(NE), (128, NE))
    k["region"] = np.broadcast_to(np.arange(NE) * REGION, (128, NE))
    k["token"] = np.arange(B * T).reshape(NT, 128).T
    k["tile"] = np.arange(MAXT).reshape(-1, 128).T
    return {n: np.ascontiguousarray(a, dtype=f) for n, a in k.items()}


def kernel(L0_attn_hidden_states, L0_attn_ln_weight, L0_attn_in_proj_w, L0_attn_conv_w, L0_attn_conv_b, L0_attn_dt_bias,
           L0_attn_A_log, L0_attn_D, L0_attn_norm_weight, L0_attn_out_proj_w, L0_ffn_gate_w, L0_ffn_experts_w1,
           L0_ffn_experts_w2, L0_ffn_shared_gate_up, L0_ffn_shared_down):
    import concourse.bacc as bacc
    from concourse.bass_utils import run_bass_kernel_spmd

    def columns(a):
        return np.asarray(a).reshape(-1, 128).T

    def rows(a):
        a = np.asarray(a)
        return a.reshape(-1, 128, a.shape[1]).transpose(1, 0, 2)

    def everywhere(a):
        return np.broadcast_to(np.asarray(a), (128, len(a)))

    x = np.asarray(L0_attn_hidden_states)
    tiles = x.reshape(PAIRS, 2, NT // PAIRS, HALF, H).transpose(1, 3, 2, 0, 4).reshape(128, NT, H)
    w_in = np.asarray(L0_attn_in_proj_w)
    arrays = constants()
    arrays["w_gate"] = rows(w_in[:CI].T)
    arrays["w_xbc"] = rows(w_in[CI:CI + NB * 128].T)
    arrays["w_dt"] = rows(w_in[CI + NB * 128:].T)
    arrays["w_out"] = rows(np.asarray(L0_attn_out_proj_w).T)
    arrays["ln_w"] = columns(L0_attn_ln_weight)
    arrays["norm_w"] = columns(L0_attn_norm_weight)
    arrays["conv_b"] = columns(L0_attn_conv_b)
    arrays["conv_w"] = rows(L0_attn_conv_w)
    arrays["skip"] = columns(np.repeat(np.asarray(L0_attn_D), P))
    arrays["dt_bias"] = everywhere(L0_attn_dt_bias)
    arrays["a_log"] = everywhere(L0_attn_A_log)
    gu = np.asarray(L0_ffn_shared_gate_up).T
    arrays["router_w"] = rows(np.asarray(L0_ffn_gate_w).T)
    arrays["sg_w"] = rows(gu[:, :SI])
    arrays["su_w"] = rows(gu[:, SI:])
    down = np.zeros((SB * 128, H), np.float32)
    down[:SI] = np.asarray(L0_ffn_shared_down).T
    arrays["sd_w"] = rows(down)
    arrays = {n: np.ascontiguousarray(a) for n, a in arrays.items()}
    w1 = np.asarray(L0_ffn_experts_w1).transpose(0, 2, 1).reshape(NE, KH, 128, EI).transpose(0, 2, 1, 3)
    w2 = np.asarray(L0_ffn_experts_w2).transpose(0, 2, 1).reshape(NE, 2, EK, H).transpose(0, 2, 1, 3)
    big = {"x": tiles, "w1": w1.reshape(NE, 128, KH * EI), "w2": w2.reshape(NE, EK, 2 * H)}
    big = {n: np.ascontiguousarray(a) for n, a in big.items()}

    nc = bacc.Bacc("TRN2", target_bir_lowering=False, num_devices=1)
    src = {n: nc.dram_tensor("in_" + n, a.shape, F32, kind="ExternalInput").ap() for n, a in arrays.items()}
    dram = {n: nc.dram_tensor("in_" + n, a.shape, F32, kind="ExternalInput").ap() for n, a in big.items()}
    out = nc.dram_tensor("out", (128, NT, H), F32, kind="ExternalOutput").ap()
    build(nc, src, dram, out)
    feed = {"in_" + n: a for n, a in (arrays | big).items()}
    got = run_bass_kernel_spmd(nc, [feed], core_ids=[0]).results[0]["out"]
    return got.reshape(2, HALF, NT // PAIRS, PAIRS, H).transpose(3, 0, 2, 1, 4).reshape(B, T, H)
```

```python
import numpy as np
import concourse.bass as bass
from concourse import mybir
from contextlib import ExitStack, contextmanager

F32 = mybir.dt.float32
ALU = mybir.AluOpType
ACT = mybir.ActivationFunctionType

B, T, H = 4, 1024, 256
CI, NS, NH, P = 512, 64, 64, 8
TAPS, CH = 4, 32
EPS = 1e-5
TILE = 128
NT = B * T // TILE
HALF = TILE // 2
PAIRS = B // 2
KH = H // 128
XB = CI // 128
NB = XB + 1
CT = TILE // CH
HQ = 4
HG = NH // HQ
GT = 4
NG = NT // GT
NE, EI, TOPK = 64, 176, 6
EK = EI // 2
SI = 2 * EI
SB = -(-SI // 128)
REGION = B * T + 128
MAXT = 256
assert MAXT >= B * T * TOPK // 128 + NE
FIELDS = 2
LEAD = 2


def done(n, back=0):
    return n + 1 + LEAD - back


def wait_alone(eng, sem, value, passed):
    eng.wait_ge(sem, value)
    eng.sem_inc(passed, 1)


@contextmanager
def loop_semaphores(nc, names):
    with ExitStack() as ctx:
        sems = {name: ctx.enter_context(nc.semaphore(name)) for name in names.split()}
        with nc.Block() as block:
            @block.vector
            def _(dve):
                for s in sems.values():
                    dve.sem_inc(s, LEAD)
        yield sems
        with nc.Block() as block:
            @block.vector
            def _(dve):
                for s in sems.values():
                    dve.sem_clear(s)


def load_constants(nc, sb, once, src):
    c = {}
    loaded, scaled = once("constants_loaded"), once("constants_scaled")
    for name, ap in src.items():
        c[name] = sb("c_" + name, list(ap.shape), F32)
    with nc.Block() as block:
        @block.sync
        def _(sp):
            for name, ap in src.items():
                sp.dma_start(c[name][:], ap).then_inc(loaded, 16)
            sp.wait_ge(loaded, 16 * len(src))

        @block.scalar
        def _(act):
            act.wait_ge(loaded, 16 * len(src))
            nc.scalar.activation(c["a_log"][:], c["a_log"][:], ACT.Exp).then_inc(scaled, 1)

        @block.vector
        def _(dve):
            dve.wait_ge(loaded, 16 * len(src))
            for b in range(XB):
                nc.vector.tensor_scalar(c["w_out"][:, b, :], c["w_out"][:, b, :],
                                        c["norm_w"][:, b:b + 1], None, ALU.mult)
            nc.vector.tensor_scalar(c["skip"][:], c["skip"][:], 0.5, None, ALU.mult).then_inc(scaled, 1)
            dve.wait_ge(scaled, 2)
    return c


def norm_in(nc, c, res, x_tiles):
    names = ("x_loaded0 x_loaded1 stats mean_var var_eps rstd nbias ln sum_sq ms_eps rms xn turned "
             "scaled kept dt_done dt_kept kept_stats dve_passed pool_passed")
    with loop_semaphores(nc, names) as s, ExitStack() as ctx:
        def sb(name, shape):
            return ctx.enter_context(nc.sbuf_tensor(name, shape, F32))
        xin = sb("p1_x", [128, 2, GT, H])
        xl = sb("p1_xl", [128, 2, GT, H])
        sq = sb("p1_sq", [128, 2, GT, H])
        st = sb("p1_st", [128, 2, GT, 6])
        mv = sb("p1_mv", [128, 2, GT, 2])
        small = sb("p1_small", [128, 2, 6, GT])
        xs = sb("p1_xs", [128, 2, KH, GT * TILE])
        ps_turn = [[ctx.enter_context(nc.psum_tensor(f"p1_turn{q}{k}", [128, GT * TILE], F32)) for k in range(KH)]
                   for q in range(2)]
        ps_dt = [ctx.enter_context(nc.psum_tensor(f"p1_dt{q}", [128, GT, NH], F32)) for q in range(2)]
        block = ctx.enter_context(nc.Block())

        @block.sync
        def _(sp):
            with sp.Fori(0, NG // 2) as it:
                for q in range(2):
                    n = 2 * it + q
                    sp.wait_ge(s["ln"], done(n, 2))
                    sp.dma_start(xin[:, q], x_tiles[:, bass.ds(n * GT, GT), :]).then_inc(s[f"x_loaded{q}"], 16)

        @block.vector
        def _(dve):
            with dve.Fori(0, NG // 2) as it:
                for q in range(2):
                    n = 2 * it + q
                    veps, mseps = small[:, q, 0], small[:, q, 1]
                    dve.wait_ge(s[f"x_loaded{q}"], 16 * it + 16 + LEAD)
                    for t in range(GT):
                        last = nc.vector.bn_stats(st[:, q, t, :], xin[:, q, t, :])
                    last.then_inc(s["stats"], 1)
                    wait_alone(dve, s["stats"], done(n), s["dve_passed"])
                    for t in range(GT):
                        last = nc.vector.bn_aggr(mv[:, q, t, :], st[:, q, t, :])
                    last.then_inc(s["mean_var"], 1)
                    dve.wait_ge(s["mean_var"], done(n))
                    nc.vector.tensor_scalar(veps, mv[:, q, :, 1], EPS, None, ALU.add).then_inc(s["var_eps"], 1)
                    dve.wait_ge(s["rstd"], done(n))
                    nc.vector.scalar_tensor_tensor(small[:, q, 3], mv[:, q, :, 0], -1.0, small[:, q, 2],
                                                   ALU.mult, ALU.mult).then_inc(s["nbias"], 1)
                    dve.wait_ge(s["nbias"], done(n))
                    nc.vector.tensor_copy(res["rstd"][:, bass.ds(n * GT, GT)], small[:, q, 2])
                    nc.vector.tensor_copy(res["nbias"][:, bass.ds(n * GT, GT)], small[:, q, 3]).then_inc(s["kept_stats"], 1)
                    dve.wait_ge(s["sum_sq"], done(n))
                    nc.vector.tensor_scalar(mseps, small[:, q, 4], 1.0 / H, EPS, ALU.mult, ALU.add)\
                        .then_inc(s["ms_eps"], 1)
                    dve.wait_ge(s["rms"], done(n))
                    for t in range(GT):
                        last = nc.vector.tensor_scalar(xl[:, q, t, :], xl[:, q, t, :], small[:, q, 5, t:t + 1],
                                                       None, ALU.mult)
                    last.then_inc(s["xn"], 1)
                    dve.wait_ge(s["dt_done"], done(n))
                    nc.vector.tensor_tensor(res["dt"][:, bass.ds(n * GT, GT), :], ps_dt[q][:, :, :],
                                            c["dt_bias"][:, None, :].to_broadcast([128, GT, NH]),
                                            ALU.add).then_inc(s["dt_kept"], 1)

        @block.gpsimd
        def _(pool):
            with pool.Fori(0, NG // 2) as it:
                for q in range(2):
                    n = 2 * it + q
                    pool.wait_ge(s["var_eps"], done(n))
                    nc.gpsimd.tensor_tensor(small[:, q, 2], small[:, q, 0], c["minus_half"][:, 0:GT], ALU.pow)\
                        .then_inc(s["rstd"], 1)
                    pool.wait_ge(s["ms_eps"], done(n))
                    nc.gpsimd.tensor_tensor(small[:, q, 5], small[:, q, 1], c["minus_half"][:, 0:GT], ALU.pow)\
                        .then_inc(s["rms"], 1)
                    wait_alone(pool, s["scaled"], done(n), s["pool_passed"])
                    for k in range(KH):
                        last = nc.gpsimd.tensor_copy(res["tokT"][:, bass.ds(n * GT, GT), k, :],
                                                     xs[:, q, k, :].rearrange("p (a b) -> p a b", a=GT))
                    last.then_inc(s["kept"], 1)

        @block.scalar
        def _(act):
            with act.Fori(0, NG // 2) as it:
                for q in range(2):
                    n = 2 * it + q
                    act.wait_ge(s["nbias"], done(n))
                    act.wait_ge(s["turned"], done(n, 2))
                    for t in range(GT):
                        last = nc.scalar.activation(xl[:, q, t, :], xin[:, q, t, :], ACT.Identity,
                                                    bias=small[:, q, 3, t:t + 1], scale=small[:, q, 2, t:t + 1])
                    last.then_inc(s["ln"], 1)
                    act.wait_ge(s["ln"], done(n))
                    for t in range(GT):
                        last = nc.scalar.activation(sq[:, q, t, :], xl[:, q, t, :], ACT.Square,
                                                    accum_out=small[:, q, 4, t:t + 1])
                    last.then_inc(s["sum_sq"], 1)
                    act.wait_ge(s["turned"], done(n))
                    act.wait_ge(s["kept"], done(n, 2))
                    act.wait_ge(s["dt_done"], done(n, 2))
                    for k in range(KH):
                        last = nc.scalar.activation(xs[:, q, k, :], ps_turn[q][k][:, :], ACT.Identity,
                                                    scale=c["ln_w"][:, k:k + 1])
                    last.then_inc(s["scaled"], 1)

        @block.tensor
        def _(pe):
            with pe.Fori(0, NG // 2) as it:
                for q in range(2):
                    n = 2 * it + q
                    pe.wait_ge(s["xn"], done(n))
                    pe.wait_ge(s["scaled"], done(n, 2))
                    for k in range(KH):
                        for t in range(GT):
                            last = nc.tensor.transpose(ps_turn[q][k][:, t * TILE:(t + 1) * TILE],
                                                       xl[:, q, t, k * 128:(k + 1) * 128], c["ident"][:])
                    last.then_inc(s["turned"], 1)
                    pe.wait_ge(s["scaled"], done(n))
                    pe.wait_ge(s["dt_kept"], done(n, 2))
                    for t in range(GT):
                        for k in range(KH):
                            last = nc.tensor.matmul(ps_dt[q][:, t, :], xs[:, q, k, t * TILE:(t + 1) * TILE],
                                                    c["w_dt"][:, k, :], start=(k == 0), stop=(k == KH - 1))
                    last.then_inc(s["dt_done"], 1)


def decays(nc, c, res):
    QT = 8
    NQ = NT // QT
    W = QT * NH
    names = "absolute small_exp one_more log correction correction2 halved softplus dA sums exps states_dt permuted permuted_kept"
    with loop_semaphores(nc, names) as s, ExitStack() as ctx:
        def sb(name, shape):
            return ctx.enter_context(nc.sbuf_tensor(name, shape, F32))
        e = sb("p2_e", [128, W])
        u = sb("p2_u", [128, W])
        lg = sb("p2_l", [128, W])
        ps = [ctx.enter_context(nc.psum_tensor(f"p2_sum{k}", [128, W], F32)) for k in range(3)]
        ps_perm = [ctx.enter_context(nc.psum_tensor(f"p2_perm{k}", [128, W], F32)) for k in range(CT)]
        block = ctx.enter_context(nc.Block())

        def piece(name, n):
            return res[name][:, n * QT:(n + 1) * QT, :].rearrange("p a b -> p (a b)")

        @block.scalar
        def _(act):
            for n in range(NQ):
                act.wait_ge(s["correction"], done(n, 1))
                nc.scalar.activation(e[:], piece("dt", n), ACT.Abs).then_inc(s["absolute"], 1)
                act.wait_ge(s["absolute"], done(n))
                nc.scalar.activation(e[:], e[:], ACT.Exp, scale=-1.0).then_inc(s["small_exp"], 1)
                act.wait_ge(s["one_more"], done(n))
                nc.scalar.activation(lg[:], u[:], ACT.Ln).then_inc(s["log"], 1)
                act.wait_ge(s["sums"], done(n))
                for k, name in enumerate(("to_end", "decay0", "decay1")):
                    last = nc.scalar.activation(piece(name, n), ps[k][:], ACT.Exp)
                last.then_inc(s["exps"], 1)
                act.wait_ge(s["permuted"], done(n))
                for ch in range(CT):
                    last = nc.scalar.activation(res["dAp"][:, ch, n * QT:(n + 1) * QT, :],
                                                ps_perm[ch][:, 0:QT * HG].rearrange("p (a b) -> p a b", a=QT),
                                                ACT.Copy)
                last.then_inc(s["permuted_kept"], 1)

        @block.vector
        def _(dve):
            for n in range(NQ):
                z = piece("dt", n)
                dve.wait_ge(s["small_exp"], done(n))
                nc.vector.tensor_scalar(u[:], e[:], 1.0, None, ALU.add).then_inc(s["one_more"], 1)
                dve.wait_ge(s["log"], done(n))
                nc.vector.scalar_tensor_tensor(u[:], u[:], -1.0, e[:], ALU.add, ALU.subtract).then_inc(s["correction"], 1)
                dve.wait_ge(s["correction"], done(n))
                nc.vector.tensor_tensor(u[:], lg[:], u[:], ALU.subtract).then_inc(s["correction2"], 1)
                dve.wait_ge(s["correction2"], done(n))
                nc.vector.scalar_tensor_tensor(z, z, 0.0, u[:], ALU.max, ALU.add).then_inc(s["softplus"], 1)
                dve.wait_ge(s["softplus"], done(n))
                nc.vector.scalar_tensor_tensor(res["dA"][:, n * QT:(n + 1) * QT, :], res["dt"][:, n * QT:(n + 1) * QT, :], -1.0,
                                               c["a_log"][:, None, :].to_broadcast([128, QT, NH]),
                                               ALU.mult, ALU.mult).then_inc(s["dA"], 1)
                dve.wait_ge(s["exps"], done(n))
                nc.vector.scalar_tensor_tensor(piece("to_end", n), piece("to_end", n), 0.25, z, ALU.mult, ALU.mult)\
                    .then_inc(s["states_dt"], 1)
                dve.wait_ge(s["dA"], done(n))
                dve.wait_ge(s["states_dt"], done(n))
                nc.vector.tensor_scalar(z, z, 0.5, None, ALU.mult).then_inc(s["halved"], 1)

        @block.tensor
        def _(pe):
            for n in range(NQ):
                pe.wait_ge(s["dA"], done(n))
                pe.wait_ge(s["exps"], done(n, 1))
                dA = piece("dA", n)
                for k, name in enumerate(("later", "whole0", "whole1")):
                    last = nc.tensor.matmul(ps[k][:], c[name][:], dA, start=True, stop=True)
                last.then_inc(s["sums"], 1)
                pe.wait_ge(s["permuted_kept"], done(n, 1))
                for ch in range(CT):
                    rows = slice(CH * ch, CH * ch + CH)
                    for h in range(HQ):
                        src = res["dA"][rows, n * QT:(n + 1) * QT, :].rearrange("p a (g h) -> p a g h", h=HQ)[:, :, :, h]
                        last = nc.tensor.matmul(ps_perm[ch][CH * h:CH * h + CH, 0:QT * HG], c["ident"][rows, rows], src,
                                                start=True, stop=True)
                last.then_inc(s["permuted"], 1)


def scan(nc, once, c, res, x_tiles):
    names = ("proj_xbc proj_gate tap_now taps_a taps_b conv taps_halo conv_tanh xbc gate_tanh gate turned_x turned_bc moved_bc b_kept "
             "cb_done cb_masked masked_dA stage_dA "
             "d0 d1 d2 d3 e0 e1 e2 e3 m0 m1 m2 m3 x_dt x_dec spread y_diag e_sum e_exp y_off0 y_off1 "
             "s0 s1 decayed0 state0 decayed1 state1 "
             "y_scaled y_both y_skip y_skipped y_gated y_sq out_done sum_sq ms_eps rms xl attn x_loaded0 x_loaded1 pool_passed")
    with loop_semaphores(nc, names) as s, ExitStack() as ctx:
        def sb(name, shape):
            return ctx.enter_context(nc.sbuf_tensor(name, shape, F32))

        def bank(name):
            return ctx.enter_context(nc.psum_tensor(name, [128, 512], F32))
        xw = sb("xw", [128, 2, NB, 2, TAPS - 1 + HALF])
        cv = sb("cv", [128, 2, NB, 2, HALF])
        th = sb("th", [128, 2, NB, TILE])
        gate = sb("gate", [128, 2, CI])
        gth = gate
        cx = sb("cx", [NS, 2, HALF])
        brep = sb("brep", [128, 2, 2, HQ, CH])
        bn = sb("bn", [128, 2, NS])
        cbm = sb("cbm", [128, 2, CT, CH])
        v = sb("v", [128, 2, CT, HG, CH])
        m = v
        dst = sb("dst", [128, 2, CI])
        xdt = sb("xdt", [128, 2, CI])
        xdec = sb("xdec", [128, 2, CI])
        xbd = sb("xbd", [128, 2, CT, HG, HQ * P])
        et = sb("et", [128, 2, CI])
        state = sb("state", [128, 2, CI])
        y = sb("y", [128, 2, CI])
        ysq = et
        xin = sb("xin", [128, 2, H])
        xl = sb("xl", [128, 2, H])
        small = sb("small", [128, 2, 4])
        pa, pb, pc, pd, pg, ph = (bank(f"bank_{k}") for k in ("xbc", "bc", "out", "x", "diag", "off"))
        ring = [bank("ring0"), bank("ring1")]
        cb = [pb[:, 0:HALF], pa[:, 0:HALF]]
        off = [p[:, 0:256].rearrange("p (k t) -> p k t", k=XB) for p in (ph, pc)]

        cleared = once("scan_cleared")
        with nc.Block() as block:
            @block.vector
            def _(dve):
                nc.vector.memset(xw[:], 0.0)
                nc.vector.memset(state[:], 0.0)
                nc.vector.memset(xbd[:], 0.0).then_inc(cleared, 1)
                dve.wait_ge(cleared, 1)

        block = ctx.enter_context(nc.Block())


        @block.sync
        def _(sp):
            with sp.Fori(0, NT // 2) as it:
                for q in range(2):
                    n = 2 * it + q
                    sp.wait_ge(s["xl"], done(n, 2))
                    sp.dma_start(xin[:, q], x_tiles[:, bass.ds(n, 1), :].rearrange("p a b -> p (a b)")).then_inc(s[f"x_loaded{q}"], 16)

        @block.tensor
        def _(pe):
            def tokens(n):
                return [res["tokT"][:, bass.ds(n, 1), k, :].rearrange("p a b -> p (a b)") for k in range(KH)]

            def project_xbc(n):
                xt = tokens(n)
                pe.wait_ge(s["cb_masked"], done(n, 1))
                for b in range(NB):
                    out = pa[:, b * 128:(b + 1) * 128] if b < XB else pb[:, 0:128]
                    for k in range(KH):
                        last = nc.tensor.matmul(out, c["w_xbc"][:, k, b * 128:(b + 1) * 128], xt[k],
                                                start=(k == 0), stop=(k == KH - 1))
                last.then_inc(s["proj_xbc"], 1)

            def project_gate(n):
                xt = tokens(n)
                pe.wait_ge(s["tap_now"], done(n))
                for b in range(XB):
                    for k in range(KH):
                        last = nc.tensor.matmul(pa[:, b * 128:(b + 1) * 128], c["w_gate"][:, k, b * 128:(b + 1) * 128],
                                                xt[k], start=(k == 0), stop=(k == KH - 1))
                last.then_inc(s["proj_gate"], 1)

            def turn(n, q):
                xbc = cv[:, q].rearrange("p a b c -> p a (b c)")
                pe.wait_ge(s["xbc"], done(n))
                nc.tensor.transpose(pb[:, 0:128], xbc[:, XB, :], c["ident"][:]).then_inc(s["turned_bc"], 1)
                pe.wait_ge(s["e_exp"], done(n, 1))
                for b in range(XB):
                    last = nc.tensor.transpose(pd[:, b * 128:(b + 1) * 128], xbc[:, b, :], c["ident"][:])
                last.then_inc(s["turned_x"], 1)

            def c_times_b(n, q):
                xbc = cv[:, q].rearrange("p a b c -> p a (b c)")
                pe.wait_ge(s["moved_bc"], done(n))
                pe.wait_ge(s["b_kept"], done(n))
                for ch in range(CT):
                    if ch == 2:
                        pe.wait_ge(s["gate"], done(n))
                    b, half = ch // 2, slice(NS * (ch // 2), NS * (ch // 2) + NS)
                    cc = cx[:, q, CH * ch:CH * ch + CH] if b == 0 else xbc[half, XB, CH * ch:CH * ch + CH]
                    last = nc.tensor.matmul(cb[b][:, CH * (ch % 2):CH * (ch % 2) + CH],
                                            brep[half, q, ch % 2].rearrange("p a b -> p (a b)"), cc,
                                            start=True, stop=True)
                last.then_inc(s["cb_done"], 1)

            def decay_sums(n, q, chunks):
                pe.wait_ge(s["masked_dA"], done(n))
                for ch in chunks:
                    if ch >= 2:
                        pe.wait_ge(s[f"m{ch - 2}"], done(n))
                    else:
                        pe.wait_ge(s[f"state{ch}"], done(n, 1))
                    nc.tensor.matmul(ring[ch % 2][:], c["later"][:], v[:, q, ch].rearrange("p a b -> p (a b)"),
                                     start=True, stop=True).then_inc(s[f"d{ch}"], 1)

            def token_sums(n, q):
                pe.wait_ge(s["stage_dA"], done(n))
                pe.wait_ge(s["x_dec"], done(n))
                for b in range(XB):
                    last = nc.tensor.matmul(pd[:, b * 128:(b + 1) * 128], dst[:, q, b * 128:(b + 1) * 128],
                                            c["until"][:], start=True, stop=True)
                last.then_inc(s["e_sum"], 1)

            def within_chunks(n, q, chunks):
                pe.wait_ge(s["spread"], done(n))
                pe.wait_ge(s["y_both"], done(n, 1))
                for ch in chunks:
                    pe.wait_ge(s[f"m{ch}"], done(n))
                    for g in range(HG):
                        last = nc.tensor.matmul(pg[32 * (g % 4):32 * (g % 4) + 32,
                                                   128 * (g // 4) + CH * ch:128 * (g // 4) + CH * ch + CH],
                                                xbd[:, q, ch, g, :], m[:, q, ch, g, :], start=True, stop=True)
                if CT - 1 in chunks:
                    last.then_inc(s["y_diag"], 1)

            def states(n, q, j):
                xbc = cv[:, q].rearrange("p a b c -> p a (b c)")
                if j == 0:
                    pe.wait_ge(s["y_scaled"], done(n, 1))
                    pe.wait_ge(s["attn"], done(n, 1))
                    pe.wait_ge(s["state1"], done(n, 2))
                else:
                    pe.wait_ge(s["state0"], done(n))
                for b in range(2):
                    ch, half = 2 * b + j, slice(NS * b, NS * b + NS)
                    cc = cx[:, q, CH * j:CH * j + CH] if b == 0 else xbc[half, XB, CH * ch:CH * ch + CH]
                    for k in range(XB):
                        last = nc.tensor.matmul(off[b][:, k, CH * j:CH * j + CH],
                                                state[half, q, 128 * k:128 * k + 128], cc, start=True, stop=True)
                last.then_inc(s[f"y_off{j}"], 1)
                for b in range(2):
                    ch, rows = 2 * b + j, slice(CH * (2 * b + j), CH * (2 * b + j) + CH)
                    last = nc.tensor.matmul(ring[j][NS * b:NS * b + NS, :], bn[rows, q, :], xdec[rows, q, :],
                                            start=True, stop=True)
                last.then_inc(s[f"s{j}"], 1)

            def project_out(n, q):
                pe.wait_ge(s["y_gated"], done(n))
                for b in range(XB):
                    last = nc.tensor.matmul(pc[:, 0:H], y[:, q, b * 128:(b + 1) * 128], c["w_out"][:, b, :],
                                            start=(b == 0), stop=(b == XB - 1))
                pe.wait_ge(s["y_sq"], done(n))
                for b in range(XB):
                    last = nc.tensor.matmul(pc[:, H:H + 1], ysq[:, q, b * 128:(b + 1) * 128], c["ones"][:, 0:1],
                                            start=(b == 0), stop=(b == XB - 1))
                last.then_inc(s["out_done"], 1)

            def tile_round(n, q, ahead=True, behind=True):
                if ahead:
                    project_xbc(n + 1)
                decay_sums(n, q, (0, 1))
                if behind:
                    project_out(n - 1, 1 - q)
                token_sums(n, q)
                if ahead:
                    project_gate(n + 1)
                decay_sums(n, q, (2, 3))
                within_chunks(n, q, (0, 1))
                if ahead:
                    turn(n + 1, 1 - q)
                within_chunks(n, q, (2, 3))
                states(n, q, 0)
                if ahead:
                    c_times_b(n + 1, 1 - q)
                states(n, q, 1)

            project_xbc(0)
            project_gate(0)
            turn(0, 0)
            c_times_b(0, 0)
            tile_round(0, 0, behind=False)
            with pe.Fori(0, NT // 2 - 1) as it:
                tile_round(2 * it + 1, 1)
                tile_round(2 * it + 2, 0)
            tile_round(NT - 1, 1, ahead=False)
            project_out(NT - 1, 1)

        @block.scalar
        def _(act):
            def newest_tap(n, q):
                act.wait_ge(s["proj_xbc"], done(n))
                act.wait_ge(s["taps_halo"], done(n, 2))
                act.wait_ge(s["y_skipped"], done(n, 2))
                act.wait_ge(s["y_off1"], done(n, 2))
                for b in range(NB):
                    src = pa[:, b * 128:(b + 1) * 128] if b < XB else pb[:, 0:128]
                    src = src.rearrange("p (a t) -> p a t", a=2)
                    nc.scalar.activation(xw[:, q, b, :, TAPS - 1:], src, ACT.Copy)
                    last = nc.scalar.activation(cv[:, q, b], src, ACT.Identity,
                                                bias=c["conv_b"][:, b:b + 1], scale=c["conv_w"][:, b, TAPS - 1:TAPS])
                last.then_inc(s["tap_now"], 1)

            def tanhs(n, q):
                act.wait_ge(s["proj_gate"], done(n))
                act.wait_ge(s["y_gated"], done(n, 2))
                nc.scalar.activation(gth[:, q], pa[:], ACT.Tanh, scale=0.5).then_inc(s["gate_tanh"], 1)
                act.wait_ge(s["conv"], done(n))
                nc.scalar.activation(th[:, q].rearrange("p a b -> p (a b)"), cv[:, q].rearrange("p a b c -> p (a b c)"),
                                     ACT.Tanh, scale=0.5).then_inc(s["conv_tanh"], 1)

            def keep_b(n, q):
                act.wait_ge(s["turned_bc"], done(n))
                act.wait_ge(s["s1"], done(n, 2))
                nc.scalar.activation(bn[:, q], pb[:, 0:NS], ACT.Copy).then_inc(s["b_kept"], 1)

            def chunk_exps(n, chunks):
                for ch in chunks:
                    act.wait_ge(s[f"d{ch}"], done(n))
                    nc.scalar.activation(ring[ch % 2][:], ring[ch % 2][:], ACT.Exp).then_inc(s[f"e{ch}"], 1)

            def spread(n, q):
                act.wait_ge(s["x_dt"], done(n))
                act.wait_ge(s["y_diag"], done(n, 2))
                for ch in range(CT):
                    for h in range(HQ):
                        src = xdt[CH * ch:CH * ch + CH, q, :].rearrange("p (g h c) -> p g h c", h=HQ, c=P)[:, :, h, :]
                        last = nc.scalar.activation(xbd[CH * h:CH * h + CH, q, ch, :, P * h:P * h + P], src, ACT.Copy)
                last.then_inc(s["spread"], 1)

            def token_exps(n, q):
                act.wait_ge(s["e_sum"], done(n))
                act.wait_ge(s["out_done"], done(n, 2))
                nc.scalar.activation(et[:, q], pd[:], ACT.Exp).then_inc(s["e_exp"], 1)

            def layer_input(n, q, it):
                act.wait_ge(s[f"x_loaded{q}"], 16 * it + 16 + LEAD)
                act.wait_ge(s["attn"], done(n, 2))
                nc.scalar.activation(xl[:, q], xin[:, q], ACT.Identity, bias=res["nbias"][:, bass.ds(n, 1)],
                                     scale=res["rstd"][:, bass.ds(n, 1)]).then_inc(s["xl"], 1)

            def squares(n, q):
                act.wait_ge(s["y_gated"], done(n))
                nc.scalar.activation(ysq[:, q], y[:, q], ACT.Square).then_inc(s["y_sq"], 1)

            def tile_round(n, q, it, ahead=True):
                if ahead:
                    newest_tap(n + 1, 1 - q)
                chunk_exps(n, (0, 1))
                token_exps(n, q)
                if ahead:
                    tanhs(n + 1, 1 - q)
                chunk_exps(n, (2, 3))
                if ahead:
                    keep_b(n + 1, 1 - q)
                    spread(n + 1, 1 - q)
                layer_input(n, q, it)
                squares(n, q)

            newest_tap(0, 0)
            tanhs(0, 0)
            keep_b(0, 0)
            spread(0, 0)
            tile_round(0, 0, 0)
            with act.Fori(0, NT // 2 - 1) as it:
                tile_round(2 * it + 1, 1, it)
                tile_round(2 * it + 2, 0, it + 1)
            tile_round(NT - 1, 1, NT // 2 - 1, ahead=False)

        @block.gpsimd
        def _(pool):
            def stage(n, q):
                wait_alone(pool, s["e_sum"], done(n, 2), s["pool_passed"])
                dA = res["dA"][:, bass.ds(n, 1), :].rearrange("p a b -> p (a b)")
                nc.gpsimd.tensor_copy(dst[:, q].rearrange("p (a b) -> p a b", b=P),
                                      dA[:, :, None].to_broadcast([128, NH, P])).then_inc(s["stage_dA"], 1)
                pool.wait_ge(s["y_diag"], done(n, 2))
                for ch in range(CT):
                    dA = res["dAp"][:, ch, bass.ds(n, 1), :].rearrange("p a b -> p (a b)")
                    last = nc.gpsimd.tensor_tensor(v[:, q, ch], dA[:, :, None].to_broadcast([128, HG, CH]),
                                                   c["until32"][:, None, :].to_broadcast([128, HG, CH]), ALU.mult)
                last.then_inc(s["masked_dA"], 1)

            def rms(n, q):
                pool.wait_ge(s["ms_eps"], done(n))
                nc.gpsimd.tensor_tensor(small[:, q, 1:2], small[:, q, 0:1], c["minus_half"][:, 0:1], ALU.pow)\
                    .then_inc(s["rms"], 1)

            stage(0, 0)
            stage(1, 1)
            with pool.Fori(0, NT // 2 - 1) as it:
                for q in range(2):
                    n = 2 * it + q
                    rms(n, q)
                    stage(n + 2, q)
            rms(NT - 2, 0)
            rms(NT - 1, 1)

        @block.vector
        def _(dve):
            def older_taps(n, q):
                dve.wait_ge(s["tap_now"], done(n))
                for k in range(TAPS - 1):
                    if k:
                        dve.wait_ge(s[("taps_a", "taps_b")[k - 1]], done(n))
                    for b in range(NB):
                        last = nc.vector.scalar_tensor_tensor(cv[:, q, b], xw[:, q, b, :, k:k + HALF],
                                                              c["conv_w"][:, b, k:k + 1], cv[:, q, b],
                                                              ALU.mult, ALU.add)
                    last.then_inc(s[("taps_a", "taps_b", "conv")[k]], 1)
                dve.wait_ge(s["conv"], done(n))
                nc.vector.tensor_copy(xw[:, q, :, :, 0:TAPS - 1], xw[:, q, :, :, HALF:HALF + TAPS - 1])\
                    .then_inc(s["taps_halo"], 1)

            def silus(n, q):
                dve.wait_ge(s["gate_tanh"], done(n))
                nc.vector.scalar_tensor_tensor(gate[:, q], gth[:, q], 1.0, pa[:], ALU.add, ALU.mult)\
                    .then_inc(s["gate"], 1)
                dve.wait_ge(s["conv_tanh"], done(n))
                nc.vector.scalar_tensor_tensor(cv[:, q].rearrange("p a b c -> p (a b c)"),
                                               th[:, q].rearrange("p a b -> p (a b)"), 1.0,
                                               cv[:, q].rearrange("p a b c -> p (a b c)"), ALU.add, ALU.mult)\
                    .then_inc(s["xbc"], 1)

            def move_bc(n, q):
                xbc = cv[:, q].rearrange("p a b c -> p a (b c)")
                dve.wait_ge(s["xbc"], done(n))
                dve.wait_ge(s["y_off1"], done(n, 2))
                nc.vector.tensor_copy(cx[:, q], xbc[NS:2 * NS, XB, 0:HALF])
                for b in range(2):
                    bt = xbc[0:NS, XB, HALF * b:HALF * b + HALF].rearrange("p (a b) -> p a b", a=2)
                    last = nc.vector.tensor_copy(brep[NS * b:NS * b + NS, q],
                                                 bt[:, :, None, :].to_broadcast([NS, 2, HQ, CH]))
                last.then_inc(s["moved_bc"], 1)

            def scale_x(n, q):
                dve.wait_ge(s["turned_x"], done(n))
                dve.wait_ge(s["spread"], done(n, 2))
                px = pd[:].rearrange("p (h c) -> p h c", c=P)
                for out, by, sem in ((xdt, "dt", "x_dt"), (xdec, "to_end", "x_dec")):
                    if sem == "x_dec":
                        dve.wait_ge(s["s1"], done(n, 2))
                    f = res[by][:, bass.ds(n, 1), :].rearrange("p a b -> p (a b)")
                    nc.vector.tensor_tensor(out[:, q].rearrange("p (h c) -> p h c", c=P), px,
                                            f[:, :, None].to_broadcast([128, NH, P]), ALU.mult).then_inc(s[sem], 1)

            def mask_cb(n, q):
                dve.wait_ge(s["cb_done"], done(n))
                for b in range(2):
                    last = nc.vector.tensor_tensor(cbm[:, q, 2 * b:2 * b + 2], cb[b].rearrange("p (a b) -> p a b", a=2),
                                                   c["until32q"][:, None, :].to_broadcast([128, 2, CH]), ALU.mult)
                last.then_inc(s["cb_masked"], 1)

            def weigh(n, q, chunks):
                dve.wait_ge(s["cb_masked"], done(n))
                dve.wait_ge(s["y_diag"], done(n, 2))
                for ch in chunks:
                    dve.wait_ge(s[f"e{ch}"], done(n))
                    nc.vector.tensor_tensor(m[:, q, ch], ring[ch % 2][:].rearrange("p (a b) -> p a b", a=HG),
                                            cbm[:, q, ch][:, None, :].to_broadcast([128, HG, CH]), ALU.mult)\
                        .then_inc(s[f"m{ch}"], 1)

            def decay_state(n, q, j):
                st = state[:, q].rearrange("p (h c) -> p h c", c=P)
                f = res[f"decay{j}"][:, bass.ds(n, 1), :].rearrange("p a b -> p (a b)")
                dve.wait_ge(s[f"y_off{j}"], done(n))
                dve.wait_ge(s["state0" if j else "state1"], done(n) if j else done(n, 2))
                nc.vector.tensor_tensor(st, st, f[:, :, None].to_broadcast([128, NH, P]), ALU.mult)\
                    .then_inc(s[f"decayed{j}"], 1)

            def add_state(n, q, j):
                dve.wait_ge(s[f"decayed{j}"], done(n))
                dve.wait_ge(s[f"s{j}"], done(n))
                nc.vector.tensor_tensor(state[:, q], state[:, q], ring[j][:], ALU.add).then_inc(s[f"state{j}"], 1)

            def scale_off(n, q):
                dve.wait_ge(s["e_exp"], done(n))
                dve.wait_ge(s["y_sq"], done(n, 2))
                dve.wait_ge(s["out_done"], done(n, 2))
                for b in range(2):
                    yb, eb = (a[:, q].rearrange("p (k b t) -> p k b t", k=XB, b=2)[:, :, b] for a in (y, et))
                    last = nc.vector.scalar_tensor_tensor(yb, off[b], 0.5, eb, ALU.mult, ALU.mult)
                last.then_inc(s["y_scaled"], 1)

            def gated_y(n, q):
                xbc = cv[:, q].rearrange("p a b c -> p a (b c)")
                dve.wait_ge(s["y_scaled"], done(n))
                dve.wait_ge(s["y_diag"], done(n))
                nc.vector.tensor_tensor(y[:, q], y[:, q], pg[:], ALU.add).then_inc(s["y_both"], 1)
                dve.wait_ge(s["y_both"], done(n))
                for b in range(XB):
                    last = nc.vector.scalar_tensor_tensor(y[:, q, b * 128:(b + 1) * 128], xbc[:, b, :], c["skip"][:, b:b + 1],
                                                          y[:, q, b * 128:(b + 1) * 128], ALU.mult, ALU.add)
                last.then_inc(s["y_skipped"], 1)
                dve.wait_ge(s["y_skipped"], done(n))
                dve.wait_ge(s["gate"], done(n))
                nc.vector.scalar_tensor_tensor(y[:, q], y[:, q], 0.5, gate[:, q], ALU.mult, ALU.mult)\
                    .then_inc(s["y_gated"], 1)

            def mean_square(n, q):
                dve.wait_ge(s["out_done"], done(n))
                nc.vector.tensor_scalar(small[:, q, 0:1], pc[:, H:H + 1], 1.0 / CI, EPS, ALU.mult, ALU.add)\
                    .then_inc(s["ms_eps"], 1)

            def add_input(n, q):
                dve.wait_ge(s["rms"], done(n))
                dve.wait_ge(s["xl"], done(n))
                nc.vector.scalar_tensor_tensor(res["attn"][:, bass.ds(n, 1), :].rearrange("p a b -> p (a b)"),
                                               pc[:, 0:H], small[:, q, 1:2], xl[:, q], ALU.mult, ALU.add)\
                    .then_inc(s["attn"], 1)

            def tile_round(n, q, ahead=True, behind=True):
                if ahead:
                    older_taps(n + 1, 1 - q)
                weigh(n, q, (0, 1))
                if behind:
                    mean_square(n - 1, 1 - q)
                if ahead:
                    silus(n + 1, 1 - q)
                    move_bc(n + 1, 1 - q)
                if behind:
                    add_input(n - 1, 1 - q)
                weigh(n, q, (2, 3))
                if ahead:
                    scale_x(n + 1, 1 - q)
                decay_state(n, q, 0)
                add_state(n, q, 0)
                if ahead:
                    mask_cb(n + 1, 1 - q)
                decay_state(n, q, 1)
                scale_off(n, q)
                add_state(n, q, 1)
                gated_y(n, q)

            older_taps(0, 0)
            silus(0, 0)
            move_bc(0, 0)
            scale_x(0, 0)
            mask_cb(0, 0)
            tile_round(0, 0, behind=False)
            with dve.Fori(0, NT // 2 - 1) as it:
                tile_round(2 * it + 1, 1)
                tile_round(2 * it + 2, 0)
            tile_round(NT - 1, 1, ahead=False)
            mean_square(NT - 1, 1)
            add_input(NT - 1, 1)


def route(nc, once, c, tok, x_tiles, xm_rows, places):
    names = ("x_loaded0 x_loaded1 a_stats a_mean_var a_var a_rstd a_nbias a_norm x2 x2_kept b_stats b_mean_var b_var b_rstd "
             "b_nbias xm turned xm_turned logits top_max exps inv_sum probs top8 top_idx top_f top_sum top_inv "
             "weights scatters_done idx0 sel0 sel1 sel2 sel3 sel4 sel5 pos_done pos_kept slots_f slots own_rows xm_stored0 xm_stored1 dve_passed pool_passed "
             "gu0 gu1 gu2 gate_tanh0 gate_tanh1 gate_tanh2 silu0 silu1 silu2 h0 h1 h2 down down_kept run0 run1 run2 run3")
    with loop_semaphores(nc, names) as s, ExitStack() as ctx:
        def sb(name, shape, dt=F32):
            return ctx.enter_context(nc.sbuf_tensor(name, shape, dt))
        xin = sb("p3_x", [128, 2, GT, H])
        an = sb("p3_an", [128, 2, GT, H])
        x2 = sb("p3_x2", [128, 2, GT, H])
        xm = sb("p3_xm", [128, 2, GT, H])
        xmT = sb("p3_xmT", [128, 2, KH, GT * TILE])
        st = sb("p3_st", [128, 2, 2, GT, 6])
        mv = sb("p3_mv", [128, 2, 2, GT, 2])
        small = sb("p3_small", [128, 2, 12, GT])
        ex = sb("p3_ex", [128, 2, GT, NE])
        top = sb("p3_top", [128, 2, GT, 8])
        idx = sb("p3_idx", [128, 2, GT, 8], mybir.dt.uint32)
        idf = sb("p3_idf", [128, 2, GT, 8])
        sel = sb("p3_sel", [128, 2, GT, NE])
        run = sb("p3_run", [128, 2, GT, NE])
        runs = tok["run"]
        pos = sb("p3_pos", [128, 2, GT, NE])
        junk = sb("p3_junk", [128, 2, GT * TOPK, NE], mybir.dt.bfloat16)
        slot_f = sb("p3_slotf", [128, 2, GT, TOPK])
        slot = sb("p3_slot", [128, 2, GT, TOPK], mybir.dt.uint32)
        own = sb("p3_own", [128, 2, GT])
        blank = an[:].rearrange("p a b c -> p (a b c)")[:, 0:NE * REGION // 256]
        gt = sb("p3_gt", [128, 2, SB, GT * TILE])
        hT = gt
        banks = [ctx.enter_context(nc.psum_tensor(f"p3_bank{k}", [128, 512], F32)) for k in range(8)]
        turn, rt, gbank, ubank, cnt = banks[0:2], banks[2], banks[3:5], banks[5:7], banks[7]
        scattered = [once(f"scattered{q}") for q in range(2)]
        blocks = [(b, min(128, SI - 128 * b)) for b in range(SB)]

        cleared, blanked = once("route_cleared"), once("blanked")
        with nc.Block() as block:
            @block.vector
            def _(dve):
                nc.vector.memset(blank, float(B * T))
                nc.vector.memset(x2[:], 0.0)
                nc.vector.memset(runs[:], 0.0).then_inc(cleared, 1)
                dve.wait_ge(cleared, 1)

            @block.sync
            def _(sp):
                sp.wait_ge(cleared, 1)
                for half in places.rearrange("(a p r) o -> a p (r o)", a=2, p=128):
                    sp.dma_start(half, blank).then_inc(blanked, 16)
                sp.dma_start(xm_rows[B * T:B * T + 128, :], x2[:, 0, 0, :]).then_inc(blanked, 16)
                sp.wait_ge(blanked, 48)

        block = ctx.enter_context(nc.Block())

        @block.sync
        def _(sp):
            with sp.Fori(0, NG // 2) as it:
                for q in range(2):
                    n = 2 * it + q
                    sp.wait_ge(s["x2"], done(n, 2))
                    sp.dma_start(xin[:, q], x_tiles[:, bass.ds(n * GT, GT), :]).then_inc(s[f"x_loaded{q}"], 16)
                for q in range(2):
                    n = 2 * it + q
                    sp.wait_ge(s["xm"], done(n))
                    sp.dma_start(xm_rows[bass.ds(n * GT * TILE, GT * TILE), :].rearrange("(t p) h -> p t h", p=128), xm[:, q])\
                        .then_inc(s[f"xm_stored{q}"], 16)
            for q in range(2):
                sp.wait_ge(s[f"xm_stored{q}"], 16 * (NG // 2) + LEAD)

        @block.vector
        def _(dve):
            def stats(n, q, w, src, names):
                a_stats, a_mean_var, a_var, a_rstd, a_nbias = names
                for t in range(GT):
                    last = nc.vector.bn_stats(st[:, q, w, t, :], src(t))
                last.then_inc(s[a_stats], 1)
                wait_alone(dve, s[a_stats], done(n), s["dve_passed"])
                for t in range(GT):
                    last = nc.vector.bn_aggr(mv[:, q, w, t, :], st[:, q, w, t, :])
                last.then_inc(s[a_mean_var], 1)
                dve.wait_ge(s[a_mean_var], done(n))
                nc.vector.tensor_scalar(small[:, q, 3 * w], mv[:, q, w, :, 1], EPS, None, ALU.add).then_inc(s[a_var], 1)
                dve.wait_ge(s[a_rstd], done(n))
                nc.vector.scalar_tensor_tensor(small[:, q, 3 * w + 2], mv[:, q, w, :, 0], -1.0, small[:, q, 3 * w + 1],
                                               ALU.mult, ALU.mult).then_inc(s[a_nbias], 1)

            with dve.Fori(0, NG // 2) as it:
                for q in range(2):
                    n = 2 * it + q
                    stats(n, q, 0, lambda t: tok["xm"][:, bass.ds(n * GT + t, 1), :].rearrange("p a b -> p (a b)"),
                          ("a_stats", "a_mean_var", "a_var", "a_rstd", "a_nbias"))
                    dve.wait_ge(s["a_norm"], done(n))
                    dve.wait_ge(s[f"x_loaded{q}"], 16 * it + 16 + LEAD)
                    dve.wait_ge(s["x2_kept"], done(n, 2))
                    nc.vector.tensor_tensor(x2[:, q], an[:, q], xin[:, q], ALU.add).then_inc(s["x2"], 1)
                    dve.wait_ge(s["x2"], done(n))
                    stats(n, q, 1, lambda t: x2[:, q, t, :], ("b_stats", "b_mean_var", "b_var", "b_rstd", "b_nbias"))
                    dve.wait_ge(s["logits"], done(n))
                    nc.vector.tensor_reduce(small[:, q, 6], rt[:, 0:GT * NE].rearrange("p (a b) -> p a b", a=GT),
                                            mybir.AxisListType.X, ALU.max, negate=True).then_inc(s["top_max"], 1)
                    for b, rows in blocks:
                        r = (q * SB + b) % 2
                        dve.wait_ge(s[f"gate_tanh{b}"], done(n))
                        nc.vector.scalar_tensor_tensor(gt[0:rows, q, b, :], gt[0:rows, q, b, :], 1.0, gbank[r][0:rows, :],
                                                       ALU.add, ALU.mult).then_inc(s[f"silu{b}"], 1)
                        dve.wait_ge(s[f"silu{b}"], done(n))
                        nc.vector.tensor_tensor(hT[0:rows, q, b, :], gt[0:rows, q, b, :], ubank[r][0:rows, :], ALU.mult)\
                            .then_inc(s[f"h{b}"], 1)
                    dve.wait_ge(s["exps"], done(n))
                    nc.vector.reciprocal(small[:, q, 8], small[:, q, 7]).then_inc(s["inv_sum"], 1)
                    dve.wait_ge(s["inv_sum"], done(n))
                    nc.vector.tensor_tensor(ex[:, q], ex[:, q], small[:, q, 8][:, :, None].to_broadcast([128, GT, NE]),
                                            ALU.mult).then_inc(s["probs"], 1)
                    wait_alone(dve, s["probs"], done(n), s["dve_passed"])
                    for t in range(GT):
                        last = nc.vector.max(top[:, q, t, :], ex[:, q, t, :])
                    last.then_inc(s["top8"], 1)
                    wait_alone(dve, s["top8"], done(n), s["dve_passed"])
                    for t in range(GT):
                        last = nc.vector.max_index(idx[:, q, t, :], top[:, q, t, :], ex[:, q, t, :])
                    last.then_inc(s["top_idx"], 1)
                    dve.wait_ge(s["top_idx"], done(n))
                    nc.vector.tensor_copy(idf[:, q], idx[:, q]).then_inc(s["top_f"], 1)
                    nc.vector.tensor_reduce(small[:, q, 9], top[:, q, :, 0:TOPK], mybir.AxisListType.X, ALU.add)\
                        .then_inc(s["top_sum"], 1)
                    dve.wait_ge(s["top_sum"], done(n))
                    nc.vector.reciprocal(small[:, q, 10], small[:, q, 9]).then_inc(s["top_inv"], 1)
                    dve.wait_ge(s["top_inv"], done(n))
                    nc.vector.tensor_tensor(tok["weight"][:, bass.ds(n * GT, GT), :], top[:, q, :, 0:TOPK],
                                            small[:, q, 10][:, :, None].to_broadcast([128, GT, TOPK]), ALU.mult)\
                        .then_inc(s["weights"], 1)
                    dve.wait_ge(s["top_f"], done(n))
                    dve.wait_ge(s["pos_done"], done(n, 2))
                    for k in range(TOPK):
                        if k:
                            dve.wait_ge(s[f"sel{k - 1}"], done(n))
                        for t in range(GT):
                            if k == 0:
                                last = nc.vector.tensor_scalar(sel[:, q, t, :], c["expert"][:], idf[:, q, t, 0:1], None,
                                                               ALU.is_equal)
                            else:
                                last = nc.vector.scalar_tensor_tensor(sel[:, q, t, :], c["expert"][:], idf[:, q, t, k:k + 1],
                                                                      sel[:, q, t, :], ALU.is_equal, ALU.add)
                        last.then_inc(s[f"sel{k}"], 1)
                    dve.wait_ge(s[f"sel{TOPK - 1}"], done(n))
                    for t in range(GT):
                        before = runs[:] if t == 0 else run[:, q, t, :]
                        after = run[:, q, t + 1, :] if t < GT - 1 else runs[:]
                        if t == 0:
                            dve.wait_ge(s["run3"], done(n, 1))
                            nc.vector.tensor_copy(run[:, q, 0, :], runs[:]).then_inc(s["idx0"], 1)
                            dve.wait_ge(s["idx0"], done(n))
                        else:
                            dve.wait_ge(s[f"run{t - 1}"], done(n))
                        nc.vector.tensor_tensor(after, run[:, q, t, :], sel[:, q, t, :], ALU.add).then_inc(s[f"run{t}"], 1)
                    dve.wait_ge(s["pos_done"], done(n))
                    nc.vector.tensor_tensor(pos[:, q], cnt[:, 0:GT * NE].rearrange("p (a b) -> p a b", a=GT),
                                            c["region"][:, None, :].to_broadcast([128, GT, NE]), ALU.add)\
                        .then_inc(s["pos_kept"], 1)
                    dve.wait_ge(s["pos_kept"], done(n))
                    for t in range(GT):
                        for k in range(TOPK):
                            last = nc.vector.scalar_tensor_tensor(junk[:, q, t * TOPK + k, :], c["expert"][:],
                                                                  idf[:, q, t, k:k + 1], pos[:, q, t, :],
                                                                  ALU.is_equal, ALU.mult,
                                                                  accum_out=slot_f[:, q, t, k:k + 1])
                    last.then_inc(s["slots_f"], 1)
                    dve.wait_ge(s["slots_f"], done(n))
                    dve.wait_ge(s["scatters_done"], done(n, 2))
                    nc.vector.tensor_copy(slot[:, q], slot_f[:, q])
                    nc.vector.tensor_copy(own[:, q], c["token"][:, bass.ds(n * GT, GT)])
                    nc.vector.tensor_copy(tok["choice"][:, bass.ds(n * GT, GT), :], idf[:, q, :, 0:TOPK])
                    nc.vector.tensor_copy(tok["slot"][:, bass.ds(n * GT, GT), :], slot_f[:, q]).then_inc(s["slots"], 1)
        @block.gpsimd
        def _(pool):
            with pool.Fori(0, NG // 2) as it:
                for q in range(2):
                    n = 2 * it + q
                    for w, v, r in ((0, "a_var", "a_rstd"), (1, "b_var", "b_rstd")):
                        pool.wait_ge(s[v], done(n))
                        nc.gpsimd.tensor_tensor(small[:, q, 3 * w + 1], small[:, q, 3 * w], c["minus_half"][:, 0:GT], ALU.pow)\
                            .then_inc(s[r], 1)
                    wait_alone(pool, s["x2"], done(n), s["pool_passed"])
                    nc.gpsimd.tensor_copy(tok["x2"][:, bass.ds(n * GT, GT), :], x2[:, q]).then_inc(s["x2_kept"], 1)
                    wait_alone(pool, s["slots"], done(n), s["pool_passed"])
                    for t in range(GT):
                        for k in range(TOPK):
                            pool.indirect_dma_start(places, bass.IndirectOffsetOnAxis(ap=slot[:, q, t, k:k + 1], axis=0),
                                                    own[:, q, t:t + 1], None).then_inc(scattered[q], 16)
                    wait_alone(pool, scattered[q], 16 * GT * TOPK * it + 16 * GT * TOPK, s["scatters_done"])

        @block.scalar
        def _(act):
            with act.Fori(0, NG // 2) as it:
                for q in range(2):
                    n = 2 * it + q
                    act.wait_ge(s["a_nbias"], done(n))
                    act.wait_ge(s["x2"], done(n, 2))
                    for t in range(GT):
                        last = nc.scalar.activation(an[:, q, t, :],
                                                    tok["xm"][:, bass.ds(n * GT + t, 1), :].rearrange("p a b -> p (a b)"),
                                                    ACT.Identity, bias=small[:, q, 2, t:t + 1], scale=small[:, q, 1, t:t + 1])
                    last.then_inc(s["a_norm"], 1)
                    act.wait_ge(s["b_nbias"], done(n))
                    act.wait_ge(s["turned"], done(n, 2))
                    act.wait_ge(s[f"xm_stored{q}"], 16 * it + LEAD)
                    for t in range(GT):
                        last = nc.scalar.activation(xm[:, q, t, :], x2[:, q, t, :], ACT.Identity,
                                                    bias=small[:, q, 5, t:t + 1], scale=small[:, q, 4, t:t + 1])
                    last.then_inc(s["xm"], 1)
                    act.wait_ge(s["turned"], done(n))
                    act.wait_ge(s["down"], done(n, 2))
                    for k in range(KH):
                        last = nc.scalar.activation(xmT[:, q, k, :], turn[k][:], ACT.Copy)
                    last.then_inc(s["xm_turned"], 1)
                    act.wait_ge(s["top_max"], done(n))
                    act.wait_ge(s["slots_f"], done(n, 2))
                    for t in range(GT):
                        last = nc.scalar.activation(ex[:, q, t, :], rt[:, t * NE:(t + 1) * NE], ACT.Exp,
                                                    bias=small[:, q, 6, t:t + 1], accum_out=small[:, q, 7, t:t + 1])
                    last.then_inc(s["exps"], 1)
                    for b, rows in blocks:
                        act.wait_ge(s[f"gu{b}"], done(n))
                        nc.scalar.activation(gt[0:rows, q, b, :], gbank[(q * SB + b) % 2][0:rows, :], ACT.Tanh, scale=0.5)\
                            .then_inc(s[f"gate_tanh{b}"], 1)
                    act.wait_ge(s["down"], done(n))
                    for t in range(GT):
                        last = nc.scalar.activation(tok["shared"][:, bass.ds(n * GT + t, 1), :].rearrange("p a b -> p (a b)"),
                                                    turn[t // 2][:, H * (t % 2):H * (t % 2) + H], ACT.Copy, scale=0.5)
                    last.then_inc(s["down_kept"], 1)

        @block.tensor
        def _(pe):
            with pe.Fori(0, NG // 2) as it:
                for q in range(2):
                    n = 2 * it + q
                    pe.wait_ge(s["xm"], done(n))
                    pe.wait_ge(s["down_kept"], done(n, 1))
                    for k in range(KH):
                        for t in range(GT):
                            last = nc.tensor.transpose(turn[k][:, t * TILE:(t + 1) * TILE],
                                                       xm[:, q, t, k * 128:(k + 1) * 128], c["ident"][:])
                    last.then_inc(s["turned"], 1)
                    pe.wait_ge(s["xm_turned"], done(n))
                    pe.wait_ge(s["exps"], done(n, 1))
                    for t in range(GT):
                        for k in range(KH):
                            last = nc.tensor.matmul(rt[:, t * NE:(t + 1) * NE], xmT[:, q, k, t * TILE:(t + 1) * TILE],
                                                    c["router_w"][:, k, :], start=(k == 0), stop=(k == KH - 1))
                    last.then_inc(s["logits"], 1)
                    for b, rows in blocks:
                        i = q * SB + b
                        prev = (f"h{b - 2}", 0) if b >= 2 else (f"h{b + 1}", 1)
                        pe.wait_ge(s[prev[0]], done(n, prev[1]))
                        for bank, w in ((gbank, "sg_w"), (ubank, "su_w")):
                            for k in range(KH):
                                last = nc.tensor.matmul(bank[i % 2][0:rows, :], c[w][:, k, 128 * b:128 * b + rows],
                                                        xmT[:, q, k, :], start=(k == 0), stop=(k == KH - 1))
                        last.then_inc(s[f"gu{b}"], 1)
                    pe.wait_ge(s[f"h{SB - 1}"], done(n))
                    for t in range(GT):
                        for b, rows in blocks:
                            last = nc.tensor.matmul(turn[t // 2][:, H * (t % 2):H * (t % 2) + H],
                                                    hT[0:rows, q, b, t * TILE:(t + 1) * TILE], c["sd_w"][0:rows, b, :],
                                                    start=(b == 0), stop=(b == SB - 1))
                    last.then_inc(s["down"], 1)
                    pe.wait_ge(s["run3"], done(n))
                    pe.wait_ge(s["pos_kept"], done(n, 1))
                    nc.tensor.matmul(cnt[:, 0:GT * NE], c["before"][:], sel[:, q].rearrange("p a b -> p (a b)"),
                                     start=True, stop=False)
                    nc.tensor.matmul(cnt[:, 0:GT * NE], c["all"][:], run[:, q].rearrange("p a b -> p (a b)"),
                                     start=False, stop=True).then_inc(s["pos_done"], 1)


def tables(nc, once, c, tok, places, tab_dram, y_rows):
    I32 = mybir.dt.int32
    J = MAXT // 128
    with ExitStack() as ctx:
        def sb(name, shape, dt=F32):
            return ctx.enter_context(nc.sbuf_tensor(name, shape, dt))
        cnt = sb("p4_cnt", [128, NE])
        cnt_i = sb("p4_cnti", [128, NE], I32)
        num = sb("p4_num", [128, NE])
        end = sb("p4_end", [128, NE])
        begin = sb("p4_begin", [128, NE])
        hit = sb("p4_hit", [128, NE])
        first = sb("p4_first", [128, NE])
        one = sb("p4_one", [128, NE])
        cell = sb("p4_cell", [128, J, 6])
        page = sb("p4_page", [128, J], mybir.dt.uint32)
        fields = sb("p4_fields", [128, J, FIELDS], I32)
        listed = sb("p4_listed", [128, J, 128])
        zero = sb("p4_zero", [128, H])
        left = sb("p4_left", [1, 1], I32)
        ps = ctx.enter_context(nc.psum_tensor("p4_ps", [128, NE], F32))
        ps_rows = ctx.enter_context(nc.psum_tensor("p4_rows", [128, MAXT], F32))
        rounds_ready, zeroed, sp_passed = once("rounds_ready"), once("y_rows_zeroed"), once("sp_passed")
        step, counted, fields_ready, pages_ready = once("tables_step"), once("experts_counted"), once("fields_ready"), once("pages_ready")
        fields_stored, fields_loaded, rows_turned = once("fields_stored"), once("fields_loaded"), once("rows_turned")
        listed_loaded = [once(f"listed_loaded{j}") for j in range(J)]
        block = ctx.enter_context(nc.Block())

        @block.tensor
        def _(pe):
            nc.tensor.matmul(ps[:], c["all"][:], tok["run"][:], start=True, stop=True).then_inc(counted, 1)
            for j in range(J):
                pe.wait_ge(listed_loaded[j], 16)
                nc.tensor.transpose(ps_rows[:, 128 * j:128 * j + 128], listed[:, j], c["ident"][:]).then_inc(rows_turned, 1)

        @block.vector
        def _(dve):
            steps = [0]

            def then(ins):
                steps[0] += 1
                ins.then_inc(step, 1)
                dve.wait_ge(step, steps[0])
            nc.vector.memset(one[:], 1.0)
            nc.vector.memset(zero[:], 0.0)
            dve.wait_ge(counted, 1)
            then(nc.vector.tensor_scalar(cnt[:], ps[:], 127.0, None, ALU.add))
            then(nc.vector.tensor_copy(cnt_i[:], cnt[:]))
            then(nc.vector.tensor_scalar(cnt_i[:], cnt_i[:], 7, None, ALU.logical_shift_right))
            then(nc.vector.tensor_copy(num[:], cnt_i[:]))
            then(nc.vector.tensor_scalar(num[:], num[:], 1.0, None, ALU.max))
            then(nc.vector.tensor_tensor_scan(end[:], one[:], num[:], 0.0, ALU.mult, ALU.add))
            then(nc.vector.tensor_tensor(begin[:], end[:], num[:], ALU.subtract))
            nc.vector.scalar_tensor_tensor(tok["shift"][:], begin[:], 128.0, c["region"][:], ALU.mult, ALU.subtract)
            then(nc.vector.memset(tok["freed"][:, 0:2], 0))
            then(nc.vector.tensor_copy(tok["freed"][:, 2:NE], end[0:1, 0:NE - 2]))
            then(nc.vector.tensor_scalar(hit[0:1, 0:1], end[0:1, NE - 1:NE], 3.0, None, ALU.add))
            then(nc.vector.tensor_copy(tok["rounds"][:], hit[0:1, 0:1]))
            then(nc.vector.tensor_scalar(tok["rounds"][:], tok["rounds"][:], 2, None, ALU.logical_shift_right))
            then(nc.vector.tensor_copy(hit[0:1, 1:2], tok["rounds"][:]))
            then(nc.vector.tensor_scalar(hit[0:1, 1:2], hit[0:1, 1:2], -64.0, 16.0 * (MAXT + 1), ALU.mult, ALU.add))
            then(nc.vector.tensor_copy(left[:], hit[0:1, 1:2]))
            dve.sem_inc(rounds_ready, 1)
            for j in range(J):
                t = c["tile"][:, j:j + 1]
                then(nc.vector.scalar_tensor_tensor(hit[:], begin[:], t, one[:], ALU.is_le, ALU.mult,
                                                    accum_out=cell[:, j, 0:1]))
                then(nc.vector.scalar_tensor_tensor(first[:], begin[:], t, begin[:], ALU.is_le, ALU.mult))
                then(nc.vector.tensor_reduce(cell[:, j, 1:2], first[:], mybir.AxisListType.X, ALU.max))
                then(nc.vector.tensor_scalar(cell[:, j, 0:1], cell[:, j, 0:1], -1.0, None, ALU.add))
                then(nc.vector.tensor_tensor(cell[:, j, 2:3], t, cell[:, j, 1:2], ALU.subtract))
                then(nc.vector.tensor_scalar(cell[:, j, 2:3], cell[:, j, 2:3], float(REGION // 128 - 1), None, ALU.min))
                then(nc.vector.tensor_scalar(cell[:, j, 3:4], cell[:, j, 0:1], float(REGION // 128), None, ALU.mult))
                then(nc.vector.tensor_tensor(cell[:, j, 2:3], cell[:, j, 2:3], cell[:, j, 3:4], ALU.add))
                nc.vector.tensor_copy(page[:, j:j + 1], cell[:, j, 2:3]).then_inc(pages_ready, 1)
                then(nc.vector.tensor_copy(fields[:, j, 0:1], cell[:, j, 0:1]))
                then(nc.vector.tensor_scalar(fields[:, j, 1:2], fields[:, j, 0:1], 1, None, ALU.bitwise_and))
            dve.sem_inc(fields_ready, 1)
            dve.wait_ge(rows_turned, J)
            nc.vector.memset(tok["rows"][:, MAXT:MAXT + 8], 0.0)
            nc.vector.memset(tok["tile"][:, MAXT * FIELDS:], 0)
            then(nc.vector.tensor_copy(tok["rows"][:, 0:MAXT], ps_rows[:]))

        @block.sync
        def _(sp):
            sp.wait_ge(rounds_ready, 1)
            n_rounds = sp.value_load(tok["rounds"][0:1, 0:1], min_val=1, max_val=MAXT // 4)
            with sp.Fori(4 * n_rounds, MAXT + 1) as t:
                sp.dma_start(y_rows[bass.ds(t * 128, 128), :], zero[:]).then_inc(zeroed, 16)
            n_left = sp.value_load(left[0:1, 0:1], min_val=16, max_val=16 * (MAXT + 1))
            wait_alone(sp, zeroed, n_left, sp_passed)

        @block.gpsimd
        def _(pool):
            for j in range(J):
                pool.wait_ge(pages_ready, j + 1)
                pool.indirect_dma_start(listed[:, j], None, places.rearrange("(a b) o -> a (b o)", b=128),
                                        bass.IndirectOffsetOnAxis(ap=page[:, j:j + 1], axis=0)).then_inc(listed_loaded[j], 16)

        @block.scalar
        def _(act):
            act.wait_ge(fields_ready, 1)
            act.dma_start(tab_dram.rearrange("(j p) f -> p j f", p=128), fields[:]).then_inc(fields_stored, 16)
            act.wait_ge(fields_stored, 16)
            act.dma_start(tok["tile"][:, 0:MAXT * FIELDS], tab_dram.rearrange("t f -> (t f)")[None, :]).then_inc(fields_loaded, 16)
            act.wait_ge(fields_loaded, 16)


def experts(nc, once, c, tok, dram, xm_rows, y_rows):
    WIDE = 4
    x_loaded = [once(f"expert_x_loaded{q}") for q in range(WIDE)]
    names = ("w_loaded rows turned xT h tanh silu h_turned hT y y_kept pool_passed act_passed "
             "y_stored0 y_stored1 y_stored2 y_stored3")
    with loop_semaphores(nc, names) as s, ExitStack() as ctx:
        def sb(name, shape, dt=F32):
            return ctx.enter_context(nc.sbuf_tensor(name, shape, dt))

        def banks(name):
            return [ctx.enter_context(nc.psum_tensor(f"p5_{name}{q}", [128, 512], F32)) for q in range(2)]
        w1 = sb("p5_w1", [128, 2, KH * EI])
        w2 = sb("p5_w2", [EK, 2, 2 * H])
        idx = sb("p5_idx", [128, WIDE, 1], mybir.dt.uint32)
        xe = sb("p5_xe", [128, WIDE, H])
        xT = sb("p5_xT", [128, 2, KH * TILE])
        th = sb("p5_th", [128, 2, EI])
        hh = sb("p5_h", [128, 2, EI])
        hT = sb("p5_hT", [EK, 2, 2 * TILE])
        ys = sb("p5_y", [128, WIDE, H])
        ps_x, ps_h, ps_t, ps_y = banks("turn"), banks("h"), banks("ht"), banks("y")
        block = ctx.enter_context(nc.Block())

        def field(eng, n, k, top):
            return eng.value_load(tok["tile"][0:1, bass.ds(n * FIELDS + k, 1)], min_val=0, max_val=top)

        def rounds(eng):
            return eng.value_load(tok["rounds"][0:1, 0:1], min_val=1, max_val=MAXT // WIDE)

        @block.sync
        def _(sp):
            with sp.Fori(0, NE) as e:
                freed = sp.value_load(tok["freed"][0:1, bass.ds(e, 1)], min_val=0, max_val=MAXT)
                sp.wait_ge(s["y"], freed + LEAD)
                sp.wait_ge(s["w_loaded"], 32 * e + LEAD)
                sp.dma_start(w1[:, bass.ds(e % 2, 1), :].rearrange("p a b -> p (a b)"),
                             dram["w1"][bass.ds(e, 1)].rearrange("a p b -> (a p) b")).then_inc(s["w_loaded"], 16)
                sp.dma_start(w2[:, bass.ds(e % 2, 1), :].rearrange("p a b -> p (a b)"),
                             dram["w2"][bass.ds(e, 1)].rearrange("a p b -> (a p) b")).then_inc(s["w_loaded"], 16)
            sp.wait_ge(s["w_loaded"], 32 * NE + LEAD)

        @block.gpsimd
        def _(pool):
            def gather(n, q):
                wait_alone(pool, s["rows"], done(n), s["pool_passed"])
                pool.indirect_dma_start(xe[:, q], None, xm_rows, bass.IndirectOffsetOnAxis(ap=idx[:, q], axis=0))\
                    .then_inc(x_loaded[q], 16)

            for n in range(WIDE + 3):
                gather(n, n % WIDE)
            with pool.Fori(0, rounds(pool)) as it:
                for q in range(WIDE):
                    gather(WIDE * it + q + WIDE + 3, (q + 3) % WIDE)
            n_rounds = rounds(pool)
            for q in range(WIDE):
                wait_alone(pool, x_loaded[q], 16 * n_rounds + 16 + (16 if q < 3 else 0), s["pool_passed"])

        @block.tensor
        def _(pe):
            def turn(n, q, it):
                pe.wait_ge(x_loaded[q], 16 * it + 16)
                pe.wait_ge(s["xT"], done(n, 2))
                for k in range(KH):
                    last = nc.tensor.transpose(ps_x[q % 2][:, k * TILE:(k + 1) * TILE], xe[:, q, k * 128:(k + 1) * 128],
                                               c["ident"][:])
                last.then_inc(s["turned"], 1)

            def up(n, q):
                e, half = field(pe, n, 0, NE - 1), field(pe, n, 1, 1)
                pe.wait_ge(s["w_loaded"], 32 * e + 32 + LEAD)
                pe.wait_ge(s["xT"], done(n))
                pe.wait_ge(s["silu"], done(n, 2))
                for k in range(KH):
                    last = nc.tensor.matmul(ps_h[q % 2][:, 0:EI], xT[:, q % 2, k * TILE:(k + 1) * TILE],
                                            w1[:, bass.ds(half, 1), k * EI:(k + 1) * EI].rearrange("p a b -> p (a b)"),
                                            start=(k == 0), stop=(k == KH - 1))
                last.then_inc(s["h"], 1)

            def turn_hidden(n, q):
                pe.wait_ge(s["silu"], done(n))
                pe.wait_ge(s["hT"], done(n, 2))
                for k in range(2):
                    last = nc.tensor.transpose(ps_t[q % 2][0:EK, k * TILE:(k + 1) * TILE], hh[:, q % 2, k * EK:(k + 1) * EK],
                                               c["ident"][:])
                last.then_inc(s["h_turned"], 1)

            def down(n, q):
                half = field(pe, n, 1, 1)
                pe.wait_ge(s["hT"], done(n))
                pe.wait_ge(s["y_kept"], done(n, 2))
                for k in range(2):
                    last = nc.tensor.matmul(ps_y[q % 2][:, 0:H], hT[:, q % 2, k * TILE:(k + 1) * TILE],
                                            w2[:, bass.ds(half, 1), k * H:(k + 1) * H].rearrange("p a b -> p (a b)"),
                                            start=(k == 0), stop=(k == 1))
                last.then_inc(s["y"], 1)

            turn(0, 0, 0)
            up(0, 0)
            turn(1, 1, 0)
            turn(2, 2, 0)
            up(1, 1)
            turn_hidden(0, 0)
            with pe.Fori(0, rounds(pe)) as it:
                for q in range(WIDE):
                    n = WIDE * it + q
                    turn(n + 3, (q + 3) % WIDE, it + (q + 3) // WIDE)
                    up(n + 2, (q + 2) % WIDE)
                    turn_hidden(n + 1, (q + 1) % WIDE)
                    down(n, q)

        @block.vector
        def _(dve):
            def rows(n, q):
                nc.vector.tensor_copy(idx[:, q], tok["rows"][:, bass.ds(n, 1)]).then_inc(s["rows"], 1)

            def keep_xT(n, q):
                dve.wait_ge(s["turned"], done(n))
                dve.wait_ge(s["h"], done(n, 2))
                nc.vector.tensor_copy(xT[:, q % 2], ps_x[q % 2][:, 0:KH * TILE]).then_inc(s["xT"], 1)

            def silu(n, q):
                dve.wait_ge(s["tanh"], done(n))
                dve.wait_ge(s["h_turned"], done(n, 2))
                nc.vector.scalar_tensor_tensor(hh[:, q % 2], th[:, q % 2], 1.0, ps_h[q % 2][:, 0:EI], ALU.add, ALU.mult)\
                    .then_inc(s["silu"], 1)

            for q in range(WIDE):
                rows(q, q)
            keep_xT(0, 0)
            rows(WIDE, 0)
            keep_xT(1, 1)
            rows(WIDE + 1, 1)
            silu(0, 0)
            keep_xT(2, 2)
            rows(WIDE + 2, 2)
            silu(1, 1)
            with dve.Fori(0, rounds(dve)) as it:
                for q in range(WIDE):
                    n = WIDE * it + q
                    keep_xT(n + 3, (q + 3) % WIDE)
                    rows(n + 3 + WIDE, (q + 3) % WIDE)
                    silu(n + 2, (q + 2) % WIDE)

        @block.scalar
        def _(act):
            def tanh(n, q):
                act.wait_ge(s["h"], done(n))
                act.wait_ge(s["silu"], done(n, 2))
                nc.scalar.activation(th[:, q % 2], ps_h[q % 2][:, 0:EI], ACT.Tanh, scale=0.5).then_inc(s["tanh"], 1)

            def keep_hT(n, q):
                act.wait_ge(s["h_turned"], done(n))
                act.wait_ge(s["y"], done(n, 2))
                nc.scalar.activation(hT[:, q % 2], ps_t[q % 2][0:EK, 0:2 * TILE], ACT.Copy).then_inc(s["hT"], 1)

            tanh(0, 0)
            tanh(1, 1)
            keep_hT(0, 0)
            with act.Fori(0, rounds(act)) as it:
                for q in range(WIDE):
                    n = WIDE * it + q
                    tanh(n + 2, (q + 2) % WIDE)
                    keep_hT(n + 1, (q + 1) % WIDE)
                    act.wait_ge(s["y"], done(n))
                    act.wait_ge(s[f"y_stored{q}"], 16 * it + LEAD)
                    nc.scalar.activation(ys[:, q], ps_y[q % 2][:, 0:H], ACT.Copy, scale=0.5).then_inc(s["y_kept"], 1)
                    act.wait_ge(s["y_kept"], done(n))
                    act.dma_start(y_rows[bass.ds(n * 128, 128), :], ys[:, q]).then_inc(s[f"y_stored{q}"], 16)
            n_rounds = rounds(act)
            for q in range(WIDE):
                wait_alone(act, s[f"y_stored{q}"], 16 * n_rounds + LEAD, s["act_passed"])


def combine(nc, once, c, tok, y_rows, out):
    gathered = [once(f"gathered{q}") for q in range(2)]
    names = ("copied shifts slots sum0 sum1 sum2 sum3 sum4 sum5 stats mean_var var rstd nbias norm result pool_passed "
             "dve_passed stored0 stored1")
    with loop_semaphores(nc, names) as s, ExitStack() as ctx:
        def sb(name, shape, dt=F32):
            return ctx.enter_context(nc.sbuf_tensor(name, shape, dt))
        slot = sb("p6_slot", [128, 2, TOPK], mybir.dt.uint32)
        shift = sb("p6_shift", [128, 2, TOPK])
        choice = sb("p6_choice", [128, 2, TOPK])
        junk = sb("p6_junk", [128, 2, TOPK, NE])
        wt = sb("p6_w", [128, 2, TOPK])
        yg = sb("p6_y", [128, 2, TOPK, H])
        acc = sb("p6_acc", [128, 2, H])
        res = sb("p6_res", [128, 2, H])
        st = sb("p6_st", [128, 2, 6])
        mv = sb("p6_mv", [128, 2, 2])
        small = sb("p6_small", [128, 2, 4])
        block = ctx.enter_context(nc.Block())

        @block.gpsimd
        def _(pool):
            with pool.Fori(0, NT // 2) as it:
                for q in range(2):
                    n = 2 * it + q
                    wait_alone(pool, s["slots"], done(n), s["pool_passed"])
                    wait_alone(pool, s[f"sum{TOPK - 1}"], done(n, 2), s["pool_passed"])
                    for k in range(TOPK):
                        pool.indirect_dma_start(yg[:, q, k, :], None, y_rows,
                                                bass.IndirectOffsetOnAxis(ap=slot[:, q, k:k + 1], axis=0))\
                            .then_inc(gathered[q], 16)
                    if q == 1:
                        for r in range(2):
                            pool.wait_ge(s["var"], done(2 * it + r))
                            nc.gpsimd.tensor_tensor(small[:, r, 1:2], small[:, r, 0:1], c["minus_half"][:, 0:1], ALU.pow)\
                                .then_inc(s["rstd"], 1)

        @block.vector
        def _(dve):
            with dve.Fori(0, NT // 2) as it:
                for q in range(2):
                    n = 2 * it + q
                    dve.wait_ge(s[f"sum{TOPK - 1}"], done(n, 2))
                    nc.vector.tensor_copy(wt[:, q], tok["weight"][:, bass.ds(n, 1), :].rearrange("p a b -> p (a b)"))
                    nc.vector.tensor_copy(choice[:, q], tok["choice"][:, bass.ds(n, 1), :].rearrange("p a b -> p (a b)"))\
                        .then_inc(s["copied"], 1)
                    dve.wait_ge(s["copied"], done(n))
                    for k in range(TOPK):
                        last = nc.vector.scalar_tensor_tensor(junk[:, q, k], c["expert"][:], choice[:, q, k:k + 1],
                                                              tok["shift"][:], ALU.is_equal, ALU.mult,
                                                              accum_out=shift[:, q, k:k + 1])
                    last.then_inc(s["shifts"], 1)
                    dve.wait_ge(s["shifts"], done(n))
                    nc.vector.tensor_tensor(slot[:, q], tok["slot"][:, bass.ds(n, 1), :].rearrange("p a b -> p (a b)"),
                                            shift[:, q], ALU.add).then_inc(s["slots"], 1)
                for q in range(2):
                    n = 2 * it + q
                    dve.wait_ge(gathered[q], 16 * TOPK * it + 16 * TOPK)
                    dve.wait_ge(s["slots"], done(n))
                    dve.wait_ge(s["norm"], done(n, 2))
                    for k in range(TOPK):
                        if k:
                            dve.wait_ge(s[f"sum{k - 1}"], done(n))
                        before = acc[:, q] if k else tok["shared"][:, bass.ds(n, 1), :].rearrange("p a b -> p (a b)")
                        nc.vector.scalar_tensor_tensor(acc[:, q], yg[:, q, k, :], wt[:, q, k:k + 1], before,
                                                       ALU.mult, ALU.add).then_inc(s[f"sum{k}"], 1)
                    dve.wait_ge(s[f"sum{TOPK - 1}"], done(n))
                    nc.vector.bn_stats(st[:, q], acc[:, q]).then_inc(s["stats"], 1)
                    wait_alone(dve, s["stats"], done(n), s["dve_passed"])
                    nc.vector.bn_aggr(mv[:, q], st[:, q]).then_inc(s["mean_var"], 1)
                    dve.wait_ge(s["mean_var"], done(n))
                    nc.vector.tensor_scalar(small[:, q, 0:1], mv[:, q, 1:2], EPS, None, ALU.add).then_inc(s["var"], 1)
                for q in range(2):
                    n = 2 * it + q
                    dve.wait_ge(s["rstd"], done(n))
                    nc.vector.scalar_tensor_tensor(small[:, q, 2:3], mv[:, q, 0:1], -1.0, small[:, q, 1:2],
                                                   ALU.mult, ALU.mult).then_inc(s["nbias"], 1)
                    dve.wait_ge(s["norm"], done(n))
                    dve.wait_ge(s[f"stored{q}"], 16 * it + LEAD)
                    nc.vector.tensor_tensor(res[:, q], acc[:, q], tok["x2"][:, bass.ds(n, 1), :].rearrange("p a b -> p (a b)"),
                                            ALU.add).then_inc(s["result"], 1)

        @block.scalar
        def _(act):
            with act.Fori(0, NT // 2) as it:
                for q in range(2):
                    n = 2 * it + q
                    act.wait_ge(s["nbias"], done(n))
                    nc.scalar.activation(acc[:, q], acc[:, q], ACT.Identity, bias=small[:, q, 2:3], scale=small[:, q, 1:2])\
                        .then_inc(s["norm"], 1)

        @block.sync
        def _(sp):
            with sp.Fori(0, NT // 2) as it:
                for q in range(2):
                    n = 2 * it + q
                    sp.wait_ge(s["result"], done(n))
                    sp.dma_start(out[:, bass.ds(n, 1), :].rearrange("p a b -> p (a b)"), res[:, q])\
                        .then_inc(s[f"stored{q}"], 16)
            for q in range(2):
                sp.wait_ge(s[f"stored{q}"], 16 * (NT // 2) + LEAD)


def build(nc, src, dram, out):
    xm_rows = nc.dram_tensor("xm_rows", (B * T + 128, H), F32, kind="Internal").ap()
    places = nc.dram_tensor("places", (NE * REGION, 1), F32, kind="Internal").ap()
    y_rows = nc.dram_tensor("y_rows", (MAXT * 128 + 128, H), F32, kind="Internal").ap()
    tab_dram = nc.dram_tensor("tile_table", (MAXT, FIELDS), mybir.dt.int32, kind="Internal").ap()
    with ExitStack() as ctx:
        def sb(name, shape, dt=F32):
            return ctx.enter_context(nc.sbuf_tensor(name, shape, dt))
        def once(name):
            return ctx.enter_context(nc.semaphore(name))
        c = load_constants(nc, sb, once, src)
        tokT = sb("tokT", [128, NT, KH, TILE])
        attn = tokT[:].rearrange("p n k t -> p n (k t)")
        with ExitStack() as inner:
            res = {"tokT": tokT, "attn": attn}
            for name, shape in (("rstd", [128, NT]), ("nbias", [128, NT]), ("dt", [128, NT, NH]), ("dA", [128, NT, NH]),
                                ("to_end", [128, NT, NH]), ("decay0", [128, NT, NH]), ("decay1", [128, NT, NH]),
                                ("dAp", [128, CT, NT, HG])):
                res[name] = inner.enter_context(nc.sbuf_tensor("r_" + name, shape, F32))
            norm_in(nc, c, res, dram["x"])
            decays(nc, c, res)
            scan(nc, once, c, res, dram["x"])
        tok = {"xm": attn, "x2": sb("x2", [128, NT, H]), "shared": sb("shared", [128, NT, H]),
               "weight": sb("weight", [128, NT, TOPK]), "slot": sb("slot", [128, NT, TOPK]),
               "choice": sb("choice", [128, NT, TOPK]), "shift": sb("shift", [128, NE]), "rows": sb("rows", [128, MAXT + 8]),
               "run": sb("run", [128, NE]), "tile": sb("tile", [1, (MAXT + 4) * FIELDS], mybir.dt.int32),
               "freed": sb("freed", [1, NE], mybir.dt.int32), "rounds": sb("rounds", [1, 1], mybir.dt.int32)}
        route(nc, once, c, tok, dram["x"], xm_rows, places)
        tables(nc, once, c, tok, places, tab_dram, y_rows)
        experts(nc, once, c, tok, dram, xm_rows, y_rows)
        combine(nc, once, c, tok, y_rows, out)


def constants():
    p, l = np.arange(128)[:, None], np.arange(128)[None, :]
    same = (p // CH) == (l // CH)
    f = np.float32
    k = {"ident": np.eye(128), "ones": np.ones((128, 4)), "minus_half": np.full((128, 8), -0.5)}
    k["later"] = same & (p > l)
    k["until"] = same & (p <= l)
    k["until32"] = (p % CH) <= l[:, :CH]
    k["until32q"] = 0.25 * ((p % CH) <= l[:, :CH])
    for j in range(2):
        k[f"whole{j}"] = (p // CH) == 2 * (l // NS) + j
    k["before"] = p < l
    k["all"] = np.ones((128, 128))
    k["expert"] = np.broadcast_to(np.arange(NE), (128, NE))
    k["region"] = np.broadcast_to(np.arange(NE) * REGION, (128, NE))
    k["token"] = np.arange(B * T).reshape(NT, 128).T
    k["tile"] = np.arange(MAXT).reshape(-1, 128).T
    return {n: np.ascontiguousarray(a, dtype=f) for n, a in k.items()}


def kernel(L0_attn_hidden_states, L0_attn_ln_weight, L0_attn_in_proj_w, L0_attn_conv_w, L0_attn_conv_b, L0_attn_dt_bias,
           L0_attn_A_log, L0_attn_D, L0_attn_norm_weight, L0_attn_out_proj_w, L0_ffn_gate_w, L0_ffn_experts_w1,
           L0_ffn_experts_w2, L0_ffn_shared_gate_up, L0_ffn_shared_down):
    import concourse.bacc as bacc
    from concourse.bass_utils import run_bass_kernel_spmd

    def columns(a):
        return np.asarray(a).reshape(-1, 128).T

    def rows(a):
        a = np.asarray(a)
        return a.reshape(-1, 128, a.shape[1]).transpose(1, 0, 2)

    def everywhere(a):
        return np.broadcast_to(np.asarray(a), (128, len(a)))

    x = np.asarray(L0_attn_hidden_states)
    tiles = x.reshape(PAIRS, 2, NT // PAIRS, HALF, H).transpose(1, 3, 2, 0, 4).reshape(128, NT, H)
    w_in = np.asarray(L0_attn_in_proj_w)
    arrays = constants()
    arrays["w_gate"] = rows(w_in[:CI].T)
    arrays["w_xbc"] = rows(w_in[CI:CI + NB * 128].T)
    arrays["w_dt"] = rows(w_in[CI + NB * 128:].T)
    arrays["w_out"] = rows(np.asarray(L0_attn_out_proj_w).T)
    arrays["ln_w"] = columns(L0_attn_ln_weight)
    arrays["norm_w"] = columns(L0_attn_norm_weight)
    arrays["conv_b"] = columns(L0_attn_conv_b)
    arrays["conv_w"] = rows(L0_attn_conv_w)
    arrays["skip"] = columns(np.repeat(np.asarray(L0_attn_D), P))
    arrays["dt_bias"] = everywhere(L0_attn_dt_bias)
    arrays["a_log"] = everywhere(L0_attn_A_log)
    gu = np.asarray(L0_ffn_shared_gate_up).T
    arrays["router_w"] = rows(np.asarray(L0_ffn_gate_w).T)
    arrays["sg_w"] = rows(gu[:, :SI])
    arrays["su_w"] = rows(gu[:, SI:])
    down = np.zeros((SB * 128, H), np.float32)
    down[:SI] = np.asarray(L0_ffn_shared_down).T
    arrays["sd_w"] = rows(down)
    arrays = {n: np.ascontiguousarray(a) for n, a in arrays.items()}
    w1 = np.asarray(L0_ffn_experts_w1).transpose(0, 2, 1).reshape(NE, KH, 128, EI).transpose(0, 2, 1, 3)
    w2 = np.asarray(L0_ffn_experts_w2).transpose(0, 2, 1).reshape(NE, 2, EK, H).transpose(0, 2, 1, 3)
    big = {"x": tiles, "w1": w1.reshape(NE, 128, KH * EI), "w2": w2.reshape(NE, EK, 2 * H)}
    big = {n: np.ascontiguousarray(a) for n, a in big.items()}

    nc = bacc.Bacc("TRN2", target_bir_lowering=False, num_devices=1)
    src = {n: nc.dram_tensor("in_" + n, a.shape, F32, kind="ExternalInput").ap() for n, a in arrays.items()}
    dram = {n: nc.dram_tensor("in_" + n, a.shape, F32, kind="ExternalInput").ap() for n, a in big.items()}
    out = nc.dram_tensor("out", (128, NT, H), F32, kind="ExternalOutput").ap()
    build(nc, src, dram, out)
    feed = {"in_" + n: a for n, a in (arrays | big).items()}
    got = run_bass_kernel_spmd(nc, [feed], core_ids=[0]).results[0]["out"]
    return got.reshape(2, HALF, NT // PAIRS, PAIRS, H).transpose(3, 0, 2, 1, 4).reshape(B, T, H)
```

```python
import numpy as np
import concourse.bass as bass
from concourse import mybir
from contextlib import ExitStack, contextmanager

F32 = mybir.dt.float32
ALU = mybir.AluOpType
ACT = mybir.ActivationFunctionType

B, T, H = 4, 1024, 256
CI, NS, NH, P = 512, 64, 64, 8
TAPS, CH = 4, 32
EPS = 1e-5
TILE = 128
NT = B * T // TILE
HALF = TILE // 2
PAIRS = B // 2
KH = H // 128
XB = CI // 128
NB = XB + 1
CT = TILE // CH
HQ = 4
HG = NH // HQ
GT = 4
NG = NT // GT
NE, EI, TOPK = 64, 176, 6
EK = EI // 2
SI = 2 * EI
SB = -(-SI // 128)
REGION = B * T + 128
BLANK = REGION // 32
assert NE * REGION % (128 * BLANK) == 0
WB = 4
MAXT = 256
assert MAXT >= B * T * TOPK // 128 + NE
LEAD = 4


def done(n, back=0):
    return n + 1 + LEAD - back


def wait_alone(eng, sem, value, passed):
    eng.wait_ge(sem, value)
    eng.sem_inc(passed, 1)


@contextmanager
def loop_semaphores(nc, names):
    with ExitStack() as ctx:
        sems = {name: ctx.enter_context(nc.semaphore(name)) for name in names.split()}
        with nc.Block() as block:
            @block.vector
            def _(dve):
                for s in sems.values():
                    dve.sem_inc(s, LEAD)
        yield sems
        with nc.Block() as block:
            @block.vector
            def _(dve):
                for s in sems.values():
                    dve.sem_clear(s)


def load_constants(nc, sb, once, src):
    early = ("minus_half", "ident", "ln_w", "w_dt", "dt_bias", "a_log", "later", "whole0", "whole1")
    c = {name: sb("c_" + name, list(ap.shape), F32) for name, ap in src.items()}
    loaded, a_exp, late_loaded = once("constants_loaded"), once("a_exp"), once("late_constants_loaded")
    with nc.Block() as block:
        @block.sync
        def _(sp):
            for name in early:
                sp.dma_start(c[name][:], src[name]).then_inc(loaded, 16)
            sp.wait_ge(loaded, 16 * len(early))

        @block.scalar
        def _(act):
            act.wait_ge(loaded, 16 * len(early))
            nc.scalar.activation(c["a_log"][:], c["a_log"][:], ACT.Exp).then_inc(a_exp, 1)
            act.wait_ge(a_exp, 1)
    return c, {name: ap for name, ap in src.items() if name not in early}, late_loaded


def norm_in(nc, c, res, x_tiles, late, late_loaded):
    names = ("x_loaded0 x_loaded1 stats mean_var var_eps rstd nbias ln sum_sq ms_eps rms xn turned "
             "scaled kept dt_done dt_kept kept_stats dve_passed pool_passed")
    with loop_semaphores(nc, names) as s, ExitStack() as ctx:
        def sb(name, shape):
            return ctx.enter_context(nc.sbuf_tensor(name, shape, F32))
        xin = sb("p1_x", [128, 2, GT, H])
        xl = sb("p1_xl", [128, 2, GT, H])
        sq = sb("p1_sq", [128, 2, GT, H])
        st = sb("p1_st", [128, 2, GT, 6])
        mv = sb("p1_mv", [128, 2, GT, 2])
        small = sb("p1_small", [128, 2, 6, GT])
        xs = sb("p1_xs", [128, 2, KH, GT * TILE])
        ps_turn = [[ctx.enter_context(nc.psum_tensor(f"p1_turn{q}{k}", [128, GT * TILE], F32)) for k in range(KH)]
                   for q in range(2)]
        ps_dt = [ctx.enter_context(nc.psum_tensor(f"p1_dt{q}", [128, GT, NH], F32)) for q in range(2)]
        block = ctx.enter_context(nc.Block())

        @block.sync
        def _(sp):
            with sp.Fori(0, NG // 2) as it:
                for q in range(2):
                    n = 2 * it + q
                    sp.wait_ge(s["ln"], done(n, 2))
                    sp.dma_start(xin[:, q], x_tiles[:, bass.ds(n * GT, GT), :]).then_inc(s[f"x_loaded{q}"], 16)
            for name, ap in late.items():
                sp.dma_start(c[name][:], ap).then_inc(late_loaded, 16)


        @block.vector
        def _(dve):
            def variance(n, q, it):
                dve.wait_ge(s[f"x_loaded{q}"], 16 * it + 16 + LEAD)
                for t in range(GT):
                    last = nc.vector.bn_stats(st[:, q, t, :], xin[:, q, t, :])
                last.then_inc(s["stats"], 1)
                wait_alone(dve, s["stats"], done(n), s["dve_passed"])
                for t in range(GT):
                    last = nc.vector.bn_aggr(mv[:, q, t, :], st[:, q, t, :])
                last.then_inc(s["mean_var"], 1)
                dve.wait_ge(s["mean_var"], done(n))
                nc.vector.tensor_scalar(small[:, q, 0], mv[:, q, :, 1], EPS, None, ALU.add).then_inc(s["var_eps"], 1)

            def nbias(n, q):
                dve.wait_ge(s["rstd"], done(n))
                nc.vector.scalar_tensor_tensor(small[:, q, 3], mv[:, q, :, 0], -1.0, small[:, q, 2],
                                               ALU.mult, ALU.mult).then_inc(s["nbias"], 1)
                dve.wait_ge(s["nbias"], done(n))
                nc.vector.tensor_copy(res["rstd"][:, bass.ds(n * GT, GT)], small[:, q, 2])
                nc.vector.tensor_copy(res["nbias"][:, bass.ds(n * GT, GT)], small[:, q, 3]).then_inc(s["kept_stats"], 1)

            def mean_square(n, q):
                dve.wait_ge(s["sum_sq"], done(n))
                nc.vector.tensor_scalar(small[:, q, 1], small[:, q, 4], 1.0 / H, EPS, ALU.mult, ALU.add)\
                    .then_inc(s["ms_eps"], 1)

            def scale(n, q):
                dve.wait_ge(s["rms"], done(n))
                for t in range(GT):
                    last = nc.vector.tensor_scalar(xl[:, q, t, :], xl[:, q, t, :], small[:, q, 5, t:t + 1],
                                                   None, ALU.mult)
                last.then_inc(s["xn"], 1)

            def add_bias(n, q):
                dve.wait_ge(s["dt_done"], done(n))
                nc.vector.tensor_tensor(res["dt"][:, bass.ds(n * GT, GT), :], ps_dt[q][:, :, :],
                                        c["dt_bias"][:, None, :].to_broadcast([128, GT, NH]),
                                        ALU.add).then_inc(s["dt_kept"], 1)

            def group_round(n, q, it, ahead=True, behind=True):
                mean_square(n, q)
                if ahead:
                    variance(n + 1, 1 - q, it)
                scale(n, q)
                if ahead:
                    nbias(n + 1, 1 - q)
                if behind:
                    add_bias(n - 1, 1 - q)

            variance(0, 0, 0)
            nbias(0, 0)
            group_round(0, 0, 0, behind=False)
            with dve.Fori(0, NG // 2 - 1) as it:
                group_round(2 * it + 1, 1, it + 1)
                group_round(2 * it + 2, 0, it + 1)
            group_round(NG - 1, 1, None, ahead=False)
            add_bias(NG - 1, 1)

        @block.gpsimd
        def _(pool):
            def rstd(n, q):
                pool.wait_ge(s["var_eps"], done(n))
                nc.gpsimd.tensor_tensor(small[:, q, 2], small[:, q, 0], c["minus_half"][:, 0:GT], ALU.pow)\
                    .then_inc(s["rstd"], 1)

            def rms(n, q):
                pool.wait_ge(s["ms_eps"], done(n))
                nc.gpsimd.tensor_tensor(small[:, q, 5], small[:, q, 1], c["minus_half"][:, 0:GT], ALU.pow)\
                    .then_inc(s["rms"], 1)

            def keep(n, q):
                wait_alone(pool, s["scaled"], done(n), s["pool_passed"])
                for k in range(KH):
                    last = nc.gpsimd.tensor_copy(res["tokT"][:, bass.ds(n * GT, GT), k, :],
                                                 xs[:, q, k, :].rearrange("p (a b) -> p a b", a=GT))
                last.then_inc(s["kept"], 1)

            rstd(0, 0)
            rms(0, 0)
            rstd(1, 1)
            with pool.Fori(0, NG // 2 - 1) as it:
                for q in (1, 0):
                    n = 2 * it + 2 - q
                    rms(n, q)
                    rstd(n + 1, 1 - q)
                    keep(n - 1, 1 - q)
            rms(NG - 1, 1)
            keep(NG - 2, 0)
            keep(NG - 1, 1)

        @block.scalar
        def _(act):
            def norm(n, q):
                act.wait_ge(s["nbias"], done(n))
                act.wait_ge(s["turned"], done(n, 2))
                for t in range(GT):
                    last = nc.scalar.activation(xl[:, q, t, :], xin[:, q, t, :], ACT.Identity,
                                                bias=small[:, q, 3, t:t + 1], scale=small[:, q, 2, t:t + 1])
                last.then_inc(s["ln"], 1)
                act.wait_ge(s["ln"], done(n))
                for t in range(GT):
                    last = nc.scalar.activation(sq[:, q, t, :], xl[:, q, t, :], ACT.Square,
                                                accum_out=small[:, q, 4, t:t + 1])
                last.then_inc(s["sum_sq"], 1)

            def scale_turned(n, q):
                act.wait_ge(s["turned"], done(n))
                act.wait_ge(s["kept"], done(n, 2))
                act.wait_ge(s["dt_done"], done(n, 2))
                for k in range(KH):
                    last = nc.scalar.activation(xs[:, q, k, :], ps_turn[q][k][:, :], ACT.Identity,
                                                scale=c["ln_w"][:, k:k + 1])
                last.then_inc(s["scaled"], 1)

            norm(0, 0)
            norm(1, 1)
            scale_turned(0, 0)
            with act.Fori(0, NG // 2 - 1) as it:
                for q in (1, 0):
                    n = 2 * it + 2 - q
                    norm(n + 1, 1 - q)
                    scale_turned(n, q)
            scale_turned(NG - 1, 1)

        @block.tensor
        def _(pe):
            with pe.Fori(0, NG // 2) as it:
                for q in range(2):
                    n = 2 * it + q
                    pe.wait_ge(s["xn"], done(n))
                    pe.wait_ge(s["scaled"], done(n, 2))
                    for k in range(KH):
                        for t in range(GT):
                            last = nc.tensor.transpose(ps_turn[q][k][:, t * TILE:(t + 1) * TILE],
                                                       xl[:, q, t, k * 128:(k + 1) * 128], c["ident"][:])
                    last.then_inc(s["turned"], 1)
                    pe.wait_ge(s["scaled"], done(n))
                    pe.wait_ge(s["dt_kept"], done(n, 2))
                    for t in range(GT):
                        for k in range(KH):
                            last = nc.tensor.matmul(ps_dt[q][:, t, :], xs[:, q, k, t * TILE:(t + 1) * TILE],
                                                    c["w_dt"][:, k, :], start=(k == 0), stop=(k == KH - 1))
                    last.then_inc(s["dt_done"], 1)


def decays(nc, c, res):
    QT = 8
    NQ = NT // QT
    W = QT * NH
    names = "absolute small_exp one_more log correction correction2 halved softplus dA sums exps states_dt permuted permuted_kept"
    with loop_semaphores(nc, names) as s, ExitStack() as ctx:
        def sb(name, shape):
            return ctx.enter_context(nc.sbuf_tensor(name, shape, F32))
        e = sb("p2_e", [128, NQ, W])
        u = sb("p2_u", [128, NQ, W])
        lg = sb("p2_l", [128, NQ, W])
        ps = [ctx.enter_context(nc.psum_tensor(f"p2_sum{k}", [128, W], F32)) for k in range(3)]
        ps_perm = [ctx.enter_context(nc.psum_tensor(f"p2_perm{k}", [128, W], F32)) for k in range(CT)]
        block = ctx.enter_context(nc.Block())

        def piece(name, n):
            return res[name][:, n * QT:(n + 1) * QT, :].rearrange("p a b -> p (a b)")

        @block.scalar
        def _(act):
            for n in range(NQ):
                nc.scalar.activation(e[:, n], piece("dt", n), ACT.Abs).then_inc(s["absolute"], 1)
            for n in range(NQ):
                act.wait_ge(s["absolute"], done(n))
                nc.scalar.activation(e[:, n], e[:, n], ACT.Exp, scale=-1.0).then_inc(s["small_exp"], 1)
            for n in range(NQ):
                act.wait_ge(s["one_more"], done(n))
                nc.scalar.activation(lg[:, n], u[:, n], ACT.Ln).then_inc(s["log"], 1)
            for n in range(NQ):
                act.wait_ge(s["sums"], done(n))
                for k, name in enumerate(("to_end", "decay0", "decay1")):
                    last = nc.scalar.activation(piece(name, n), ps[k][:], ACT.Exp)
                last.then_inc(s["exps"], 1)
                act.wait_ge(s["permuted"], done(n))
                for ch in range(CT):
                    last = nc.scalar.activation(res["dAp"][:, ch, n * QT:(n + 1) * QT, :],
                                                ps_perm[ch][:, 0:QT * HG].rearrange("p (a b) -> p a b", a=QT),
                                                ACT.Copy)
                last.then_inc(s["permuted_kept"], 1)

        @block.vector
        def _(dve):
            for n in range(NQ):
                dve.wait_ge(s["small_exp"], done(n))
                nc.vector.tensor_scalar(u[:, n], e[:, n], 1.0, None, ALU.add).then_inc(s["one_more"], 1)
            for n in range(NQ):
                z = piece("dt", n)
                dve.wait_ge(s["log"], done(n))
                nc.vector.scalar_tensor_tensor(u[:, n], u[:, n], -1.0, e[:, n], ALU.add, ALU.subtract).then_inc(s["correction"], 1)
                dve.wait_ge(s["correction"], done(n))
                nc.vector.tensor_tensor(u[:, n], lg[:, n], u[:, n], ALU.subtract).then_inc(s["correction2"], 1)
                dve.wait_ge(s["correction2"], done(n))
                nc.vector.scalar_tensor_tensor(z, z, 0.0, u[:, n], ALU.max, ALU.add).then_inc(s["softplus"], 1)
                dve.wait_ge(s["softplus"], done(n))
                nc.vector.scalar_tensor_tensor(res["dA"][:, n * QT:(n + 1) * QT, :], res["dt"][:, n * QT:(n + 1) * QT, :], -1.0,
                                               c["a_log"][:, None, :].to_broadcast([128, QT, NH]),
                                               ALU.mult, ALU.mult).then_inc(s["dA"], 1)
            for n in range(NQ):
                z = piece("dt", n)
                dve.wait_ge(s["exps"], done(n))
                nc.vector.scalar_tensor_tensor(piece("to_end", n), piece("to_end", n), 0.25, z, ALU.mult, ALU.mult)\
                    .then_inc(s["states_dt"], 1)
                dve.wait_ge(s["dA"], done(n))
                dve.wait_ge(s["states_dt"], done(n))
                nc.vector.tensor_scalar(z, z, 0.5, None, ALU.mult).then_inc(s["halved"], 1)

        @block.tensor
        def _(pe):
            for n in range(NQ):
                pe.wait_ge(s["dA"], done(n))
                pe.wait_ge(s["exps"], done(n, 1))
                dA = piece("dA", n)
                for k, name in enumerate(("later", "whole0", "whole1")):
                    last = nc.tensor.matmul(ps[k][:], c[name][:], dA, start=True, stop=True)
                last.then_inc(s["sums"], 1)
                pe.wait_ge(s["permuted_kept"], done(n, 1))
                for ch in range(CT):
                    rows = slice(CH * ch, CH * ch + CH)
                    for h in range(HQ):
                        src = res["dA"][rows, n * QT:(n + 1) * QT, :].rearrange("p a (g h) -> p a g h", h=HQ)[:, :, :, h]
                        last = nc.tensor.matmul(ps_perm[ch][CH * h:CH * h + CH, 0:QT * HG], c["ident"][rows, rows], src,
                                                start=True, stop=True)
                last.then_inc(s["permuted"], 1)


def scan(nc, once, c, res, x_tiles, late, late_loaded, blank, zero, places, xm_rows):
    names = ("proj_x0 proj_xbc proj_gate tap0 tap0_older0 tap0_older1 conv0 tap1 tap1_older0 tap1_older1 conv taps_halo conv_tanh xbc gate_tanh gate turned_x turned_bc moved_bc b_kept "
             "cb_done cb_masked masked_dA stage_dA "
             "d0 d1 d2 d3 e0 e1 e2 e3 m0 m1 m2 m3 x_dt x_dec spread y_diag e_sum e_exp y_off0 y_off1 "
             "s0 s1 decayed0 state0 decayed1 state1 "
             "y_scaled y_both y_gated y_sq out_done ms_eps rms xl attn x_loaded0 x_loaded1 pool_passed")
    with loop_semaphores(nc, names) as s, ExitStack() as ctx:
        def sb(name, shape):
            return ctx.enter_context(nc.sbuf_tensor(name, shape, F32))

        def bank(name):
            return ctx.enter_context(nc.psum_tensor(name, [128, 512], F32))
        xw = sb("xw", [128, 2, NB, 2, TAPS - 1 + HALF])
        acc = sb("acc", [128, NB, 2, HALF])
        th = sb("th", [128, NB, TILE])
        cv = sb("cv", [128, 2, NB, 2, HALF])
        gate = sb("gate", [128, 2, CI])
        gth = gate
        cx = sb("cx", [128, 2, 2, 2, CH])
        brep = sb("brep", [128, 2, 2, HQ, CH])
        bn = sb("bn", [128, 2, NS])
        cbm = sb("cbm", [128, 2, CT, CH])
        v = sb("v", [128, 2, CT, HG, CH])
        m = v
        dst = sb("dst", [128, 2, CI])
        xdt = sb("xdt", [128, 2, CI])
        xdec = sb("xdec", [128, 2, CI])
        xbd = sb("xbd", [128, 2, CT, HG, HQ * P])
        et = sb("et", [128, 2, CI])
        state = sb("state", [128, 2, CI])
        y = sb("y", [128, 2, CI])
        ysq = et
        skip_diag = sb("skip_diag", [128, XB, 128])
        xin = sb("xin", [128, 2, H])
        xl = sb("xl", [128, 2, H])
        small = sb("small", [128, 2, 4])
        pa, pb, pc, pd, pg, ph = (bank(f"bank_{k}") for k in ("xbc", "bc", "out", "x", "diag", "off"))
        ring = [bank("ring0"), bank("ring1")]
        parts = (range(0, 2), range(2, NB))
        projected = [pa[:, 0:128], pa[:, 128:256], pb[:, 128:256], pb[:, 256:384], pb[:, 0:128]]
        cb = pb[:, 0:TILE].rearrange("p (b j l) -> p b j l", b=2, j=2)
        off = ph[:].rearrange("p (k b j l) -> p k b j l", k=XB, b=2, j=2)

        cleared, scaled, blanked = once("scan_cleared"), once("weights_scaled"), once("places_blanked")
        with nc.Block() as block:
            @block.vector
            def _(dve):
                nc.vector.memset(xw[:], 0.0)
                nc.vector.memset(state[:], 0.0)
                nc.vector.memset(cx[:], 0.0)
                nc.vector.memset(blank[:], float(B * T))
                nc.vector.memset(zero[:], 0.0)
                nc.vector.memset(xbd[:], 0.0).then_inc(cleared, 1)
                dve.wait_ge(late_loaded, 16 * len(late))
                for b in range(XB):
                    nc.vector.tensor_scalar(c["w_out"][:, b, :], c["w_out"][:, b, :],
                                            c["norm_w"][:, b:b + 1], None, ALU.mult)
                    last = nc.vector.tensor_scalar(skip_diag[:, b, :], c["ident"][:], c["skip"][:, b:b + 1], 0.5,
                                                   ALU.mult, ALU.mult)
                last.then_inc(scaled, 1)
                dve.wait_ge(cleared, 1)
                dve.wait_ge(scaled, 1)

        block = ctx.enter_context(nc.Block())


        @block.sync
        def _(sp):
            parts_of_places = places.rearrange("(a p r) o -> a p (r o)", p=128, r=BLANK)
            for part in parts_of_places:
                sp.dma_start(part, blank[:]).then_inc(blanked, 16)
            sp.dma_start(xm_rows[B * T:B * T + 128, :], zero[:]).then_inc(blanked, 16)
            with sp.Fori(0, NT // 2) as it:
                for q in range(2):
                    n = 2 * it + q
                    sp.wait_ge(s["xl"], done(n, 2))
                    sp.dma_start(xin[:, q], x_tiles[:, bass.ds(n, 1), :].rearrange("p a b -> p (a b)")).then_inc(s[f"x_loaded{q}"], 16)
            sp.wait_ge(blanked, 16 * (NE * REGION // (128 * BLANK) + 1))

        @block.tensor
        def _(pe):
            def tokens(n):
                return [res["tokT"][:, bass.ds(n, 1), k, :].rearrange("p a b -> p (a b)") for k in range(KH)]

            def project_xbc(n, part):
                xt = tokens(n)
                pe.wait_ge(s[("gate", "cb_masked")[part]], done(n, 1))
                for b in parts[part]:
                    for k in range(KH):
                        last = nc.tensor.matmul(projected[b], c["w_xbc"][:, k, b * 128:(b + 1) * 128], xt[k],
                                                start=(k == 0), stop=(k == KH - 1))
                last.then_inc(s[("proj_x0", "proj_xbc")[part]], 1)

            def project_gate(n):
                xt = tokens(n)
                pe.wait_ge(s["tap0"], done(n))
                for b in range(XB):
                    for k in range(KH):
                        last = nc.tensor.matmul(pa[:, b * 128:(b + 1) * 128], c["w_gate"][:, k, b * 128:(b + 1) * 128],
                                                xt[k], start=(k == 0), stop=(k == KH - 1))
                last.then_inc(s["proj_gate"], 1)

            def turn(n, q):
                xbc = cv[:, q].rearrange("p a b c -> p a (b c)")
                pe.wait_ge(s["xbc"], done(n))
                nc.tensor.transpose(pb[:, 0:128], xbc[:, XB, :], c["ident"][:]).then_inc(s["turned_bc"], 1)
                pe.wait_ge(s["e_exp"], done(n, 1))
                for b in range(XB):
                    last = nc.tensor.transpose(pd[:, b * 128:(b + 1) * 128], xbc[:, b, :], c["ident"][:])
                last.then_inc(s["turned_x"], 1)

            def c_times_b(n, q):
                pe.wait_ge(s["moved_bc"], done(n))
                pe.wait_ge(s["b_kept"], done(n))
                for j in range(2):
                    last = nc.tensor.matmul(cb[:, :, j, :], brep[:, q, j].rearrange("p a b -> p (a b)"),
                                            cx[:, q, j].rearrange("p a b -> p (a b)"), start=True, stop=True)
                last.then_inc(s["cb_done"], 1)

            def decay_sums(n, q, chunks):
                pe.wait_ge(s["masked_dA"], done(n))
                for ch in chunks:
                    if ch >= 2:
                        pe.wait_ge(s[f"m{ch - 2}"], done(n))
                    else:
                        pe.wait_ge(s[f"state{ch}"], done(n, 1))
                    nc.tensor.matmul(ring[ch % 2][:], c["later"][:], v[:, q, ch].rearrange("p a b -> p (a b)"),
                                     start=True, stop=True).then_inc(s[f"d{ch}"], 1)

            def token_sums(n, q):
                pe.wait_ge(s["stage_dA"], done(n))
                pe.wait_ge(s["x_dec"], done(n))
                for b in range(XB):
                    last = nc.tensor.matmul(pd[:, b * 128:(b + 1) * 128], dst[:, q, b * 128:(b + 1) * 128],
                                            c["until"][:], start=True, stop=True)
                last.then_inc(s["e_sum"], 1)

            def within_chunks(n, q, chunks):
                xbc = cv[:, q].rearrange("p a b c -> p a (b c)")
                pe.wait_ge(s["spread"], done(n))
                pe.wait_ge(s["y_both"], done(n, 1))
                if 0 in chunks:
                    for b in range(XB):
                        nc.tensor.matmul(pg[:, 128 * b:128 * b + 128], skip_diag[:, b, :], xbc[:, b, :],
                                         start=(b == 0), stop=False)
                for ch in chunks:
                    pe.wait_ge(s[f"m{ch}"], done(n))
                    for g in range(HG):
                        last = nc.tensor.matmul(pg[32 * (g % 4):32 * (g % 4) + 32,
                                                   128 * (g // 4) + CH * ch:128 * (g // 4) + CH * ch + CH],
                                                xbd[:, q, ch, g, :], m[:, q, ch, g, :], start=False,
                                                stop=(ch == CT - 1 and g >= HG - 4))
                if CT - 1 in chunks:
                    last.then_inc(s["y_diag"], 1)

            def states(n, q, j):
                if j == 0:
                    pe.wait_ge(s["y_scaled"], done(n, 1))
                    pe.wait_ge(s["state1"], done(n, 2))
                else:
                    pe.wait_ge(s["state0"], done(n))
                for k in range(XB):
                    last = nc.tensor.matmul(off[:, k, :, j, :], state[:, q, 128 * k:128 * k + 128],
                                            cx[:, q, j].rearrange("p a b -> p (a b)"), start=True, stop=True)
                last.then_inc(s[f"y_off{j}"], 1)
                for b in range(2):
                    ch, rows = 2 * b + j, slice(CH * (2 * b + j), CH * (2 * b + j) + CH)
                    last = nc.tensor.matmul(ring[j][NS * b:NS * b + NS, :], bn[rows, q, :], xdec[rows, q, :],
                                            start=True, stop=True)
                last.then_inc(s[f"s{j}"], 1)

            def project_out(n, q):
                pe.wait_ge(s["y_gated"], done(n))
                pe.wait_ge(s["attn"], done(n, 1))
                for b in range(XB):
                    last = nc.tensor.matmul(pc[:, 0:H], y[:, q, b * 128:(b + 1) * 128], c["w_out"][:, b, :],
                                            start=(b == 0), stop=(b == XB - 1))
                pe.wait_ge(s["y_sq"], done(n))
                for b in range(XB):
                    last = nc.tensor.matmul(pc[:, H:H + 1], ysq[:, q, b * 128:(b + 1) * 128], c["ones"][:, 0:1],
                                            start=(b == 0), stop=(b == XB - 1))
                last.then_inc(s["out_done"], 1)

            def tile_round(n, q, ahead=2, behind=True):
                if ahead > 0:
                    project_xbc(n + 1, 1)
                decay_sums(n, q, (0, 1))
                if behind:
                    project_out(n - 1, 1 - q)
                token_sums(n, q)
                decay_sums(n, q, (2, 3))
                within_chunks(n, q, (0, 1))
                if ahead > 0:
                    project_gate(n + 1)
                within_chunks(n, q, (2, 3))
                if ahead > 0:
                    turn(n + 1, 1 - q)
                states(n, q, 0)
                if ahead > 0:
                    c_times_b(n + 1, 1 - q)
                if ahead > 1:
                    project_xbc(n + 2, 0)
                states(n, q, 1)

            project_xbc(0, 0)
            project_xbc(0, 1)
            project_gate(0)
            turn(0, 0)
            c_times_b(0, 0)
            project_xbc(1, 0)
            tile_round(0, 0, behind=False)
            with pe.Fori(0, NT // 2 - 2) as it:
                tile_round(2 * it + 1, 1)
                tile_round(2 * it + 2, 0)
            for n in range(NT - 3, NT):
                tile_round(n, n % 2, ahead=min(2, NT - 1 - n))
            project_out(NT - 1, 1)

        @block.scalar
        def _(act):
            def newest_tap(n, q):
                act.wait_ge(s["taps_halo"], done(n, 2))
                act.wait_ge(s["xbc"], done(n, 1))
                for blocks, ready, sem in zip(parts, ("proj_x0", "proj_xbc"), ("tap0", "tap1")):
                    act.wait_ge(s[ready], done(n))
                    for b in blocks:
                        src = projected[b].rearrange("p (a t) -> p a t", a=2)
                        nc.scalar.activation(xw[:, q, b, :, TAPS - 1:], src, ACT.Copy)
                        last = nc.scalar.activation(acc[:, b], src, ACT.Identity,
                                                    bias=c["conv_b"][:, b:b + 1], scale=c["conv_w"][:, b, TAPS - 1:TAPS])
                    last.then_inc(s[sem], 1)

            def gate_tanh(n, q):
                act.wait_ge(s["proj_gate"], done(n))
                act.wait_ge(s["y_gated"], done(n, 2))
                nc.scalar.activation(gth[:, q], pa[:], ACT.Tanh, scale=0.5).then_inc(s["gate_tanh"], 1)

            def conv_tanh(n):
                act.wait_ge(s["conv"], done(n))
                nc.scalar.activation(th[:].rearrange("p a b -> p (a b)"), acc[:].rearrange("p a b c -> p (a b c)"),
                                     ACT.Tanh, scale=0.5).then_inc(s["conv_tanh"], 1)

            def keep_b(n, q):
                act.wait_ge(s["turned_bc"], done(n))
                act.wait_ge(s["s1"], done(n, 2))
                nc.scalar.activation(bn[:, q], pb[:, 0:NS], ACT.Copy).then_inc(s["b_kept"], 1)

            def chunk_exps(n, chunks):
                for ch in chunks:
                    act.wait_ge(s[f"d{ch}"], done(n))
                    nc.scalar.activation(ring[ch % 2][:], ring[ch % 2][:], ACT.Exp).then_inc(s[f"e{ch}"], 1)

            def spread(n, q):
                act.wait_ge(s["x_dt"], done(n))
                act.wait_ge(s["y_diag"], done(n, 2))
                for ch in range(CT):
                    for h in range(HQ):
                        src = xdt[CH * ch:CH * ch + CH, q, :].rearrange("p (g h c) -> p g h c", h=HQ, c=P)[:, :, h, :]
                        last = nc.scalar.activation(xbd[CH * h:CH * h + CH, q, ch, :, P * h:P * h + P], src, ACT.Copy)
                last.then_inc(s["spread"], 1)

            def token_exps(n, q):
                act.wait_ge(s["e_sum"], done(n))
                act.wait_ge(s["out_done"], done(n, 2))
                nc.scalar.activation(et[:, q], pd[:], ACT.Exp).then_inc(s["e_exp"], 1)

            def layer_input(n, q, it):
                act.wait_ge(s[f"x_loaded{q}"], 16 * it + 16 + LEAD)
                act.wait_ge(s["attn"], done(n, 2))
                nc.scalar.activation(xl[:, q], xin[:, q], ACT.Identity, bias=res["nbias"][:, bass.ds(n, 1)],
                                     scale=res["rstd"][:, bass.ds(n, 1)]).then_inc(s["xl"], 1)

            def squares(n, q):
                act.wait_ge(s["y_gated"], done(n))
                nc.scalar.activation(ysq[:, q], y[:, q], ACT.Square).then_inc(s["y_sq"], 1)

            def tile_round(n, q, it, ahead=2):
                token_exps(n, q)
                chunk_exps(n, (2, 3))
                if ahead > 0:
                    conv_tanh(n + 1)
                    gate_tanh(n + 1, 1 - q)
                    keep_b(n + 1, 1 - q)
                    spread(n + 1, 1 - q)
                layer_input(n, q, it)
                if ahead > 1:
                    newest_tap(n + 2, q)
                if ahead > 0:
                    chunk_exps(n + 1, (0, 1))
                squares(n, q)

            newest_tap(0, 0)
            gate_tanh(0, 0)
            conv_tanh(0)
            keep_b(0, 0)
            spread(0, 0)
            newest_tap(1, 1)
            chunk_exps(0, (0, 1))
            tile_round(0, 0, 0)
            with act.Fori(0, NT // 2 - 2) as it:
                tile_round(2 * it + 1, 1, it)
                tile_round(2 * it + 2, 0, it + 1)
            for n in range(NT - 3, NT):
                tile_round(n, n % 2, n // 2, ahead=min(2, NT - 1 - n))

        @block.gpsimd
        def _(pool):
            def stage(n, q):
                wait_alone(pool, s["e_sum"], done(n, 2), s["pool_passed"])
                dA = res["dA"][:, bass.ds(n, 1), :].rearrange("p a b -> p (a b)")
                nc.gpsimd.tensor_copy(dst[:, q].rearrange("p (a b) -> p a b", b=P),
                                      dA[:, :, None].to_broadcast([128, NH, P])).then_inc(s["stage_dA"], 1)
                pool.wait_ge(s["y_diag"], done(n, 2))
                for ch in range(CT):
                    dA = res["dAp"][:, ch, bass.ds(n, 1), :].rearrange("p a b -> p (a b)")
                    last = nc.gpsimd.tensor_tensor(v[:, q, ch], dA[:, :, None].to_broadcast([128, HG, CH]),
                                                   c["until32"][:, None, :].to_broadcast([128, HG, CH]), ALU.mult)
                last.then_inc(s["masked_dA"], 1)

            def rms(n, q):
                pool.wait_ge(s["ms_eps"], done(n))
                nc.gpsimd.tensor_tensor(small[:, q, 1:2], small[:, q, 0:1], c["minus_half"][:, 0:1], ALU.pow)\
                    .then_inc(s["rms"], 1)

            stage(0, 0)
            stage(1, 1)
            with pool.Fori(0, NT // 2 - 1) as it:
                for q in range(2):
                    n = 2 * it + q
                    rms(n, q)
                    stage(n + 2, q)
            rms(NT - 2, 0)
            rms(NT - 1, 1)

        @block.vector
        def _(dve):
            def older_taps(n, q, part):
                sems = (("tap0", "tap0_older0", "tap0_older1", "conv0"), ("tap1", "tap1_older0", "tap1_older1", "conv"))[part]
                for k in range(TAPS - 1):
                    dve.wait_ge(s[sems[k]], done(n))
                    for b in parts[part]:
                        last = nc.vector.scalar_tensor_tensor(acc[:, b], xw[:, q, b, :, k:k + HALF],
                                                              c["conv_w"][:, b, k:k + 1], acc[:, b],
                                                              ALU.mult, ALU.add)
                    last.then_inc(s[sems[k + 1]], 1)
                if part == 0:
                    return
                dve.wait_ge(s["conv"], done(n))
                nc.vector.tensor_copy(xw[:, q, :, :, 0:TAPS - 1], xw[:, q, :, :, HALF:HALF + TAPS - 1])\
                    .then_inc(s["taps_halo"], 1)

            def silu_gate(n, q):
                dve.wait_ge(s["gate_tanh"], done(n))
                nc.vector.scalar_tensor_tensor(gate[:, q], gth[:, q], 1.0, pa[:], ALU.add, ALU.mult)\
                    .then_inc(s["gate"], 1)

            def silu_conv(n, q):
                dve.wait_ge(s["conv_tanh"], done(n))
                dve.wait_ge(s["y_diag"], done(n, 2))
                nc.vector.scalar_tensor_tensor(cv[:, q].rearrange("p a b c -> p (a b c)"),
                                               th[:].rearrange("p a b -> p (a b)"), 1.0,
                                               acc[:].rearrange("p a b c -> p (a b c)"), ALU.add, ALU.mult)\
                    .then_inc(s["xbc"], 1)

            def move_bc(n, q):
                xbc = cv[:, q].rearrange("p a b c -> p a (b c)")
                dve.wait_ge(s["xbc"], done(n))
                dve.wait_ge(s["y_off1"], done(n, 2))
                for b in range(2):
                    ct = xbc[NS:2 * NS, XB, HALF * b:HALF * b + HALF].rearrange("p (a b) -> p a b", a=2)
                    nc.vector.tensor_copy(cx[NS * b:NS * b + NS, q, :, b, :], ct)
                    bt = xbc[0:NS, XB, HALF * b:HALF * b + HALF].rearrange("p (a b) -> p a b", a=2)
                    last = nc.vector.tensor_copy(brep[NS * b:NS * b + NS, q],
                                                 bt[:, :, None, :].to_broadcast([NS, 2, HQ, CH]))
                last.then_inc(s["moved_bc"], 1)

            def scale_x(n, q):
                dve.wait_ge(s["turned_x"], done(n))
                dve.wait_ge(s["spread"], done(n, 2))
                px = pd[:].rearrange("p (h c) -> p h c", c=P)
                for out, by, sem in ((xdt, "dt", "x_dt"), (xdec, "to_end", "x_dec")):
                    if sem == "x_dec":
                        dve.wait_ge(s["s1"], done(n, 2))
                    f = res[by][:, bass.ds(n, 1), :].rearrange("p a b -> p (a b)")
                    nc.vector.tensor_tensor(out[:, q].rearrange("p (h c) -> p h c", c=P), px,
                                            f[:, :, None].to_broadcast([128, NH, P]), ALU.mult).then_inc(s[sem], 1)

            def mask_cb(n, q):
                dve.wait_ge(s["cb_done"], done(n))
                nc.vector.tensor_tensor(cbm[:, q], pb[:, 0:TILE].rearrange("p (a b) -> p a b", a=CT),
                                        c["until32q"][:, None, :].to_broadcast([128, CT, CH]), ALU.mult)\
                    .then_inc(s["cb_masked"], 1)

            def weigh(n, q, chunks):
                dve.wait_ge(s["cb_masked"], done(n))
                dve.wait_ge(s["y_diag"], done(n, 2))
                for ch in chunks:
                    dve.wait_ge(s[f"e{ch}"], done(n))
                    nc.vector.tensor_tensor(m[:, q, ch], ring[ch % 2][:].rearrange("p (a b) -> p a b", a=HG),
                                            cbm[:, q, ch][:, None, :].to_broadcast([128, HG, CH]), ALU.mult)\
                        .then_inc(s[f"m{ch}"], 1)

            def decay_state(n, q, j):
                st = state[:, q].rearrange("p (h c) -> p h c", c=P)
                f = res[f"decay{j}"][:, bass.ds(n, 1), :].rearrange("p a b -> p (a b)")
                dve.wait_ge(s[f"y_off{j}"], done(n))
                dve.wait_ge(s["state0" if j else "state1"], done(n) if j else done(n, 2))
                nc.vector.tensor_tensor(st, st, f[:, :, None].to_broadcast([128, NH, P]), ALU.mult)\
                    .then_inc(s[f"decayed{j}"], 1)

            def add_state(n, q, j):
                dve.wait_ge(s[f"decayed{j}"], done(n))
                dve.wait_ge(s[f"s{j}"], done(n))
                nc.vector.tensor_tensor(state[:, q], state[:, q], ring[j][:], ALU.add).then_inc(s[f"state{j}"], 1)

            def scale_off(n, q):
                dve.wait_ge(s["e_exp"], done(n))
                dve.wait_ge(s["y_sq"], done(n, 2))
                dve.wait_ge(s["out_done"], done(n, 2))
                nc.vector.scalar_tensor_tensor(y[:, q], ph[:], 0.5, et[:, q], ALU.mult, ALU.mult)\
                    .then_inc(s["y_scaled"], 1)

            def gated_y(n, q):
                dve.wait_ge(s["y_scaled"], done(n))
                dve.wait_ge(s["y_diag"], done(n))
                nc.vector.tensor_tensor(y[:, q], y[:, q], pg[:], ALU.add).then_inc(s["y_both"], 1)
                dve.wait_ge(s["y_both"], done(n))
                dve.wait_ge(s["gate"], done(n))
                nc.vector.scalar_tensor_tensor(y[:, q], y[:, q], 0.5, gate[:, q], ALU.mult, ALU.mult)\
                    .then_inc(s["y_gated"], 1)

            def mean_square(n, q):
                dve.wait_ge(s["out_done"], done(n))
                nc.vector.tensor_scalar(small[:, q, 0:1], pc[:, H:H + 1], 1.0 / CI, EPS, ALU.mult, ALU.add)\
                    .then_inc(s["ms_eps"], 1)

            def add_input(n, q):
                dve.wait_ge(s["rms"], done(n))
                dve.wait_ge(s["xl"], done(n))
                nc.vector.scalar_tensor_tensor(res["attn"][:, bass.ds(n, 1), :].rearrange("p a b -> p (a b)"),
                                               pc[:, 0:H], small[:, q, 1:2], xl[:, q], ALU.mult, ALU.add)\
                    .then_inc(s["attn"], 1)

            def tile_round(n, q, ahead=True, behind=True):
                if ahead:
                    older_taps(n + 1, 1 - q, 0)
                weigh(n, q, (0, 1))
                if ahead:
                    older_taps(n + 1, 1 - q, 1)
                if behind:
                    mean_square(n - 1, 1 - q)
                weigh(n, q, (2, 3))
                if ahead:
                    silu_conv(n + 1, 1 - q)
                    move_bc(n + 1, 1 - q)
                if behind:
                    add_input(n - 1, 1 - q)
                if ahead:
                    scale_x(n + 1, 1 - q)
                    silu_gate(n + 1, 1 - q)
                decay_state(n, q, 0)
                add_state(n, q, 0)
                if ahead:
                    mask_cb(n + 1, 1 - q)
                decay_state(n, q, 1)
                scale_off(n, q)
                add_state(n, q, 1)
                gated_y(n, q)

            older_taps(0, 0, 0)
            older_taps(0, 0, 1)
            silu_conv(0, 0)
            move_bc(0, 0)
            scale_x(0, 0)
            silu_gate(0, 0)
            mask_cb(0, 0)
            tile_round(0, 0, behind=False)
            with dve.Fori(0, NT // 2 - 1) as it:
                tile_round(2 * it + 1, 1)
                tile_round(2 * it + 2, 0)
            tile_round(NT - 1, 1, ahead=False)
            mean_square(NT - 1, 1)
            add_input(NT - 1, 1)


def route(nc, once, c, tok, x_tiles, xm_rows, places):
    names = ("x_loaded0 x_loaded1 a_stats a_mean_var a_var a_rstd a_nbias a_norm x2 b_stats b_mean_var b_var b_rstd "
             "b_nbias xm turned xm_turned logits top_max exps inv_sum probs top8 top_idx top_f top_sum top_inv "
             "weights scatters_done sel0 sel1 sel2 sel3 sel4 sel5 pos_done pos_kept slots_f slots xm_stored0 xm_stored1 dve_passed pool_passed "
             "gu0 gu1 gu2 gate_tanh0 gate_tanh1 gate_tanh2 silu0 silu1 silu2 h0 h1 h2 down down_kept before0 run0 run1 run2 run3")
    with loop_semaphores(nc, names) as s, ExitStack() as ctx:
        def sb(name, shape, dt=F32):
            return ctx.enter_context(nc.sbuf_tensor(name, shape, dt))
        xin = sb("p3_x", [128, 2, GT, H])
        an = sb("p3_an", [128, 2, GT, H])
        xm = sb("p3_xm", [128, 2, GT, H])
        xmT = sb("p3_xmT", [128, 2, KH, GT * TILE])
        st = sb("p3_st", [128, 2, 2, GT, 6])
        mv = sb("p3_mv", [128, 2, 2, GT, 2])
        small = sb("p3_small", [128, 2, 12, GT])
        ex = sb("p3_ex", [128, 2, GT, NE])
        top = sb("p3_top", [128, 2, GT, 8])
        idx = sb("p3_idx", [128, 2, GT, 8], mybir.dt.uint32)
        idf = sb("p3_idf", [128, 2, GT, 8])
        sel = sb("p3_sel", [128, 2, GT, NE])
        run = sb("p3_run", [128, 2, GT, NE])
        runs = tok["run"]
        pos = sb("p3_pos", [128, 2, GT, NE])
        junk = sb("p3_junk", [128, 2, GT * TOPK, NE], mybir.dt.bfloat16)
        slot_f = sb("p3_slotf", [128, 2, GT, TOPK])
        slot, own, scattered = tok["scatter_to"], tok["own"], tok["scattered"]
        gt = sb("p3_gt", [128, 2, SB, GT * TILE])
        hT = gt
        banks = [ctx.enter_context(nc.psum_tensor(f"p3_bank{k}", [128, 512], F32)) for k in range(8)]
        turn, rt, gbank, ubank, cnt = banks[0:2], banks[2], banks[3:5], banks[5:7], banks[7]
        blocks = [(b, min(128, SI - 128 * b)) for b in range(SB)]

        cleared = once("route_cleared")
        with nc.Block() as block:
            @block.vector
            def _(dve):
                nc.vector.memset(runs[:], 0.0).then_inc(cleared, 1)
                dve.wait_ge(cleared, 1)

        block = ctx.enter_context(nc.Block())

        def tile_of(a, n):
            return a[:, bass.ds(n, 1), :].rearrange("p a b -> p (a b)")

        def group_of(a, n):
            return a[:, bass.ds(n * GT, GT), :]

        @block.sync
        def _(sp):
            with sp.Fori(0, NG // 2) as it:
                for q in range(2):
                    n = 2 * it + q
                    sp.wait_ge(s["x2"], done(n, 2))
                    sp.dma_start(xin[:, q], group_of(x_tiles, n)).then_inc(s[f"x_loaded{q}"], 16)
                for q in range(2):
                    n = 2 * it + q
                    sp.wait_ge(s["xm"], done(n))
                    sp.dma_start(xm_rows[bass.ds(n * GT * TILE, GT * TILE), :].rearrange("(t p) h -> p t h", p=128), xm[:, q])\
                        .then_inc(s[f"xm_stored{q}"], 16)
            for q in range(2):
                sp.wait_ge(s[f"xm_stored{q}"], 16 * (NG // 2) + LEAD)

        @block.vector
        def _(dve):
            def variance(n, q, w, src, a_stats, a_mean_var, a_var):
                for t in range(GT):
                    last = nc.vector.bn_stats(st[:, q, w, t, :], tile_of(src, n * GT + t))
                last.then_inc(s[a_stats], 1)
                wait_alone(dve, s[a_stats], done(n), s["dve_passed"])
                for t in range(GT):
                    last = nc.vector.bn_aggr(mv[:, q, w, t, :], st[:, q, w, t, :])
                last.then_inc(s[a_mean_var], 1)
                dve.wait_ge(s[a_mean_var], done(n))
                nc.vector.tensor_scalar(small[:, q, 3 * w], mv[:, q, w, :, 1], EPS, None, ALU.add).then_inc(s[a_var], 1)

            def nbias(n, q, w, a_rstd, a_nbias):
                dve.wait_ge(s[a_rstd], done(n))
                nc.vector.scalar_tensor_tensor(small[:, q, 3 * w + 2], mv[:, q, w, :, 0], -1.0, small[:, q, 3 * w + 1],
                                               ALU.mult, ALU.mult).then_inc(s[a_nbias], 1)

            def add_attention(n, q, it):
                dve.wait_ge(s["a_norm"], done(n))
                dve.wait_ge(s[f"x_loaded{q}"], 16 * it + 16 + LEAD)
                nc.vector.tensor_tensor(group_of(tok["x2"], n), an[:, q], xin[:, q], ALU.add).then_inc(s["x2"], 1)
                wait_alone(dve, s["x2"], done(n), s["dve_passed"])

            def largest_logit(n, q):
                dve.wait_ge(s["logits"], done(n))
                nc.vector.tensor_reduce(small[:, q, 6], rt[:, 0:GT * NE].rearrange("p (a b) -> p a b", a=GT),
                                        mybir.AxisListType.X, ALU.max, negate=True).then_inc(s["top_max"], 1)

            def hidden(n, q, b):
                rows, r = blocks[b][1], (q * SB + b) % 2
                dve.wait_ge(s[f"gate_tanh{b}"], done(n))
                nc.vector.scalar_tensor_tensor(gt[0:rows, q, b, :], gt[0:rows, q, b, :], 1.0, gbank[r][0:rows, :],
                                               ALU.add, ALU.mult).then_inc(s[f"silu{b}"], 1)
                dve.wait_ge(s[f"silu{b}"], done(n))
                nc.vector.tensor_tensor(hT[0:rows, q, b, :], gt[0:rows, q, b, :], ubank[r][0:rows, :], ALU.mult)\
                    .then_inc(s[f"h{b}"], 1)

            def choose(n, q):
                dve.wait_ge(s["exps"], done(n))
                nc.vector.reciprocal(small[:, q, 8], small[:, q, 7]).then_inc(s["inv_sum"], 1)
                dve.wait_ge(s["inv_sum"], done(n))
                nc.vector.tensor_tensor(ex[:, q], ex[:, q], small[:, q, 8][:, :, None].to_broadcast([128, GT, NE]),
                                        ALU.mult).then_inc(s["probs"], 1)
                wait_alone(dve, s["probs"], done(n), s["dve_passed"])
                for t in range(GT):
                    last = nc.vector.max(top[:, q, t, :], ex[:, q, t, :])
                last.then_inc(s["top8"], 1)
                wait_alone(dve, s["top8"], done(n), s["dve_passed"])
                for t in range(GT):
                    last = nc.vector.max_index(idx[:, q, t, :], top[:, q, t, :], ex[:, q, t, :])
                last.then_inc(s["top_idx"], 1)

            def normalise(n, q):
                dve.wait_ge(s["top_idx"], done(n))
                nc.vector.tensor_copy(idf[:, q], idx[:, q]).then_inc(s["top_f"], 1)
                nc.vector.tensor_reduce(small[:, q, 9], top[:, q, :, 0:TOPK], mybir.AxisListType.X, ALU.add)\
                    .then_inc(s["top_sum"], 1)
                dve.wait_ge(s["top_sum"], done(n))
                nc.vector.reciprocal(small[:, q, 10], small[:, q, 9]).then_inc(s["top_inv"], 1)
                dve.wait_ge(s["top_inv"], done(n))
                nc.vector.tensor_tensor(group_of(tok["weight"], n), top[:, q, :, 0:TOPK],
                                        small[:, q, 10][:, :, None].to_broadcast([128, GT, TOPK]), ALU.mult)\
                    .then_inc(s["weights"], 1)

            def mark(n, q):
                dve.wait_ge(s["top_f"], done(n))
                dve.wait_ge(s["pos_done"], done(n, 2))
                for k in range(TOPK):
                    if k:
                        dve.wait_ge(s[f"sel{k - 1}"], done(n))
                    for t in range(GT):
                        if k == 0:
                            last = nc.vector.tensor_scalar(sel[:, q, t, :], c["expert"][:], idf[:, q, t, 0:1], None,
                                                           ALU.is_equal)
                        else:
                            last = nc.vector.scalar_tensor_tensor(sel[:, q, t, :], c["expert"][:], idf[:, q, t, k:k + 1],
                                                                  sel[:, q, t, :], ALU.is_equal, ALU.add)
                    last.then_inc(s[f"sel{k}"], 1)
                dve.wait_ge(s[f"sel{TOPK - 1}"], done(n))
                for t in range(GT):
                    after = run[:, q, t + 1, :] if t < GT - 1 else runs[:]
                    if t == 0:
                        dve.wait_ge(s["run3"], done(n, 1))
                        nc.vector.tensor_copy(run[:, q, 0, :], runs[:]).then_inc(s["before0"], 1)
                        dve.wait_ge(s["before0"], done(n))
                    else:
                        dve.wait_ge(s[f"run{t - 1}"], done(n))
                    nc.vector.tensor_tensor(after, run[:, q, t, :], sel[:, q, t, :], ALU.add).then_inc(s[f"run{t}"], 1)

            def find_places(n, q):
                dve.wait_ge(s["pos_done"], done(n))
                nc.vector.tensor_tensor(pos[:, q], cnt[:, 0:GT * NE].rearrange("p (a b) -> p a b", a=GT),
                                        c["region"][:, None, :].to_broadcast([128, GT, NE]), ALU.add)\
                    .then_inc(s["pos_kept"], 1)
                dve.wait_ge(s["pos_kept"], done(n))
                for t in range(GT):
                    for k in range(TOPK):
                        last = nc.vector.scalar_tensor_tensor(junk[:, q, t * TOPK + k, :], c["expert"][:],
                                                              idf[:, q, t, k:k + 1], pos[:, q, t, :],
                                                              ALU.is_equal, ALU.mult,
                                                              accum_out=slot_f[:, q, t, k:k + 1])
                last.then_inc(s["slots_f"], 1)
                dve.wait_ge(s["slots_f"], done(n))
                dve.wait_ge(s["scatters_done"], done(n, 2))
                nc.vector.tensor_copy(slot[:, q], slot_f[:, q])
                nc.vector.tensor_copy(own[:, q], c["token"][:, bass.ds(n * GT, GT)])
                nc.vector.tensor_copy(group_of(tok["choice"], n), idf[:, q, :, 0:TOPK])
                nc.vector.tensor_copy(group_of(tok["slot"], n), slot_f[:, q]).then_inc(s["slots"], 1)

            def variance_a(n, q):
                variance(n, q, 0, tok["xm"], "a_stats", "a_mean_var", "a_var")

            def variance_b(n, q):
                variance(n, q, 1, tok["x2"], "b_stats", "b_mean_var", "b_var")

            def group_round(n, q, it, ahead=True):
                if ahead:
                    variance_a(n + 1, 1 - q)
                largest_logit(n, q)
                hidden(n, q, 0)
                if ahead:
                    nbias(n + 1, 1 - q, 0, "a_rstd", "a_nbias")
                choose(n, q)
                if ahead:
                    add_attention(n + 1, 1 - q, it)
                    variance_b(n + 1, 1 - q)
                normalise(n, q)
                if ahead:
                    nbias(n + 1, 1 - q, 1, "b_rstd", "b_nbias")
                hidden(n, q, 1)
                mark(n, q)
                hidden(n, q, 2)
                find_places(n, q)

            variance_a(0, 0)
            nbias(0, 0, 0, "a_rstd", "a_nbias")
            add_attention(0, 0, 0)
            variance_b(0, 0)
            nbias(0, 0, 1, "b_rstd", "b_nbias")
            group_round(0, 0, 0)
            with dve.Fori(0, NG // 2 - 1) as it:
                group_round(2 * it + 1, 1, it + 1)
                group_round(2 * it + 2, 0, it + 1)
            group_round(NG - 1, 1, None, ahead=False)

        @block.gpsimd
        def _(pool):
            def rstd(n, q, w, var, rstd):
                pool.wait_ge(s[var], done(n))
                nc.gpsimd.tensor_tensor(small[:, q, 3 * w + 1], small[:, q, 3 * w], c["minus_half"][:, 0:GT], ALU.pow)\
                    .then_inc(s[rstd], 1)

            def group_round(n, q, it, ahead=True):
                if ahead:
                    rstd(n + 1, 1 - q, 0, "a_var", "a_rstd")
                wait_alone(pool, s["slots"], done(n, 1), s["pool_passed"])
                scatter_group(nc, tok, 1 - q, range(0, GT // 2))
                if ahead:
                    rstd(n + 1, 1 - q, 1, "b_var", "b_rstd")
                scatter_group(nc, tok, 1 - q, range(GT // 2, GT))
                wait_alone(pool, scattered[1 - q], 16 * GT * TOPK * it + 16 * GT * TOPK, s["scatters_done"])

            for n in range(2):
                rstd(n, n, 0, "a_var", "a_rstd")
                rstd(n, n, 1, "b_var", "b_rstd")
            with pool.Fori(0, NG // 2 - 1) as it:
                group_round(2 * it + 1, 1, it)
                group_round(2 * it + 2, 0, it)
            group_round(NG - 1, 1, NG // 2 - 1, ahead=False)

        @block.scalar
        def _(act):
            def normed_attention(n, q):
                act.wait_ge(s["a_nbias"], done(n))
                act.wait_ge(s["x2"], done(n, 2))
                for t in range(GT):
                    last = nc.scalar.activation(an[:, q, t, :], tile_of(tok["xm"], n * GT + t), ACT.Identity,
                                                bias=small[:, q, 2, t:t + 1], scale=small[:, q, 1, t:t + 1])
                last.then_inc(s["a_norm"], 1)

            def normed_x2(n, q, it):
                act.wait_ge(s["b_nbias"], done(n))
                act.wait_ge(s["turned"], done(n, 2))
                act.wait_ge(s[f"xm_stored{q}"], 16 * it + LEAD)
                for t in range(GT):
                    last = nc.scalar.activation(xm[:, q, t, :], tile_of(tok["x2"], n * GT + t), ACT.Identity,
                                                bias=small[:, q, 5, t:t + 1], scale=small[:, q, 4, t:t + 1])
                last.then_inc(s["xm"], 1)

            def keep_turned(n, q):
                act.wait_ge(s["turned"], done(n))
                act.wait_ge(s["gu2"], done(n, 2))
                for k in range(KH):
                    last = nc.scalar.activation(xmT[:, q, k, :], turn[k][:], ACT.Copy)
                last.then_inc(s["xm_turned"], 1)

            def exps(n, q):
                act.wait_ge(s["top_max"], done(n))
                act.wait_ge(s["slots_f"], done(n, 2))
                for t in range(GT):
                    last = nc.scalar.activation(ex[:, q, t, :], rt[:, t * NE:(t + 1) * NE], ACT.Exp,
                                                bias=small[:, q, 6, t:t + 1], accum_out=small[:, q, 7, t:t + 1])
                last.then_inc(s["exps"], 1)

            def gate_tanh(n, q, b):
                rows = blocks[b][1]
                act.wait_ge(s[f"gu{b}"], done(n))
                act.wait_ge(s["down"], done(n, 2))
                nc.scalar.activation(gt[0:rows, q, b, :], gbank[(q * SB + b) % 2][0:rows, :], ACT.Tanh, scale=0.5)\
                    .then_inc(s[f"gate_tanh{b}"], 1)

            def keep_shared(n):
                act.wait_ge(s["down"], done(n))
                for t in range(GT):
                    last = nc.scalar.activation(tile_of(tok["shared"], n * GT + t),
                                                turn[t // 2][:, H * (t % 2):H * (t % 2) + H], ACT.Copy, scale=0.5)
                last.then_inc(s["down_kept"], 1)

            def group_round(n, q, it, ahead=True):
                exps(n, q)
                gate_tanh(n, q, 0)
                if ahead:
                    normed_attention(n + 1, 1 - q)
                gate_tanh(n, q, 1)
                if ahead:
                    normed_x2(n + 1, 1 - q, it)
                gate_tanh(n, q, 2)
                if ahead:
                    keep_turned(n + 1, 1 - q)
                keep_shared(n)

            normed_attention(0, 0)
            normed_x2(0, 0, 0)
            keep_turned(0, 0)
            group_round(0, 0, 0)
            with act.Fori(0, NG // 2 - 1) as it:
                group_round(2 * it + 1, 1, it + 1)
                group_round(2 * it + 2, 0, it + 1)
            group_round(NG - 1, 1, None, ahead=False)

        @block.tensor
        def _(pe):
            def transposes(n, q):
                pe.wait_ge(s["xm"], done(n))
                pe.wait_ge(s["down_kept"], done(n, 2))
                for k in range(KH):
                    for t in range(GT):
                        last = nc.tensor.transpose(turn[k][:, t * TILE:(t + 1) * TILE],
                                                   xm[:, q, t, k * 128:(k + 1) * 128], c["ident"][:])
                last.then_inc(s["turned"], 1)

            def logits(n, q):
                pe.wait_ge(s["xm_turned"], done(n))
                pe.wait_ge(s["exps"], done(n, 1))
                for t in range(GT):
                    for k in range(KH):
                        last = nc.tensor.matmul(rt[:, t * NE:(t + 1) * NE], xmT[:, q, k, t * TILE:(t + 1) * TILE],
                                                c["router_w"][:, k, :], start=(k == 0), stop=(k == KH - 1))
                last.then_inc(s["logits"], 1)

            def gate_up(n, q, b):
                i, rows = q * SB + b, blocks[b][1]
                before, back = (f"h{b - 2}", 0) if b >= 2 else (f"h{b + 1}", 1)
                pe.wait_ge(s[before], done(n, back))
                for bank, w in ((gbank, "sg_w"), (ubank, "su_w")):
                    for k in range(KH):
                        last = nc.tensor.matmul(bank[i % 2][0:rows, :], c[w][:, k, 128 * b:128 * b + rows],
                                                xmT[:, q, k, :], start=(k == 0), stop=(k == KH - 1))
                last.then_inc(s[f"gu{b}"], 1)

            def down(n, q):
                pe.wait_ge(s[f"h{SB - 1}"], done(n))
                for t in range(GT):
                    for b, rows in blocks:
                        last = nc.tensor.matmul(turn[t // 2][:, H * (t % 2):H * (t % 2) + H],
                                                hT[0:rows, q, b, t * TILE:(t + 1) * TILE], c["sd_w"][0:rows, b, :],
                                                start=(b == 0), stop=(b == SB - 1))
                last.then_inc(s["down"], 1)

            def counts(n, q):
                pe.wait_ge(s["run3"], done(n))
                pe.wait_ge(s["pos_kept"], done(n, 1))
                nc.tensor.matmul(cnt[:, 0:GT * NE], c["before"][:], sel[:, q].rearrange("p a b -> p (a b)"),
                                 start=True, stop=False)
                nc.tensor.matmul(cnt[:, 0:GT * NE], c["all"][:], run[:, q].rearrange("p a b -> p (a b)"),
                                 start=False, stop=True).then_inc(s["pos_done"], 1)

            def group_round(n, q, ahead=True):
                for b in range(SB):
                    gate_up(n, q, b)
                if ahead:
                    transposes(n + 1, 1 - q)
                    logits(n + 1, 1 - q)
                counts(n, q)
                down(n, q)

            transposes(0, 0)
            logits(0, 0)
            group_round(0, 0)
            with pe.Fori(0, NG // 2 - 1) as it:
                group_round(2 * it + 1, 1)
                group_round(2 * it + 2, 0)
            group_round(NG - 1, 1, ahead=False)


def scatter_group(nc, tok, q, tiles):
    for t in tiles:
        for k in range(TOPK):
            nc.gpsimd.indirect_dma_start(tok["places"], bass.IndirectOffsetOnAxis(ap=tok["scatter_to"][:, q, t, k:k + 1], axis=0),
                                         tok["own"][:, q, t:t + 1], None).then_inc(tok["scattered"][q], 16)


def tables(nc, once, c, tok, places, tab_dram):
    I32 = mybir.dt.int32
    J = MAXT // 128
    with ExitStack() as ctx:
        def sb(name, shape, dt=F32):
            return ctx.enter_context(nc.sbuf_tensor(name, shape, dt))
        cnt = sb("p4_cnt", [128, NE])
        cnt_i = sb("p4_cnti", [128, NE], I32)
        num = sb("p4_num", [128, NE])
        end = sb("p4_end", [128, NE])
        begin = sb("p4_begin", [128, NE])
        hit = sb("p4_hit", [128, NE])
        first = sb("p4_first", [128, NE])
        one = sb("p4_one", [128, NE])
        cell = sb("p4_cell", [128, J, 7])
        page = sb("p4_page", [128, J], mybir.dt.uint32)
        expert = sb("p4_expert", [128, J], I32)
        listed = sb("p4_listed", [128, J, 128])
        ps = ctx.enter_context(nc.psum_tensor("p4_ps", [128, NE], F32))
        ps_rows = ctx.enter_context(nc.psum_tensor("p4_rows", [128, MAXT], F32))
        step, counted, experts_ready, pages_ready = once("tables_step"), once("experts_counted"), once("experts_ready"), once("pages_ready")
        experts_stored, experts_loaded, rows_turned = once("experts_stored"), once("experts_loaded"), once("rows_turned")
        listed_loaded = [once(f"listed_loaded{j}") for j in range(J)]
        block = ctx.enter_context(nc.Block())

        @block.tensor
        def _(pe):
            nc.tensor.matmul(ps[:], c["all"][:], tok["run"][:], start=True, stop=True).then_inc(counted, 1)
            for j in range(J):
                pe.wait_ge(listed_loaded[j], 16)
                nc.tensor.transpose(ps_rows[:, 128 * j:128 * j + 128], listed[:, j], c["ident"][:]).then_inc(rows_turned, 1)

        @block.vector
        def _(dve):
            steps = [0]

            def then(ins):
                steps[0] += 1
                ins.then_inc(step, 1)
                dve.wait_ge(step, steps[0])
            nc.vector.memset(one[:], 1.0)
            dve.wait_ge(counted, 1)
            then(nc.vector.tensor_scalar(cnt[:], ps[:], 127.0, None, ALU.add))
            then(nc.vector.tensor_copy(cnt_i[:], cnt[:]))
            then(nc.vector.tensor_scalar(cnt_i[:], cnt_i[:], 7, None, ALU.logical_shift_right))
            then(nc.vector.tensor_copy(num[:], cnt_i[:]))
            then(nc.vector.tensor_scalar(num[:], num[:], 1.0, None, ALU.max))
            then(nc.vector.tensor_tensor_scan(end[:], one[:], num[:], 0.0, ALU.mult, ALU.add))
            then(nc.vector.tensor_tensor(begin[:], end[:], num[:], ALU.subtract))
            nc.vector.scalar_tensor_tensor(tok["shift"][:], begin[:], 128.0, c["region"][:], ALU.mult, ALU.subtract)
            then(nc.vector.memset(tok["freed"][:, 0:WB], 0))
            then(nc.vector.tensor_copy(tok["freed"][:, WB:NE], end[0:1, 0:NE - WB]))
            then(nc.vector.tensor_scalar(hit[0:1, 0:1], end[0:1, NE - 1:NE], 3.0, None, ALU.add))
            then(nc.vector.tensor_copy(tok["rounds"][:], hit[0:1, 0:1]))
            then(nc.vector.tensor_scalar(tok["rounds"][:], tok["rounds"][:], 2, None, ALU.logical_shift_right))
            then(nc.vector.tensor_copy(hit[0:1, 1:2], tok["rounds"][:]))
            then(nc.vector.tensor_scalar(hit[0:1, 1:2], hit[0:1, 1:2], -64.0, 16.0 * (MAXT + 1), ALU.mult, ALU.add))
            then(nc.vector.tensor_copy(tok["left"][:], hit[0:1, 1:2]))
            for j in range(J):
                t = c["tile"][:, j:j + 1]
                then(nc.vector.scalar_tensor_tensor(hit[:], begin[:], t, one[:], ALU.is_le, ALU.mult,
                                                    accum_out=cell[:, j, 0:1]))
                then(nc.vector.scalar_tensor_tensor(first[:], begin[:], t, begin[:], ALU.is_le, ALU.mult))
                then(nc.vector.tensor_reduce(cell[:, j, 1:2], first[:], mybir.AxisListType.X, ALU.max))
                then(nc.vector.tensor_scalar(cell[:, j, 0:1], cell[:, j, 0:1], -1.0, None, ALU.add))
                then(nc.vector.tensor_tensor(cell[:, j, 2:3], t, cell[:, j, 1:2], ALU.subtract))
                then(nc.vector.tensor_scalar(cell[:, j, 2:3], cell[:, j, 2:3], float(REGION // 128 - 1), None, ALU.min))
                then(nc.vector.tensor_scalar(cell[:, j, 3:4], cell[:, j, 0:1], float(REGION // 128), None, ALU.mult))
                then(nc.vector.tensor_tensor(cell[:, j, 2:3], cell[:, j, 2:3], cell[:, j, 3:4], ALU.add))
                nc.vector.tensor_copy(page[:, j:j + 1], cell[:, j, 2:3]).then_inc(pages_ready, 1)
                then(nc.vector.tensor_scalar(cell[:, j, 4:5], t, -2.0, None, ALU.add))
                then(nc.vector.scalar_tensor_tensor(hit[:], begin[:], cell[:, j, 4:5], one[:], ALU.is_le, ALU.mult,
                                                    accum_out=cell[:, j, 5:6]))
                then(nc.vector.tensor_scalar(cell[:, j, 5:6], cell[:, j, 5:6], 1.0, -1.0, ALU.max, ALU.add))
                then(nc.vector.tensor_copy(expert[:, j:j + 1], cell[:, j, 5:6]))
                then(nc.vector.tensor_scalar(expert[:, j:j + 1], expert[:, j:j + 1], WB - 1, None, ALU.bitwise_and))
                then(nc.vector.tensor_copy(cell[:, j, 6:7], expert[:, j:j + 1]))
                then(nc.vector.scalar_tensor_tensor(cell[:, j, 6:7], cell[:, j, 6:7], float(NE), cell[:, j, 0:1],
                                                    ALU.mult, ALU.add))
                nc.vector.tensor_copy(expert[:, j:j + 1], cell[:, j, 6:7]).then_inc(experts_ready, 1)
            dve.wait_ge(rows_turned, J)
            nc.vector.memset(tok["rows"][:, MAXT:MAXT + 8], 0.0)
            nc.vector.memset(tok["tile"][:, MAXT:], 0)
            then(nc.vector.tensor_copy(tok["rows"][:, 0:MAXT].rearrange("p (t j) -> p j t", j=J),
                                       ps_rows[:].rearrange("p (j t) -> p j t", j=J)))

        @block.gpsimd
        def _(pool):
            scatter_group(nc, tok, 1, range(GT))
            pool.wait_ge(tok["scattered"][1], 16 * GT * TOPK * (NG // 2))
            for j in range(J):
                pool.wait_ge(pages_ready, j + 1)
                pool.indirect_dma_start(listed[:, j], None, places.rearrange("(a b) o -> a (b o)", b=128),
                                        bass.IndirectOffsetOnAxis(ap=page[:, j:j + 1], axis=0)).then_inc(listed_loaded[j], 16)

        @block.scalar
        def _(act):
            act.wait_ge(experts_ready, J)
            act.dma_start(tab_dram.rearrange("(p j) -> p j", p=128), expert[:]).then_inc(experts_stored, 16)
            act.wait_ge(experts_stored, 16)
            act.dma_start(tok["tile"][:, 0:MAXT], tab_dram[None, :]).then_inc(experts_loaded, 16)
            act.wait_ge(experts_loaded, 16)


def experts(nc, once, c, tok, dram, xm_rows, y_rows):
    WIDE = 4
    x_loaded = [once(f"expert_x_loaded{q}") for q in range(WIDE)]
    zeroed = once("y_rows_zeroed")
    names = ("w_loaded rows turned xT h tanh silu h_turned hT y y_kept pool_passed act_passed sp_passed "
             "y_stored0 y_stored1 y_stored2 y_stored3")
    with loop_semaphores(nc, names) as s, ExitStack() as ctx:
        def sb(name, shape, dt=F32):
            return ctx.enter_context(nc.sbuf_tensor(name, shape, dt))

        def banks(name):
            return [ctx.enter_context(nc.psum_tensor(f"p5_{name}{q}", [128, 512], F32)) for q in range(2)]
        w1 = sb("p5_w1", [128, WB, KH * EI])
        w2 = sb("p5_w2", [EK, WB, 2 * H])
        idx = sb("p5_idx", [128, WIDE, 1], mybir.dt.uint32)
        xe = sb("p5_xe", [128, WIDE, H])
        xT = sb("p5_xT", [128, 2, KH * TILE])
        th = sb("p5_th", [128, 2, EI])
        hh = sb("p5_h", [128, 2, EI])
        hT = sb("p5_hT", [EK, 2, 2 * TILE])
        ys = sb("p5_y", [128, WIDE, H])
        ps_x, ps_h, ps_t, ps_y = banks("turn"), banks("h"), banks("ht"), banks("y")
        block = ctx.enter_context(nc.Block())

        def expert_of(eng, n):
            both = eng.value_load(tok["tile"][0:1, bass.ds(n, 1)], min_val=0, max_val=NE * WB - 1)
            return both % NE, both // NE

        def rounds(eng):
            return eng.value_load(tok["rounds"][0:1, 0:1], min_val=1, max_val=MAXT // WIDE)

        @block.sync
        def _(sp):
            def load(e):
                freed = sp.value_load(tok["freed"][0:1, bass.ds(e, 1)], min_val=0, max_val=MAXT)
                sp.wait_ge(s["y"], freed + LEAD)
                sp.wait_ge(s["w_loaded"], 32 * e + LEAD)
                sp.dma_start(w1[:, bass.ds(e % WB, 1), :].rearrange("p a b -> p (a b)"),
                             dram["w1"][bass.ds(e, 1)].rearrange("a p b -> (a p) b")).then_inc(s["w_loaded"], 16)
                sp.dma_start(w2[:, bass.ds(e % WB, 1), :].rearrange("p a b -> p (a b)"),
                             dram["w2"][bass.ds(e, 1)].rearrange("a p b -> (a p) b")).then_inc(s["w_loaded"], 16)

            with sp.Fori(0, WB) as e:
                load(e)
            with sp.Fori(WIDE * rounds(sp), MAXT + 1) as t:
                sp.dma_start(y_rows[bass.ds(t * 128, 128), :], tok["zero"][:]).then_inc(zeroed, 16)
            with sp.Fori(WB, NE) as e:
                load(e)
            sp.wait_ge(s["w_loaded"], 32 * NE + LEAD)
            n_left = sp.value_load(tok["left"][0:1, 0:1], min_val=16, max_val=16 * (MAXT + 1))
            wait_alone(sp, zeroed, n_left, s["sp_passed"])

        @block.gpsimd
        def _(pool):
            def gather(n, q):
                wait_alone(pool, s["rows"], done(n), s["pool_passed"])
                pool.indirect_dma_start(xe[:, q], None, xm_rows, bass.IndirectOffsetOnAxis(ap=idx[:, q], axis=0))\
                    .then_inc(x_loaded[q], 16)

            for n in range(WIDE + 3):
                gather(n, n % WIDE)
            with pool.Fori(0, rounds(pool)) as it:
                for q in range(WIDE):
                    gather(WIDE * it + q + WIDE + 3, (q + 3) % WIDE)
            n_rounds = rounds(pool)
            for q in range(WIDE):
                wait_alone(pool, x_loaded[q], 16 * n_rounds + 16 + (16 if q < 3 else 0), s["pool_passed"])

        @block.tensor
        def _(pe):
            def turn(n, q, it):
                pe.wait_ge(x_loaded[q], 16 * it + 16)
                for k in range(KH):
                    last = nc.tensor.transpose(ps_x[q % 2][:, k * TILE:(k + 1) * TILE], xe[:, q, k * 128:(k + 1) * 128],
                                               c["ident"][:])
                last.then_inc(s["turned"], 1)

            def up(n, q):
                e, buffer_2 = expert_of(pe, n)
                buffer = e % WB
                pe.wait_ge(s["w_loaded"], 32 * e + 32 + LEAD)
                pe.wait_ge(s["xT"], done(n))
                for k in range(KH):
                    last = nc.tensor.matmul(ps_h[q % 2][:, 0:EI], xT[:, q % 2, k * TILE:(k + 1) * TILE],
                                            w1[:, bass.ds(buffer, 1), k * EI:(k + 1) * EI].rearrange("p a b -> p (a b)"),
                                            start=(k == 0), stop=(k == KH - 1))
                last.then_inc(s["h"], 1)
                return buffer_2

            def turn_hidden(n, q):
                pe.wait_ge(s["silu"], done(n))
                for k in range(2):
                    last = nc.tensor.transpose(ps_t[q % 2][0:EK, k * TILE:(k + 1) * TILE], hh[:, q % 2, k * EK:(k + 1) * EK],
                                               c["ident"][:])
                last.then_inc(s["h_turned"], 1)

            def down(n, q, buffer):
                pe.wait_ge(s["hT"], done(n))
                pe.wait_ge(s["y_kept"], done(n, 2))
                for k in range(2):
                    last = nc.tensor.matmul(ps_y[q % 2][:, 0:H], hT[:, q % 2, k * TILE:(k + 1) * TILE],
                                            w2[:, bass.ds(buffer, 1), k * H:(k + 1) * H].rearrange("p a b -> p (a b)"),
                                            start=(k == 0), stop=(k == 1))
                last.then_inc(s["y"], 1)

            turn(0, 0, 0)
            up(0, 0)
            turn(1, 1, 0)
            turn(2, 2, 0)
            up(1, 1)
            turn_hidden(0, 0)
            with pe.Fori(0, rounds(pe)) as it:
                for q in range(WIDE):
                    n = WIDE * it + q
                    turn(n + 3, (q + 3) % WIDE, it + (q + 3) // WIDE)
                    buffer = up(n + 2, (q + 2) % WIDE)
                    turn_hidden(n + 1, (q + 1) % WIDE)
                    down(n, q, buffer)

        @block.vector
        def _(dve):
            def rows(n, q):
                nc.vector.tensor_copy(idx[:, q], tok["rows"][:, bass.ds(n, 1)]).then_inc(s["rows"], 1)

            def keep_xT(n, q):
                dve.wait_ge(s["turned"], done(n))
                dve.wait_ge(s["h"], done(n, 2))
                nc.vector.tensor_copy(xT[:, q % 2], ps_x[q % 2][:, 0:KH * TILE]).then_inc(s["xT"], 1)

            def silu(n, q):
                dve.wait_ge(s["tanh"], done(n))
                dve.wait_ge(s["h_turned"], done(n, 2))
                nc.vector.scalar_tensor_tensor(hh[:, q % 2], th[:, q % 2], 1.0, ps_h[q % 2][:, 0:EI], ALU.add, ALU.mult)\
                    .then_inc(s["silu"], 1)

            for q in range(WIDE):
                rows(q, q)
            keep_xT(0, 0)
            rows(WIDE, 0)
            keep_xT(1, 1)
            rows(WIDE + 1, 1)
            silu(0, 0)
            keep_xT(2, 2)
            rows(WIDE + 2, 2)
            silu(1, 1)
            with dve.Fori(0, rounds(dve)) as it:
                for q in range(WIDE):
                    n = WIDE * it + q
                    keep_xT(n + 3, (q + 3) % WIDE)
                    rows(n + 3 + WIDE, (q + 3) % WIDE)
                    silu(n + 2, (q + 2) % WIDE)

        @block.scalar
        def _(act):
            def tanh(n, q):
                act.wait_ge(s["h"], done(n))
                act.wait_ge(s["silu"], done(n, 2))
                nc.scalar.activation(th[:, q % 2], ps_h[q % 2][:, 0:EI], ACT.Tanh, scale=0.5).then_inc(s["tanh"], 1)

            def keep_hT(n, q):
                act.wait_ge(s["h_turned"], done(n))
                act.wait_ge(s["y"], done(n, 2))
                nc.scalar.activation(hT[:, q % 2], ps_t[q % 2][0:EK, 0:2 * TILE], ACT.Copy).then_inc(s["hT"], 1)

            tanh(0, 0)
            tanh(1, 1)
            keep_hT(0, 0)
            with act.Fori(0, rounds(act)) as it:
                for q in range(WIDE):
                    n = WIDE * it + q
                    tanh(n + 2, (q + 2) % WIDE)
                    keep_hT(n + 1, (q + 1) % WIDE)
                    act.wait_ge(s["y"], done(n))
                    act.wait_ge(s[f"y_stored{q}"], 16 * it + LEAD)
                    nc.scalar.activation(ys[:, q], ps_y[q % 2][:, 0:H], ACT.Copy, scale=0.5).then_inc(s["y_kept"], 1)
                    act.wait_ge(s["y_kept"], done(n))
                    act.dma_start(y_rows[bass.ds(n * 128, 128), :], ys[:, q]).then_inc(s[f"y_stored{q}"], 16)
            n_rounds = rounds(act)
            for q in range(WIDE):
                wait_alone(act, s[f"y_stored{q}"], 16 * n_rounds + LEAD, s["act_passed"])


def combine(nc, once, c, tok, y_rows, out):
    WIDE, AHEAD = 4, 3
    LOOPS = (NT - WIDE - 2) // WIDE
    gathered = [once(f"gathered{q}") for q in range(WIDE)]
    names = ("copied shifts slots sum0 sum1 sum2 sum3 sum4 sum5 stats mean_var var rstd nbias norm result pool_passed "
             "dve_passed stored0 stored1 stored2 stored3")
    with loop_semaphores(nc, names) as s, ExitStack() as ctx:
        def sb(name, shape, dt=F32):
            return ctx.enter_context(nc.sbuf_tensor(name, shape, dt))
        slot = sb("p6_slot", [128, WIDE, TOPK], mybir.dt.uint32)
        shift = sb("p6_shift", [128, WIDE, TOPK])
        choice = sb("p6_choice", [128, WIDE, TOPK])
        junk = sb("p6_junk", [128, WIDE, TOPK, NE])
        wt = sb("p6_w", [128, WIDE, TOPK])
        yg = sb("p6_y", [128, WIDE, TOPK, H])
        acc = sb("p6_acc", [128, WIDE, H])
        res = sb("p6_res", [128, WIDE, H])
        st = sb("p6_st", [128, WIDE, 6])
        mv = sb("p6_mv", [128, WIDE, 2])
        small = sb("p6_small", [128, WIDE, 4])
        block = ctx.enter_context(nc.Block())

        def tile_of(a, n):
            return a[:, bass.ds(n, 1), :].rearrange("p a b -> p (a b)")

        @block.gpsimd
        def _(pool):
            def gather(n, q):
                wait_alone(pool, s["slots"], done(n), s["pool_passed"])
                for k in range(TOPK):
                    pool.indirect_dma_start(yg[:, q, k, :], None, y_rows,
                                            bass.IndirectOffsetOnAxis(ap=slot[:, q, k:k + 1], axis=0))\
                        .then_inc(gathered[q], 16)

            def rstd(n, q):
                pool.wait_ge(s["var"], done(n))
                nc.gpsimd.tensor_tensor(small[:, q, 1:2], small[:, q, 0:1], c["minus_half"][:, 0:1], ALU.pow)\
                    .then_inc(s["rstd"], 1)

            for n in range(AHEAD + 2):
                gather(n, n % WIDE)
            rstd(0, 0)
            with pool.Fori(0, LOOPS) as it:
                for q in range(WIDE):
                    n = WIDE * it + q + 2
                    gather(n + AHEAD, (q + 2 + AHEAD) % WIDE)
                    rstd(n - 1, (q + 1) % WIDE)
            for n in range(WIDE * LOOPS + 2, NT):
                if n + AHEAD < NT:
                    gather(n + AHEAD, (n + AHEAD) % WIDE)
                rstd(n - 1, (n - 1) % WIDE)
            rstd(NT - 1, (NT - 1) % WIDE)

        @block.vector
        def _(dve):
            def slots(n, q):
                dve.wait_ge(s[f"sum{TOPK - 1}"], done(n, WIDE))
                nc.vector.tensor_copy(wt[:, q], tile_of(tok["weight"], n))
                nc.vector.tensor_copy(choice[:, q], tile_of(tok["choice"], n)).then_inc(s["copied"], 1)
                dve.wait_ge(s["copied"], done(n))
                for k in range(TOPK):
                    last = nc.vector.scalar_tensor_tensor(junk[:, q, k], c["expert"][:], choice[:, q, k:k + 1],
                                                          tok["shift"][:], ALU.is_equal, ALU.mult,
                                                          accum_out=shift[:, q, k:k + 1])
                last.then_inc(s["shifts"], 1)
                dve.wait_ge(s["shifts"], done(n))
                nc.vector.tensor_tensor(slot[:, q], tile_of(tok["slot"], n), shift[:, q], ALU.add).then_inc(s["slots"], 1)

            def sums(n, q, it):
                dve.wait_ge(gathered[q], 16 * TOPK * it + 16 * TOPK)
                dve.wait_ge(s["result"], done(n, WIDE))
                for k in range(TOPK):
                    if k:
                        dve.wait_ge(s[f"sum{k - 1}"], done(n))
                    before = acc[:, q] if k else tile_of(tok["shared"], n)
                    nc.vector.scalar_tensor_tensor(acc[:, q], yg[:, q, k, :], wt[:, q, k:k + 1], before,
                                                   ALU.mult, ALU.add).then_inc(s[f"sum{k}"], 1)
                dve.wait_ge(s[f"sum{TOPK - 1}"], done(n))
                nc.vector.bn_stats(st[:, q], acc[:, q]).then_inc(s["stats"], 1)
                wait_alone(dve, s["stats"], done(n), s["dve_passed"])
                nc.vector.bn_aggr(mv[:, q], st[:, q]).then_inc(s["mean_var"], 1)
                dve.wait_ge(s["mean_var"], done(n))
                nc.vector.tensor_scalar(small[:, q, 0:1], mv[:, q, 1:2], EPS, None, ALU.add).then_inc(s["var"], 1)

            def nbias(n, q):
                dve.wait_ge(s["rstd"], done(n))
                nc.vector.scalar_tensor_tensor(small[:, q, 2:3], mv[:, q, 0:1], -1.0, small[:, q, 1:2],
                                               ALU.mult, ALU.mult).then_inc(s["nbias"], 1)

            def result(n, q, it):
                dve.wait_ge(s["norm"], done(n))
                dve.wait_ge(s[f"stored{q}"], 16 * it + LEAD)
                nc.vector.tensor_tensor(res[:, q], acc[:, q], tile_of(tok["x2"], n), ALU.add).then_inc(s["result"], 1)

            for n in range(WIDE):
                slots(n, n)
            for n in range(2):
                sums(n, n, 0)
                slots(n + WIDE, n)
            nbias(0, 0)
            with dve.Fori(0, LOOPS) as it:
                for q in range(WIDE):
                    n = WIDE * it + q + 2
                    sums(n, (q + 2) % WIDE, it + (q + 2) // WIDE)
                    slots(n + WIDE, (q + 2) % WIDE)
                    nbias(n - 1, (q + 1) % WIDE)
                    result(n - 2, q, it)
            for n in range(WIDE * LOOPS + 2, NT):
                sums(n, n % WIDE, n // WIDE)
                if n + WIDE < NT:
                    slots(n + WIDE, n % WIDE)
                nbias(n - 1, (n - 1) % WIDE)
                result(n - 2, (n - 2) % WIDE, (n - 2) // WIDE)
            nbias(NT - 1, (NT - 1) % WIDE)
            for n in (NT - 2, NT - 1):
                result(n, n % WIDE, n // WIDE)

        @block.scalar
        def _(act):
            with act.Fori(0, NT // WIDE) as it:
                for q in range(WIDE):
                    n = WIDE * it + q
                    act.wait_ge(s["nbias"], done(n))
                    nc.scalar.activation(acc[:, q], acc[:, q], ACT.Identity, bias=small[:, q, 2:3], scale=small[:, q, 1:2])\
                        .then_inc(s["norm"], 1)

        @block.sync
        def _(sp):
            with sp.Fori(0, NT // WIDE) as it:
                for q in range(WIDE):
                    n = WIDE * it + q
                    sp.wait_ge(s["result"], done(n))
                    sp.dma_start(tile_of(out, n), res[:, q]).then_inc(s[f"stored{q}"], 16)
            for q in range(WIDE):
                sp.wait_ge(s[f"stored{q}"], 16 * (NT // WIDE) + LEAD)


def build(nc, src, dram, out):
    xm_rows = nc.dram_tensor("xm_rows", (B * T + 128, H), F32, kind="Internal").ap()
    places = nc.dram_tensor("places", (NE * REGION, 1), F32, kind="Internal").ap()
    y_rows = nc.dram_tensor("y_rows", (MAXT * 128 + 128, H), F32, kind="Internal").ap()
    tab_dram = nc.dram_tensor("tile_table", (MAXT,), mybir.dt.int32, kind="Internal").ap()
    with ExitStack() as ctx:
        def sb(name, shape, dt=F32):
            return ctx.enter_context(nc.sbuf_tensor(name, shape, dt))
        def once(name):
            return ctx.enter_context(nc.semaphore(name))
        c, late, late_loaded = load_constants(nc, sb, once, src)
        tokT = sb("tokT", [128, NT, KH, TILE])
        attn = tokT[:].rearrange("p n k t -> p n (k t)")
        blank, zero = sb("blank", [128, BLANK]), sb("zero", [128, H])
        with ExitStack() as inner:
            res = {"tokT": tokT, "attn": attn}
            for name, shape in (("rstd", [128, NT]), ("nbias", [128, NT]), ("dt", [128, NT, NH]), ("dA", [128, NT, NH]),
                                ("to_end", [128, NT, NH]), ("decay0", [128, NT, NH]), ("decay1", [128, NT, NH]),
                                ("dAp", [128, CT, NT, HG])):
                res[name] = inner.enter_context(nc.sbuf_tensor("r_" + name, shape, F32))
            norm_in(nc, c, res, dram["x"], late, late_loaded)
            decays(nc, c, res)
            scan(nc, once, c, res, dram["x"], late, late_loaded, blank, zero, places, xm_rows)
        tok = {"places": places, "scatter_to": sb("scatter_to", [128, 2, GT, TOPK], mybir.dt.uint32),
               "own": sb("own", [128, 2, GT]),
               "scattered": [once(f"scattered{q}") for q in range(2)],
               "zero": zero,
               "left": sb("left", [1, 1], mybir.dt.int32),
               "xm": attn, "x2": sb("x2", [128, NT, H]), "shared": sb("shared", [128, NT, H]),
               "weight": sb("weight", [128, NT, TOPK]), "slot": sb("slot", [128, NT, TOPK]),
               "choice": sb("choice", [128, NT, TOPK]), "shift": sb("shift", [128, NE]), "rows": sb("rows", [128, MAXT + 8]),
               "run": sb("run", [128, NE]), "tile": sb("tile", [1, MAXT + 4], mybir.dt.int32),
               "freed": sb("freed", [1, NE], mybir.dt.int32), "rounds": sb("rounds", [1, 1], mybir.dt.int32)}
        route(nc, once, c, tok, dram["x"], xm_rows, places)
        tables(nc, once, c, tok, places, tab_dram)
        experts(nc, once, c, tok, dram, xm_rows, y_rows)
        combine(nc, once, c, tok, y_rows, out)


def constants():
    p, l = np.arange(128)[:, None], np.arange(128)[None, :]
    same = (p // CH) == (l // CH)
    f = np.float32
    k = {"ident": np.eye(128), "ones": np.ones((128, 4)), "minus_half": np.full((128, 8), -0.5)}
    k["later"] = same & (p > l)
    k["until"] = same & (p <= l)
    k["until32"] = (p % CH) <= l[:, :CH]
    k["until32q"] = 0.25 * ((p % CH) <= l[:, :CH])
    for j in range(2):
        k[f"whole{j}"] = (p // CH) == 2 * (l // NS) + j
    k["before"] = p < l
    k["all"] = np.ones((128, 128))
    k["expert"] = np.broadcast_to(np.arange(NE), (128, NE))
    k["region"] = np.broadcast_to(np.arange(NE) * REGION, (128, NE))
    k["token"] = np.arange(B * T).reshape(NT, 128).T
    k["tile"] = np.arange(MAXT).reshape(128, -1)
    return {n: np.ascontiguousarray(a, dtype=f) for n, a in k.items()}


def kernel(L0_attn_hidden_states, L0_attn_ln_weight, L0_attn_in_proj_w, L0_attn_conv_w, L0_attn_conv_b, L0_attn_dt_bias,
           L0_attn_A_log, L0_attn_D, L0_attn_norm_weight, L0_attn_out_proj_w, L0_ffn_gate_w, L0_ffn_experts_w1,
           L0_ffn_experts_w2, L0_ffn_shared_gate_up, L0_ffn_shared_down):
    import concourse.bacc as bacc
    from concourse.bass_utils import run_bass_kernel_spmd

    def columns(a):
        return np.asarray(a).reshape(-1, 128).T

    def rows(a):
        a = np.asarray(a)
        return a.reshape(-1, 128, a.shape[1]).transpose(1, 0, 2)

    def everywhere(a):
        return np.broadcast_to(np.asarray(a), (128, len(a)))

    x = np.asarray(L0_attn_hidden_states)
    tiles = x.reshape(PAIRS, 2, NT // PAIRS, HALF, H).transpose(1, 3, 2, 0, 4).reshape(128, NT, H)
    w_in = np.asarray(L0_attn_in_proj_w)
    arrays = constants()
    arrays["w_gate"] = rows(w_in[:CI].T)
    arrays["w_xbc"] = rows(w_in[CI:CI + NB * 128].T)
    arrays["w_dt"] = rows(w_in[CI + NB * 128:].T)
    arrays["w_out"] = rows(np.asarray(L0_attn_out_proj_w).T)
    arrays["ln_w"] = columns(L0_attn_ln_weight)
    arrays["norm_w"] = columns(L0_attn_norm_weight)
    arrays["conv_b"] = columns(L0_attn_conv_b)
    arrays["conv_w"] = rows(L0_attn_conv_w)
    arrays["skip"] = columns(np.repeat(np.asarray(L0_attn_D), P))
    arrays["dt_bias"] = everywhere(L0_attn_dt_bias)
    arrays["a_log"] = everywhere(L0_attn_A_log)
    gu = np.asarray(L0_ffn_shared_gate_up).T
    arrays["router_w"] = rows(np.asarray(L0_ffn_gate_w).T)
    arrays["sg_w"] = rows(gu[:, :SI])
    arrays["su_w"] = rows(gu[:, SI:])
    down = np.zeros((SB * 128, H), np.float32)
    down[:SI] = np.asarray(L0_ffn_shared_down).T
    arrays["sd_w"] = rows(down)
    arrays = {n: np.ascontiguousarray(a) for n, a in arrays.items()}
    w1 = np.asarray(L0_ffn_experts_w1).transpose(0, 2, 1).reshape(NE, KH, 128, EI).transpose(0, 2, 1, 3)
    w2 = np.asarray(L0_ffn_experts_w2).transpose(0, 2, 1).reshape(NE, 2, EK, H).transpose(0, 2, 1, 3)
    big = {"x": tiles, "w1": w1.reshape(NE, 128, KH * EI), "w2": w2.reshape(NE, EK, 2 * H)}
    big = {n: np.ascontiguousarray(a) for n, a in big.items()}

    nc = bacc.Bacc("TRN2", target_bir_lowering=False, num_devices=1)
    src = {n: nc.dram_tensor("in_" + n, a.shape, F32, kind="ExternalInput").ap() for n, a in arrays.items()}
    dram = {n: nc.dram_tensor("in_" + n, a.shape, F32, kind="ExternalInput").ap() for n, a in big.items()}
    out = nc.dram_tensor("out", (128, NT, H), F32, kind="ExternalOutput").ap()
    build(nc, src, dram, out)
    feed = {"in_" + n: a for n, a in (arrays | big).items()}
    got = run_bass_kernel_spmd(nc, [feed], core_ids=[0]).results[0]["out"]
    return got.reshape(2, HALF, NT // PAIRS, PAIRS, H).transpose(3, 0, 2, 1, 4).reshape(B, T, H)
```
